# Optimizing a Trainium2 kernel written in Bass

```python
import numpy as np
import jax
import jax.numpy as jnp

def _softmax(x, axis=-1):
    return jax.nn.softmax(x, axis=axis)

def _gelu(x):
    return jax.nn.gelu(x, approximate=True)

def _silu(x):
    return jax.nn.silu(x)

def _sigmoid(x):
    return jax.nn.sigmoid(x)

def _layernorm(x, axis=-1, eps=1e-05):
    m = jnp.mean(x, axis=axis, keepdims=True)
    v = jnp.var(x, axis=axis, keepdims=True)
    return (x - m) / jnp.sqrt(v + eps)

def _scatter_add(tgt, idx, src, axis=0):
    return tgt.at[idx].add(src)

def _segment_sum(src, seg, n):
    return jax.ops.segment_sum(src, seg, n)
kernel_name = 'mk_gnn_resnorm_d2_gnn_r32_b40e53'

def setup_inputs(seed: int=0):
    np.random.seed(seed)
    _w = jnp.asarray

    def _rec_inputs():
        import jax
        import jax.numpy as jnp
        _gk = jax.random.key(seed)
        x = -0.0003019 + 1 * jax.random.normal(jax.random.fold_in(_gk, 1), (1250, 512), jnp.float32)
        src = jax.random.randint(jax.random.fold_in(_gk, 2), (20000,), 0, 1250, jnp.int32)
        dst = jnp.minimum((1250 * jax.random.uniform(jax.random.fold_in(_gk, 3), (20000,)) ** 2.0).astype(jnp.int32), 39999)
        _o = jnp.argsort(dst, stable=True)
        src = src[_o]
        dst = dst[_o]
        edge_attr_32 = jax.random.uniform(jax.random.fold_in(_gk, 11), (20000, 32), jnp.float32, 0.0, 1)
        edge_attr_4 = 0.000937891 + 0.999965 * jax.random.normal(jax.random.fold_in(_gk, 12), (20000, 4), jnp.float32)
        return (x, src, dst, edge_attr_32, edge_attr_4)
    x, src, dst, edge_attr_32, edge_attr_4 = _rec_inputs()

    def _L0_gnn_setup():
        import jax, jax.numpy as jnp
        import numpy as np
        N = 1250
        IN_DIM = 512
        OUT_DIM = 512
        E_RAND = 20000
        SLOPE = 0.1
        key = jax.random.key(seed)
        k1, k2, k3, k4, k5 = jax.random.split(key, 5)
        features = jax.random.normal(k1, (N, IN_DIM), dtype=jnp.float32)
        src = jax.random.randint(k2, (E_RAND,), 0, N)
        dst = jax.random.randint(k3, (E_RAND,), 0, N)
        loops = jnp.arange(N)
        edges = jnp.stack([jnp.concatenate([src, loops]), jnp.concatenate([dst, loops])], axis=1).astype(jnp.int32)
        W = jax.random.normal(k4, (IN_DIM, OUT_DIM), dtype=jnp.float32) / np.sqrt(IN_DIM)
        b = jnp.zeros((OUT_DIM,), dtype=jnp.float32)
        a = jax.random.normal(k5, (2 * OUT_DIM, 1), dtype=jnp.float32) * np.sqrt(2.0 / (2 * OUT_DIM))
        return {'features': features, 'edges': edges, 'W': W, 'b': b, 'a': a}
    _L0_gnn_all = _L0_gnn_setup()
    _L0_gnn_in = {k: v for k, v in _L0_gnn_all.items() if k in ('W', 'b', 'a')}
    del _L0_gnn_all

    def _L1_gnn_setup():
        import jax, jax.numpy as jnp
        import numpy as np
        import math
        N, E = (625, 6250)
        MUL = 128
        D = MUL + 3 * MUL
        EDGE_ATTR = 32
        HID = 32
        LOG2 = math.log(2.0)

        def ssp(x):
            return jax.nn.softplus(x) - LOG2

        def split_irreps(x):
            return (x[:, :MUL], x[:, MUL:].reshape(x.shape[0], MUL, 3))

        def merge_irreps(x0, x1):
            return jnp.concatenate([x0, x1.reshape(x1.shape[0], MUL * 3)], axis=-1)

        def irrep_linear(x, W0, b0, W1):
            x0, x1 = split_irreps(x)
            y0 = x0 @ W0 + b0
            y1 = jnp.einsum('nuc,uv->nvc', x1, W1)
            return merge_irreps(y0, y1)
        key = jax.random.key(seed)
        ks = iter(jax.random.split(key, 32))

        def randn(shape, scale=1.0):
            return (scale * jax.random.normal(next(ks), shape)).astype(jnp.float32)
        inp = {'x': randn((N, D)), 'edge_sh': randn((E, 4)), 'edge_attr': jax.random.uniform(next(ks), (E, EDGE_ATTR), dtype=jnp.float32), 'edge_index': jax.random.randint(next(ks), (2, E), 0, N, dtype=jnp.int32), 'W_pre0': randn((MUL, MUL), MUL ** (-0.5)), 'b_pre0': jnp.zeros((MUL,), jnp.float32), 'W_pre1': randn((MUL, MUL), MUL ** (-0.5)), 'W_nd0': randn((MUL, MUL), MUL ** (-0.5)), 'b_nd0': jnp.zeros((MUL,), jnp.float32), 'W_nd1': randn((MUL, MUL), MUL ** (-0.5)), 'W_g1': randn((2 * MUL, 2 * MUL), (2 * MUL) ** (-0.5)), 'b_g1': jnp.zeros((2 * MUL,), jnp.float32), 'W_g2': randn((2 * MUL, 2 * MUL), (2 * MUL) ** (-0.5)), 'b_g2': jnp.zeros((2 * MUL,), jnp.float32), 'W_f1': randn((EDGE_ATTR, HID), EDGE_ATTR ** (-0.5)), 'W_f2': randn((HID, 4 * MUL), HID ** (-0.5)), 'W_s1': randn((3 * MUL, HID), (3 * MUL) ** (-0.5)), 'W_s2': randn((HID, 4 * MUL), HID ** (-0.5)), 'W_o0': randn((MUL, MUL), MUL ** (-0.5)), 'b_o0': jnp.zeros((MUL,), jnp.float32), 'W_o1': randn((MUL, MUL), MUL ** (-0.5))}
        return inp
    _L1_gnn_all = _L1_gnn_setup()
    _L1_gnn_in = {k: v for k, v in _L1_gnn_all.items() if k in ('W_pre0', 'b_pre0', 'W_pre1', 'W_nd0', 'b_nd0', 'W_nd1', 'W_g1', 'b_g1', 'W_g2', 'b_g2', 'W_f1', 'W_f2', 'W_s1', 'W_s2', 'W_o0', 'b_o0', 'W_o1')}
    del _L1_gnn_all
    return {'x': x, 'src': src, 'dst': dst, 'edge_attr_32': edge_attr_32, 'edge_attr_4': edge_attr_4, 'L0_gnn_W': _L0_gnn_in['W'], 'L0_gnn_b': _L0_gnn_in['b'], 'L0_gnn_a': _L0_gnn_in['a'], 'L1_gnn_W_pre0': _L1_gnn_in['W_pre0'], 'L1_gnn_b_pre0': _L1_gnn_in['b_pre0'], 'L1_gnn_W_pre1': _L1_gnn_in['W_pre1'], 'L1_gnn_W_nd0': _L1_gnn_in['W_nd0'], 'L1_gnn_b_nd0': _L1_gnn_in['b_nd0'], 'L1_gnn_W_nd1': _L1_gnn_in['W_nd1'], 'L1_gnn_W_g1': _L1_gnn_in['W_g1'], 'L1_gnn_b_g1': _L1_gnn_in['b_g1'], 'L1_gnn_W_g2': _L1_gnn_in['W_g2'], 'L1_gnn_b_g2': _L1_gnn_in['b_g2'], 'L1_gnn_W_f1': _L1_gnn_in['W_f1'], 'L1_gnn_W_f2': _L1_gnn_in['W_f2'], 'L1_gnn_W_s1': _L1_gnn_in['W_s1'], 'L1_gnn_W_s2': _L1_gnn_in['W_s2'], 'L1_gnn_W_o0': _L1_gnn_in['W_o0'], 'L1_gnn_b_o0': _L1_gnn_in['b_o0'], 'L1_gnn_W_o1': _L1_gnn_in['W_o1']}

def reference(x, src, dst, edge_attr_32, edge_attr_4, L0_gnn_W, L0_gnn_b, L0_gnn_a, L1_gnn_W_pre0, L1_gnn_b_pre0, L1_gnn_W_pre1, L1_gnn_W_nd0, L1_gnn_b_nd0, L1_gnn_W_nd1, L1_gnn_W_g1, L1_gnn_b_g1, L1_gnn_W_g2, L1_gnn_b_g2, L1_gnn_W_f1, L1_gnn_W_f2, L1_gnn_W_s1, L1_gnn_W_s2, L1_gnn_W_o0, L1_gnn_b_o0, L1_gnn_W_o1):
    import jax
    import jax.numpy as jnp

    def _L0_gnn_ref(features, edges, W, b, a):
        import jax, jax.numpy as jnp
        import numpy as np
        N = 1250
        IN_DIM = 512
        OUT_DIM = 512
        E_RAND = 20000
        SLOPE = 0.1
        emb = features @ W + b
        a_src = a[:OUT_DIM, 0]
        a_dst = a[OUT_DIM:, 0]
        s_node = emb @ a_src
        t_node = emb @ a_dst
        src = edges[:, 0]
        dst = edges[:, 1]
        e = jnp.exp(jax.nn.leaky_relu(s_node[src] + t_node[dst], negative_slope=SLOPE))
        row_sum = jax.ops.segment_sum(e, src, num_segments=N)
        results = jax.ops.segment_sum(e[:, None] * emb[dst], src, num_segments=N)
        return results / row_sum[:, None]

    def _L1_gnn_ref(x, edge_sh, edge_attr, edge_index, W_pre0, b_pre0, W_pre1, W_nd0, b_nd0, W_nd1, W_g1, b_g1, W_g2, b_g2, W_f1, W_f2, W_s1, W_s2, W_o0, b_o0, W_o1):
        import jax, jax.numpy as jnp
        import numpy as np
        import math
        N, E = (625, 6250)
        MUL = 128
        D = MUL + 3 * MUL
        EDGE_ATTR = 32
        HID = 32
        LOG2 = math.log(2.0)

        def ssp(x):
            return jax.nn.softplus(x) - LOG2

        def split_irreps(x):
            return (x[:, :MUL], x[:, MUL:].reshape(x.shape[0], MUL, 3))

        def merge_irreps(x0, x1):
            return jnp.concatenate([x0, x1.reshape(x1.shape[0], MUL * 3)], axis=-1)

        def irrep_linear(x, W0, b0, W1):
            x0, x1 = split_irreps(x)
            y0 = x0 @ W0 + b0
            y1 = jnp.einsum('nuc,uv->nvc', x1, W1)
            return merge_irreps(y0, y1)
        edge_dst, edge_src = (edge_index[0], edge_index[1])
        old_x = x
        pre = irrep_linear(x, W_pre0, b_pre0, W_pre1)
        p0, p1 = split_irreps(pre)
        pd0 = p0[edge_dst]
        ip1 = jnp.einsum('eum,eum->eu', p1[edge_dst], p1[edge_src]) / 3.0
        s0 = jnp.concatenate([pd0, pd0, ip1], axis=-1)
        x0, x1 = split_irreps(x)
        n1 = jnp.sqrt(jnp.sum(x1 * x1, axis=-1) / 3.0)
        g = jax.nn.silu(jnp.concatenate([x0, n1], -1) @ W_g1 + b_g1) @ W_g2 + b_g2
        xg = merge_irreps(g[:, :MUL], x1 * g[:, MUL:, None])
        x = irrep_linear(xg, W_nd0, b_nd0, W_nd1)
        self_x = x
        w = ssp(edge_attr @ W_f1) @ W_f2 * (ssp(s0 @ W_s1) @ W_s2)
        w1, w2, w3, w4 = jnp.split(w, 4, axis=-1)
        x0e, x1e = split_irreps(x[edge_src])
        sh0, sh1 = (edge_sh[:, 0], edge_sh[:, 1:4])
        out0 = w1 * x0e * sh0[:, None] + w4 * (jnp.einsum('eum,em->eu', x1e, sh1) / jnp.sqrt(3.0))
        out1 = w2[:, :, None] * x0e[:, :, None] * sh1[:, None, :] + w3[:, :, None] * x1e * sh0[:, None, None]
        edge_feat = merge_irreps(out0, out1)
        out = jax.ops.segment_sum(edge_feat, edge_dst, num_segments=old_x.shape[0])
        out = out + self_x
        out = irrep_linear(out, W_o0, b_o0, W_o1)
        return out + old_x
    edge_index = jnp.stack([src, dst])
    edge_index_t = jnp.stack([src, dst], axis=1)
    x = _layernorm(x + _L0_gnn_ref(x, edge_index_t, L0_gnn_W, L0_gnn_b, L0_gnn_a), axis=-1)
    x = _layernorm(x + _L1_gnn_ref(x, edge_attr_4, edge_attr_32, edge_index, L1_gnn_W_pre0, L1_gnn_b_pre0, L1_gnn_W_pre1, L1_gnn_W_nd0, L1_gnn_b_nd0, L1_gnn_W_nd1, L1_gnn_W_g1, L1_gnn_b_g1, L1_gnn_W_g2, L1_gnn_b_g2, L1_gnn_W_f1, L1_gnn_W_f2, L1_gnn_W_s1, L1_gnn_W_s2, L1_gnn_W_o0, L1_gnn_b_o0, L1_gnn_W_o1), axis=-1)
    return x

_drawn_inputs = setup_inputs


def setup_inputs(seed=0):
    import zlib

    import numpy as np

    out = dict(_drawn_inputs(seed))
    spreads = {'L0_gnn_b': (0.0, 0.1),
     'L1_gnn_b_pre0': (0.0, 0.374),
     'L1_gnn_b_nd0': (0.0, 0.1),
     'L1_gnn_b_g1': (0.0, 0.1),
     'L1_gnn_b_g2': (0.0, 0.1),
     'L1_gnn_b_o0': (0.0, 0.37)}
    factors = {}
    for name, (base, spread) in spreads.items():
        noise = np.random.default_rng([zlib.crc32(name.encode()), seed]).standard_normal(out[name].shape)
        drawn = base * np.exp(spread * noise) if base else spread * noise
        out[name] = jnp.asarray(drawn.astype(out[name].dtype))
    for name, factor in factors.items():
        out[name] = (out[name] * factor).astype(out[name].dtype)
    return out
```

```python
import numpy as np
import concourse.bass as bass
from concourse import mybir
from contextlib import ExitStack

F32 = mybir.dt.float32
F32R = mybir.dt.float32r
I32 = mybir.dt.int32
BF16 = mybir.dt.bfloat16
ALU = mybir.AluOpType
ACT = mybir.ActivationFunctionType
AX = mybir.AxisListType

N, D, E = 1250, 512, 20000
MUL, HID, EA, SH = 128, 32, 32, 4
P = 128
NB = -(-N // P)
NPAD = NB * P
LASTN = N - (NB - 1) * P
EP = 125
EC = E // EP
GE = 2 * P
NG = (E + NB * (GE - 1)) // GE
NT = 2 * NG
assert NG % 4 == 0
ROW = EA + SH + 2
IL, JD = EA + SH, EA + SH + 1
XT = D + 2
TC, ONE = D, D + 1
TW = D + 3 * MUL
R = 4
SLOPE = 0.1
EPS = 1e-5
NS = 4


def build(nc, x, src, dst, edge_rows, W, b, a, W_pre0, b_pre0, W_pre1, W_nd0, b_nd0, W_nd1, W_g1, b_g1,
          W_g2, b_g2, W_f1, W_f2, W_s1, W_s2, W_o0, b_o0, W_o1, out):
    ctx = ExitStack()
    with ctx:
        def sb(name, shape, dt=F32, scope=ctx):
            return scope.enter_context(nc.sbuf_tensor(name, shape, dt))

        def sem(name):
            return ctx.enter_context(nc.semaphore(name))

        slots_d = nc.dram_tensor("slots_d", [P * NT, ROW], F32, kind="Internal").ap()
        xt_d = nc.dram_tensor("xt_d", [NPAD, XT], F32, kind="Internal").ap()
        tab_d = nc.dram_tensor("tab_d", [NPAD, TW], F32, kind="Internal").ap()

        ident = sb("ident", [P, P])
        below = sb("below", [P, P])
        ones = sb("ones", [P, P])
        iota_i = sb("iota_i", [P, P], I32)
        iota = sb("iota", [P, P])
        odd32 = sb("odd32", [P, 1])
        upper = sb("upper", [P, 1])
        half = sb("half", [P, 1])
        epsc = sb("epsc", [P, 1])

        W_sb = sb("W_sb", [P, 4, D])
        b_bc = sb("b_bc", [P, D])
        bnd_bc = sb("bnd_bc", [P, MUL])
        bo_bc = sb("bo_bc", [P, MUL])
        bpre = sb("bpre", [P, 1])
        bg1 = sb("bg1", [P, 2])
        bg2 = sb("bg2", [P, 2])
        wpre0 = sb("wpre0", [P, P])
        wpre1 = sb("wpre1", [P, P])
        wnd0 = sb("wnd0", [P, P])
        wnd1 = sb("wnd1", [P, P])
        wo0 = sb("wo0", [P, P])
        wo1 = sb("wo1", [P, P])
        wg1 = sb("wg1", [P, 2, 2 * P])
        wg2 = sb("wg2", [P, 2, 2 * P])
        ws1 = sb("ws1", [P, 3, HID])
        ws1ab = sb("ws1ab", [P, 4, HID])
        ws1c = sb("ws1c", [P, 4, HID])
        wf1 = sb("wf1", [HID, HID])
        wf1r = sb("wf1r", [HID, 4, HID])
        wstack = sb("wstack", [P, 2, D], F32R)

        gblk = sb("gblk", [P, NG], I32)

        ring = sb("ring", [P, R * 2 * TW])
        er = ring[0:EP, 0:EC * ROW].rearrange("p (c w) -> p c w", w=ROW)
        xg = ring[:, 0:R * 2 * XT].rearrange("p (r k w) -> p r k w", r=R, k=2)
        xj = ring[:, :].rearrange("p (r k w) -> p r k w", r=R, k=2)
        ed = sb("ed", [P, R, 2, ROW])

        xt = sb("xt", [P, NB, XT])
        s_bc = sb("s_bc", [P, NB, P])
        acc = sb("acc", [P, NB, D + 1])
        x1 = sb("x1", [P, NB, D])
        selfx = xt[:, :, 0:D]
        p1h = sb("p1h", [P, NB, 3 * MUL], F32R)
        p1l = sb("p1l", [P, NB, 3 * MUL], F32R)
        P0 = sb("P0", [P, NB, P])

        sorting = ExitStack()
        a_bc = sb("a_bc", [P, 2, D], scope=sorting)
        wfull = sb("wfull", [P, 2, D], scope=sorting)
        whi = sb("whi", [P, 2, D], F32R, scope=sorting)
        si = sb("si", [EP, 2, EC], I32, scope=sorting)
        blk_i = sb("blk_i", [EP, EC], I32, scope=sorting)
        loc_i = sb("loc_i", [EP, EC], I32, scope=sorting)
        blk = sb("blk", [EP, EC], scope=sorting)
        oh10 = sb("oh10", [EP, NB, EC], scope=sorting)
        inc = sb("inc", [EP, NB, EC], scope=sorting)
        prev = sb("prev", [EP, NB], scope=sorting)
        rowtot = sb("rowtot", [EP, NB], scope=sorting)
        ones10 = sb("ones10", [P, NB], scope=sorting)
        ngf = sb("ngf", [P, NB], scope=sorting)
        ngi = sb("ngi", [P, NB], I32, scope=sorting)
        ngincl = sb("ngincl", [P, NB], scope=sorting)
        start = sb("start", [P, NB], scope=sorting)
        off = sb("off", [P, NB], scope=sorting)
        slot = sb("slot", [EP, EC], scope=sorting)
        slot_i = sb("slot_i", [EP, EC], I32, scope=sorting)
        slot_t = sb("slot_t", [EP, EC], I32, scope=sorting)
        slot_p = sb("slot_p", [EP, EC], I32, scope=sorting)
        rowpos = sb("rowpos", [EP, EC], I32, scope=sorting)
        cnt = sb("cnt", [P, NG], scope=sorting)
        fill = sb("fill", [P, 22, ROW], scope=sorting)
        stage = sb("stage", [EP, 2, NS, ROW], scope=sorting)
        stage_pos = sb("stage_pos", [EP, 2, NS], I32, scope=sorting)
        wa = sb("wa", [P, 4, 2], scope=sorting)
        wa_bc = sb("wa_bc", [P, 2, D], scope=sorting)
        junk = sb("junk", [P, D], scope=sorting)
        score = sb("score", [P, 2, NB], scope=sorting)
        score0 = sb("score0", [P, 2], scope=sorting)

        ps = ctx.enter_context(nc.psum_tensor("ps", [P, 8, 512], F32))

        consts = sem("consts")
        pool_c = sem("pool_c")
        in_e = sem("in_e")
        in_x = sem("in_x")
        in_w = sem("in_w")
        in_er = sem("in_er")
        fill_ready = sem("fill_ready")
        filled = sem("filled")
        wa_ready = sem("wa_ready")
        wabc_ready = sem("wabc_ready")
        score_ready = sem("score_ready")
        sbc_ready = sem("sbc_ready")
        rowtot_ready = sem("rowtot_ready")
        base_ready = sem("base_ready")
        xt_ready = sem("xt_ready")
        xt_out = sem("xt_out")
        vc = sem("vc")
        vn = [0]

        def link(eng, ins):
            vn[0] += 1
            ins.then_inc(vc, 1)
            eng.wait_ge(vc, vn[0])

        with nc.Block() as block:
            loads = [0]

            @block.sync
            def _(sp):
                sp.dma_start(si[:, 0, :], src.rearrange("(p c) -> p c", p=EP)).then_inc(in_e, 16)
                sp.dma_start(si[:, 1, :], dst.rearrange("(p c) -> p c", p=EP)).then_inc(in_e, 16)
                sp.wait_ge(consts, 1)
                sp.dma_start(xt[:, 0:NB - 1, 0:D], x[0:(NB - 1) * P, :].rearrange("(b p) n -> p b n", p=P)).then_inc(in_x, 16)
                sp.dma_start(xt[0:LASTN, NB - 1, 0:D], x[(NB - 1) * P:N, :]).then_inc(in_x, 16)
                sp.dma_start(er, edge_rows.rearrange("(p c) w -> p c w", p=EP)).then_inc(in_er, 16)
                sp.wait_ge(fill_ready, 1)
                sd = slots_d.rearrange("(p t) w -> p t w", p=P)
                for c in range(NT // 22):
                    sp.dma_start(sd[:, 22 * c:22 * c + 22, :], fill[:, :, :]).then_inc(filled, 16)
                sp.wait_ge(filled, 16 * (NT // 22))
                sp.wait_ge(xt_ready, 1)
                sp.dma_start(xt_d.rearrange("(b p) n -> p b n", p=P), xt[:, :, :]).then_inc(xt_out, 16)
                sp.wait_ge(xt_out, 16)

            @block.scalar
            def _(act):
                def load(dst_, src_):
                    loads[0] += 1
                    act.dma_start(dst_, src_).then_inc(in_w, 16)
                load(W_sb[:, :, :], W.rearrange("(c p) n -> p c n", p=P))
                load(a_bc[:, :, :].rearrange("p c n -> p (c n)"), a.rearrange("n o -> (o n)").partition_broadcast(P))
                load(b_bc[:, :], b.partition_broadcast(P))
                load(bnd_bc[:, :], b_nd0.partition_broadcast(P))
                load(bo_bc[:, :], b_o0.partition_broadcast(P))
                load(bpre[:, :], b_pre0.rearrange("(p o) -> p o", o=1))
                for c in range(2):
                    load(bg1[:, c:c + 1], b_g1[P * c:P * c + P].rearrange("(p o) -> p o", o=1))
                    load(bg2[:, c:c + 1], b_g2[P * c:P * c + P].rearrange("(p o) -> p o", o=1))
                for d_, s_ in ((wpre0, W_pre0), (wpre1, W_pre1), (wnd0, W_nd0), (wnd1, W_nd1), (wo0, W_o0), (wo1, W_o1), (wf1, W_f1)):
                    load(d_[:, :], s_)
                load(wg1[:, :, :], W_g1.rearrange("(c p) n -> p c n", p=P))
                load(wg2[:, :, :], W_g2.rearrange("(c p) n -> p c n", p=P))
                load(ws1[:, :, :], W_s1.rearrange("(c p) n -> p c n", p=P))
                for q in range(4):
                    load(wfull[32 * q:32 * q + 32, 0, :], W_s2)
                    load(wfull[32 * q:32 * q + 32, 1, :], W_f2)
                act.wait_ge(in_w, 16 * loads[0])
                act.wait_ge(wabc_ready, 1)
                act.activation(wa_bc[:, :, :], ps[:, 0:2, :], ACT.Copy).then_inc(wabc_ready, 1)
                act.wait_ge(sbc_ready, 1)
                act.activation(s_bc[:, :, :].rearrange("p b n -> p (b n)"),
                               ps[:, 2:5, :].rearrange("p b n -> p (b n)")[:, 0:NB * P], ACT.Copy).then_inc(sbc_ready, 1)

            NLOADS = 28

            @block.gpsimd
            def _(g):
                g.memset(xt[:, NB - 1, :], 0.0).then_inc(consts, 1)
                g.iota(iota_i[:, :], [[1, P]], base=0, channel_multiplier=0).then_inc(pool_c, 1)
                g.memset(ident[:, :], 0.0).then_inc(pool_c, 1)
                g.memset(ones[:, :], 1.0).then_inc(pool_c, 1)
                g.memset(fill[:, :, :], 0.0).then_inc(pool_c, 1)
                g.wait_ge(pool_c, 4)
                g.tensor_copy(iota[:, :], iota_i[:, :]).then_inc(pool_c, 1)
                g.affine_select(out=ident[:, :], in_=ident[:, :], compare_op=ALU.not_equal, fill=1.0, base=0,
                                pattern=[[-1, P]], channel_multiplier=1).then_inc(pool_c, 1)
                g.affine_select(out=below[:, :], in_=ones[:, :], compare_op=ALU.is_gt, fill=0.0, base=0,
                                pattern=[[1, P]], channel_multiplier=-1).then_inc(pool_c, 1)
                g.memset(fill[:, :, IL], -1.0).then_inc(fill_ready, 1)
                g.memset(odd32[:, :], 0.0).then_inc(pool_c, 1)
                g.memset(upper[:, :], 0.0).then_inc(pool_c, 1)
                g.memset(half[:, :], 0.5).then_inc(pool_c, 1)
                g.memset(epsc[:, :], EPS).then_inc(pool_c, 1)
                g.memset(ones10[:, :], 1.0).then_inc(pool_c, 1)
                g.memset(acc[:, :, :], 0.0).then_inc(pool_c, 1)
                g.wait_ge(pool_c, 13)
                g.affine_select(out=acc[:, NB - 1, D:D + 1], in_=acc[:, NB - 1, D:D + 1], compare_op=ALU.is_gt, fill=1.0,
                                base=LASTN, pattern=[[0, 1]], channel_multiplier=-1).then_inc(pool_c, 1)

            @block.vector
            def _(v):
                v.wait_ge(in_e, 32)
                link(v, v.tensor_scalar(blk_i[:, :], si[:, 0, :], 7, None, ALU.arith_shift_right))
                link(v, v.tensor_scalar(loc_i[:, :], si[:, 0, :], P - 1, None, ALU.bitwise_and))
                link(v, v.tensor_copy(blk[:, :], blk_i[:, :]))
                for q in range(NB):
                    ins = v.tensor_scalar(oh10[:, q, :], blk[:, :], float(q), None, ALU.is_equal)
                link(v, ins)
                v.wait_ge(pool_c, 14)
                v.memset(odd32[32:64, :], 1.0)
                v.memset(odd32[96:128, :], 1.0)
                link(v, v.memset(upper[64:128, :], 1.0))
                link(v, v.tensor_tensor_scan(inc[:, :, :].rearrange("p b c -> p (b c)"),
                                             ones[0:EP, 0:1].to_broadcast([EP, NB * EC]),
                                             oh10[:, :, :].rearrange("p b c -> p (b c)"), 0.0, ALU.mult, ALU.add))
                link(v, v.memset(prev[:, 0:1], 0.0))
                link(v, v.tensor_copy(prev[:, 1:NB], inc[:, 0:NB - 1, EC - 1]))
                link(v, v.tensor_tensor(rowtot[:, :], inc[:, :, EC - 1], prev[:, :], ALU.subtract))
                v.sem_inc(rowtot_ready, 1)
                v.wait_ge(base_ready, 1)
                link(v, v.tensor_scalar(ngi[:, :], ps[:, 5, 0:NB], float(GE - 1), None, ALU.add))
                link(v, v.tensor_scalar(ngi[:, :], ngi[:, :], 8, None, ALU.arith_shift_right))
                link(v, v.tensor_copy(ngf[:, :], ngi[:, :]))
                link(v, v.tensor_tensor_scan(ngincl[:, :], ones10[:, :], ngf[:, :], 0.0, ALU.mult, ALU.add))
                link(v, v.tensor_tensor(start[:, :], ngincl[:, :], ngf[:, :], ALU.subtract))
                link(v, v.tensor_scalar(off[:, :], start[:, :], float(GE), -1.0, ALU.mult, ALU.add))
                link(v, v.tensor_tensor(off[0:EP, :], off[0:EP, :], ps[0:EP, 6, 0:NB], ALU.add))
                link(v, v.tensor_tensor(off[0:EP, :], off[0:EP, :], prev[:, :], ALU.subtract))
                link(v, v.tensor_tensor(inc[:, :, :], inc[:, :, :], off[0:EP, :].unsqueeze(2).to_broadcast([EP, NB, EC]), ALU.add))
                link(v, v.tensor_tensor(inc[:, :, :], inc[:, :, :], oh10[:, :, :], ALU.mult))
                link(v, v.tensor_reduce(slot[:, :], inc[:, :, :].rearrange("p b c -> p c b"), AX.X, ALU.add))
                link(v, v.tensor_copy(slot_i[:, :], slot[:, :]))
                link(v, v.tensor_scalar(slot_t[:, :], slot_i[:, :], 7, None, ALU.arith_shift_right))
                link(v, v.tensor_scalar(slot_p[:, :], slot_i[:, :], P - 1, None, ALU.bitwise_and))
                link(v, v.scalar_tensor_tensor(rowpos[:, :], slot_p[:, :], float(NT), slot_t[:, :], ALU.mult, ALU.add))
                link(v, v.tensor_scalar(cnt[:, :], iota[:, 0:NG], start[:, 1:2], None, ALU.is_ge))
                for q in range(2, NB):
                    link(v, v.scalar_tensor_tensor(cnt[:, :], iota[:, 0:NG], start[:, q:q + 1], cnt[:, :], ALU.is_ge, ALU.add))
                link(v, v.tensor_copy(gblk[:, :], cnt[:, :]))
                v.wait_ge(in_er, 16)
                v.tensor_copy(er[:, :, IL], loc_i[:, :])
                link(v, v.tensor_copy(er[:, :, JD].bitcast(I32), si[:, 1, :]))
                v.wait_ge(in_w, 16 * NLOADS)
                for c in range(4):
                    for h in range(2):
                        link(v, v.scalar_tensor_tensor(junk[:, :], W_sb[:, c, :], 1.0, a_bc[:, h, :], ALU.mult, ALU.mult,
                                                       accum_out=wa[:, c, h:h + 1]))
                for h in range(2):
                    link(v, v.scalar_tensor_tensor(junk[:, :], b_bc[:, :], 1.0, a_bc[:, h, :], ALU.mult, ALU.mult,
                                                   accum_out=score0[:, h:h + 1]))
                v.sem_inc(wa_ready, 1)
                v.wait_ge(wabc_ready, 2)
                v.wait_ge(in_x, 32)
                for q in range(NB):
                    for h in range(2):
                        link(v, v.scalar_tensor_tensor(junk[:, :], xt[:, q, 0:D], 1.0, wa_bc[:, h, :], ALU.mult, ALU.mult,
                                                       accum_out=score[:, h, q:q + 1]))
                for h in range(2):
                    link(v, v.tensor_scalar(score[:, h, :], score[:, h, :], score0[:, h:h + 1], None, ALU.add))
                v.sem_inc(score_ready, 1)
                v.tensor_copy(xt[:, :, TC], score[:, 1, :])
                link(v, v.memset(xt[:, :, ONE], 1.0))
                v.sem_inc(xt_ready, 1)
                link(v, v.tensor_tensor(ws1ab[:, 0, :], ws1[:, 0, :], ws1[:, 1, :], ALU.add))
                for q in range(1, 4):
                    v.tensor_copy(ws1ab[:, q, :], ws1ab[:, 0, :])
                for q in range(4):
                    v.tensor_scalar(ws1c[:, q, :], ws1[:, 2, :], 1.0 / 3.0, None, ALU.mult)
                    v.tensor_copy(wf1r[:, q, :], wf1[:, :])
                link(v, v.tensor_copy(whi[:, :, :], wfull[:, :, :]))
                for q in range(2):
                    v.scalar_tensor_tensor(junk[:, :], whi[:, q, :].bitcast(F32), upper[:, 0:1], wfull[:, q, :], ALU.mult, ALU.subtract)
                    link(v, v.scalar_tensor_tensor(wstack[:, q, :], whi[:, q, :].bitcast(F32), upper[:, 0:1], wfull[:, q, :], ALU.mult, ALU.subtract))
                    link(v, v.tensor_scalar(wstack[:, q, :], wstack[:, q, :].bitcast(F32), -1.0, None, ALU.mult))

            @block.tensor
            def _(pe):
                pe.wait_ge(pool_c, 14)
                pe.wait_ge(rowtot_ready, 1)
                pe.matmul(ps[:, 5, 0:NB], ones[0:EP, :], rowtot[:, :], start=True, stop=True)
                pe.matmul(ps[0:EP, 6, 0:NB], below[0:EP, 0:EP], rowtot[:, :], start=True, stop=True).then_inc(base_ready, 1)
                pe.wait_ge(wa_ready, 1)
                for h in range(2):
                    for c in range(4):
                        mm = pe.matmul(ps[:, h, P * c:P * c + P], wa[:, c, h:h + 1].to_broadcast([P, P]), ident[:, :],
                                       start=True, stop=True)
                mm.then_inc(wabc_ready, 1)
                pe.wait_ge(score_ready, 1)
                for q in range(NB):
                    mm = pe.matmul(ps[:, 2 + q // 4, P * (q % 4):P * (q % 4) + P],
                                   score[:, 0, q:q + 1].to_broadcast([P, P]), ident[:, :], start=True, stop=True)
                mm.then_inc(sbc_ready, 1)
            assert loads[0] == NLOADS, loads[0]

        staged = sem("staged")
        issue = sem("issue")
        scattered = [sem("scattered0"), sem("scattered1")]
        with nc.Block() as block:
            @block.vector
            def _(v):
                def batch(c, h, guard):
                    if guard is not None:
                        v.wait_ge(scattered[h], guard)
                    v.tensor_scalar(stage[:, h, :, :].bitcast(I32), er[:, bass.ds(c, NS), :].bitcast(I32), 0, None, ALU.bitwise_or)
                    v.tensor_copy(stage_pos[:, h, :], rowpos[:, bass.ds(c, NS)]).then_inc(staged, 1)
                batch(0, 0, None)
                batch(NS, 1, None)
                with v.Fori(1, EC // (2 * NS)) as i:
                    for h in range(2):
                        batch(i * (2 * NS) + h * NS, h, i * (16 * NS))

            @block.gpsimd
            def _(g):
                with g.Fori(0, EC // (2 * NS)) as i:
                    for h in range(2):
                        g.wait_ge(staged, i * 2 + (h + 1))
                        g.sem_inc(issue, 1)
                        for k in range(NS):
                            g.indirect_dma_start(slots_d[:, :], bass.IndirectOffsetOnAxis(ap=stage_pos[:, h, k:k + 1], axis=0),
                                                 stage[:, h, k, :], None).then_inc(scattered[h], 16)
                for h in range(2):
                    g.wait_ge(scattered[h], 16 * NS * (EC // (2 * NS)))

        sd2 = slots_d.rearrange("(p t) w -> p t w", p=P)

        sorting.close()
        sweep1 = ExitStack()
        junk2 = sb("junk2", [P, 2, P], scope=sweep1)
        sv = sb("sv", [P, R, 2], scope=sweep1)
        z = sb("z", [P, R, 2], scope=sweep1)
        zl = sb("zl", [P, R, 2], scope=sweep1)
        ev = sb("ev", [P, R, 2], scope=sweep1)
        aw = sb("aw", [P, R, 2, P], scope=sweep1)

        ed_in = [sem(f"ed_in{r}") for r in range(R)]
        xg_in = [sem(f"xg_in{r}") for r in range(R)]
        s_done = sem("s_done")
        z_done = sem("z_done")
        zl_done = sem("zl_done")
        e_done = sem("e_done")
        a_done = sem("a_done")
        row_done = sem("row_done")
        acc_done = sem("acc_done")
        issue1 = sem("issue1")

        def turn(eng, body):
            for g in range(R):
                body(g, g, 1)
            with eng.Fori(0, (NG - R) // R) as j:
                for c in range(R):
                    body(j * R + (R + c), c, j + 2)

        def skewed(eng, early, late, after=None):
            for g in range(R):
                early(g, g, 1)
                if g:
                    late(g - 1, g - 1, 1)
                if after:
                    after(g, g, 1)
            with eng.Fori(0, (NG - R) // R) as j:
                for c in range(R):
                    early(j * R + (R + c), c, j + 2)
                    late(j * R + (R + c - 1), (c - 1) % R, j + (2 if c else 1))
                    if after:
                        after(j * R + (R + c), c, j + 2)
            late(NG - 1, R - 1, NG // R)

        def first(g, m):
            return isinstance(g, int) and g < m

        with nc.Block() as block:
            @block.sync
            def _(sp):
                def load(g, r, n):
                    if not first(g, R):
                        sp.wait_ge(a_done, g - (R - 1))
                    sp.dma_start(ed[:, r, :, :], sd2[:, bass.ds(g * 2, 2), :]).then_inc(ed_in[r], 16)
                turn(sp, load)

            @block.gpsimd
            def _(gp):
                def gather(g, r, n):
                    if not first(g, R):
                        gp.wait_ge(row_done, g - (R - 1))
                        gp.sem_inc(issue1, 1)
                    gp.wait_ge(ed_in[r], n * 16)
                    gp.sem_inc(issue1, 1)
                    for k in range(2):
                        gp.indirect_dma_start(xg[:, r, k, :], None, xt_d[:, :],
                                              bass.IndirectOffsetOnAxis(ap=ed[:, r, k, JD:JD + 1].bitcast(I32), axis=0))\
                          .then_inc(xg_in[r], 16)
                turn(gp, gather)

            @block.vector
            def _(v):
                def early(g, r, n):
                    blk_r = v.value_load(gblk[0:1, bass.ds(g, 1)], min_val=0, max_val=NB - 1)
                    v.wait_ge(ed_in[r], n * 16)
                    for k in range(2):
                        ins = v.scalar_tensor_tensor(junk2[:, k, :], iota[:, :], ed[:, r, k, IL:IL + 1],
                                                     s_bc[:, bass.ds(blk_r, 1), :].rearrange("p b n -> p (b n)"),
                                                     ALU.is_equal, ALU.mult, accum_out=sv[:, r, k:k + 1])
                    ins.then_inc(s_done, 1)
                    v.wait_ge(s_done, g + 1)
                    v.wait_ge(xg_in[r], n * 32)
                    v.tensor_tensor(z[:, r, :], sv[:, r, :], xg[:, r, :, TC], ALU.add).then_inc(z_done, 1)
                    v.wait_ge(z_done, g + 1)
                    v.scalar_tensor_tensor(zl[:, r, :], z[:, r, :], SLOPE, z[:, r, :], ALU.mult, ALU.max).then_inc(zl_done, 1)

                def late(g, r, n):
                    v.wait_ge(e_done, g + 1)
                    for k in range(2):
                        ins = v.tensor_scalar(aw[:, r, k, :], iota[:, :], ed[:, r, k, IL:IL + 1], ev[:, r, k:k + 1],
                                              ALU.is_equal, ALU.mult)
                    ins.then_inc(a_done, 1)

                def later(g, r):
                    blk_r = v.value_load(gblk[0:1, bass.ds(g, 1)], min_val=0, max_val=NB - 1)
                    v.wait_ge(row_done, g + 1)
                    u = r % 2
                    if not first(g, 1):
                        v.wait_ge(acc_done, g)
                    dst_ = acc[:, bass.ds(blk_r, 1), :].rearrange("p b n -> p (b n)")
                    v.tensor_tensor(dst_, dst_, ps[:, 2 * u:2 * u + 2, :].rearrange("p b n -> p (b n)")[:, 0:D + 1],
                                    ALU.add).then_inc(acc_done, 1)

                def late_all(g, r, n):
                    late(g, r, n)
                    if not first(g, 1):
                        later(g - 1, (r - 1) % R)
                skewed(v, early, late_all)
                later(NG - 1, R - 1)

            @block.scalar
            def _(act):
                def body(g, r, n):
                    act.wait_ge(zl_done, g + 1)
                    act.activation(ev[:, r, :], zl[:, r, :], ACT.Exp).then_inc(e_done, 1)
                turn(act, body)

            @block.tensor
            def _(pe):
                def body(g, r, n):
                    u = r % 2
                    pe.wait_ge(a_done, g + 1)
                    if not first(g, 2):
                        pe.wait_ge(acc_done, g - 1)
                    for k in range(2):
                        pe.matmul(ps[:, 2 * u, :], aw[:, r, k, :], xg[:, r, k, 0:D], start=(k == 0), stop=(k == 1))
                        mm = pe.matmul(ps[:, 2 * u + 1, 0:1], aw[:, r, k, :], xg[:, r, k, ONE:ONE + 1],
                                       start=(k == 0), stop=(k == 1))
                    mm.then_inc(row_done, 1)
                turn(pe, body)

        sweep1.close()
        nodes = ExitStack()
        rcp = sb("rcp", [P, 2], scope=nodes)
        ya = sb("ya", [P, 2, D], scope=nodes)
        yT = sb("yT", [P, 2, D], scope=nodes)
        hb = sb("hb", [P, 2, D], scope=nodes)
        stats = sb("stats", [P, 2, 6], scope=nodes)
        mv = sb("mv", [P, 2, 2], scope=nodes)
        sd_ = sb("sd_", [P, 2], scope=nodes)
        rstd = sb("rstd", [P, 2], scope=nodes)
        x1c = sb("x1c", [P, 2, D], scope=nodes)
        xT = sb("xT", [P, 4, GE], scope=nodes)
        sq = sb("sq", [P, 3, GE], scope=nodes)
        n1T = sb("n1T", [P, GE], scope=nodes)
        p0T = sb("p0T", [P, GE], scope=nodes)
        uT = sb("uT", [P, 2, GE], scope=nodes)
        eT = sb("eT", [P, 2, GE], scope=nodes)
        hT = sb("hT", [P, 2, GE], scope=nodes)
        gT = sb("gT", [P, 2, GE], scope=nodes)
        xgT = sb("xgT", [P, 3, GE], scope=nodes)
        tabrow = sb("tabrow", [P, 2, TW], scope=nodes)
        issue3 = sem("issue3")
        q_v = sem("q_v")
        q_a = sem("q_a")
        q_p = sem("q_p")
        tab_out = sem("tab_out")
        VN, AN, PN = 20, 9, 8

        def pair_psum(k0, n):
            return ps[:, k0:k0 + n, :]

        with nc.Block() as block:
            @block.vector
            def _(v):
                link(v, v.tensor_tensor(xt[:, :, 0:D], xt[:, :, 0:D], b_bc[:, :].unsqueeze(1).to_broadcast([P, NB, D]), ALU.add))
                with v.Fori(0, NB // 2) as q:
                    vb = q * VN
                    step = [0]

                    def done(ins):
                        step[0] += 1
                        ins.then_inc(q_v, 1)

                    def own():
                        v.wait_ge(q_v, vb + step[0])
                    two = bass.ds(q * 2, 2)
                    done(v.tensor_scalar(rcp[:, :], acc[:, two, D], 1.0, None, ALU.mult))
                    own()
                    done(v.reciprocal(rcp[:, :], rcp[:, :]))
                    own()
                    v.tensor_scalar(ya[:, 0, :], acc[:, bass.ds(q * 2, 1), 0:D].rearrange("p b n -> p (b n)"), rcp[:, 0:1], None, ALU.mult)
                    done(v.tensor_scalar(ya[:, 1, :], acc[:, bass.ds(q * 2 + 1, 1), 0:D].rearrange("p b n -> p (b n)"), rcp[:, 1:2], None, ALU.mult))
                    v.wait_ge(q_p, q * PN + 2)
                    done(v.tensor_tensor(hb[:, :, :], xt[:, two, 0:D], pair_psum(2, 2), ALU.add))
                    own()
                    for k in range(2):
                        ins = v.bn_stats(stats[:, k, :], hb[:, k, :])
                    done(ins)
                    own()
                    v.sem_inc(issue3, 1)
                    for k in range(2):
                        ins = v.bn_aggr(mv[:, k, :], stats[:, k, :])
                    done(ins)
                    v.wait_ge(q_a, q * AN + 2)
                    done(v.reciprocal(rstd[:, :], sd_[:, :]))
                    own()
                    for k in range(2):
                        ins = v.tensor_scalar(x1c[:, k, :], hb[:, k, :], mv[:, k, 0:1], rstd[:, k:k + 1], ALU.subtract, ALU.mult)
                    done(ins)
                    own()
                    done(v.tensor_scalar(x1[:, two, :], x1c[:, :, :], 1.0, None, ALU.mult))
                    v.wait_ge(q_a, q * AN + 3)
                    done(v.tensor_tensor(sq[:, :, :], xT[:, 1:4, :], xT[:, 1:4, :], ALU.mult))
                    own()
                    done(v.tensor_tensor(sq[:, 0, :], sq[:, 0, :], sq[:, 1, :], ALU.add))
                    own()
                    done(v.tensor_tensor(sq[:, 0, :], sq[:, 0, :], sq[:, 2, :], ALU.add))
                    v.wait_ge(q_p, q * PN + 4)
                    for k in range(2):
                        v.tensor_copy(tabrow[:, k, D:TW], ps[:, 6 + k, 0:3 * MUL])
                    done(v.tensor_scalar(p1h[:, two, :], ps[:, 6:8, 0:3 * MUL], 1.0, None, ALU.mult))
                    own()
                    done(v.tensor_tensor(p1l[:, two, :], ps[:, 6:8, 0:3 * MUL], p1h[:, two, :].bitcast(F32), ALU.subtract))
                    v.wait_ge(q_a, q * AN + 7)
                    done(v.tensor_scalar(eT[:, :, :], eT[:, :, :], 1.0, None, ALU.add))
                    own()
                    done(v.reciprocal(eT[:, :, :], eT[:, :, :]))
                    own()
                    done(v.tensor_tensor(hT[:, :, :], uT[:, :, :], eT[:, :, :], ALU.mult))
                    v.wait_ge(q_a, q * AN + 9)
                    done(v.tensor_tensor(xgT[:, :, :], xT[:, 1:4, :], gT[:, 1, :].unsqueeze(1).to_broadcast([P, 3, GE]), ALU.mult))
                    v.wait_ge(q_p, q * PN + 8)
                    v.tensor_copy(tabrow[:, :, P:D], ps[:, 0:2, P:D])
                    done(v.tensor_tensor(tabrow[:, :, 0:P], ps[:, 0:2, 0:P], bnd_bc[:, :].unsqueeze(1).to_broadcast([P, 2, P]), ALU.add))
                    own()
                    done(v.tensor_scalar(selfx[:, two, :], tabrow[:, :, 0:D], 1.0, None, ALU.mult))
                    assert step[0] == VN, step[0]
                    v.wait_ge(tab_out, q * 16 + 16)

            @block.scalar
            def _(act):
                with act.Fori(0, NB // 2) as q:
                    step = [0]

                    def done(ins):
                        step[0] += 1
                        ins.then_inc(q_a, 1)
                    act.wait_ge(q_p, q * PN + 1)
                    done(act.activation(yT[:, :, :], pair_psum(0, 2), ACT.Copy))
                    act.wait_ge(q_v, q * VN + 6)
                    done(act.activation(sd_[:, :], mv[:, :, 1], ACT.Sqrt, bias=epsc[:, 0:1]))
                    act.wait_ge(q_p, q * PN + 3)
                    done(act.activation(xT[:, :, :], pair_psum(0, 2), ACT.Copy))
                    act.wait_ge(q_v, q * VN + 12)
                    done(act.activation(n1T[:, :], sq[:, 0, :], ACT.Sqrt, scale=1.0 / 3.0))
                    act.wait_ge(q_p, q * PN + 4)
                    done(act.activation(p0T[:, :], ps[:, 2, 0:GE], ACT.Identity, bias=bpre[:, 0:1]))
                    act.wait_ge(q_p, q * PN + 5)
                    for h in range(2):
                        ins = act.activation(uT[:, h, :], ps[:, 3, GE * h:GE * h + GE], ACT.Identity, bias=bg1[:, h:h + 1])
                    done(ins)
                    act.wait_ge(q_a, q * AN + 6)
                    done(act.activation(eT[:, :, :], uT[:, :, :], ACT.Exp, scale=-1.0))
                    act.wait_ge(q_p, q * PN + 6)
                    done(act.activation(P0[:, bass.ds(q * 2, 2), :], ps[:, 2, GE:512].rearrange("p (k n) -> p k n", k=2), ACT.Copy))
                    act.wait_ge(q_p, q * PN + 7)
                    for h in range(2):
                        ins = act.activation(gT[:, h, :], ps[:, 4, GE * h:GE * h + GE], ACT.Identity, bias=bg2[:, h:h + 1])
                    done(ins)
                    for _ in range(AN - step[0]):
                        act.sem_inc(q_a, 1)

            @block.tensor
            def _(pe):
                with pe.Fori(0, NB // 2) as q:
                    pe.wait_ge(q_v, q * VN + 3)
                    for k in range(2):
                        for c in range(4):
                            mm = pe.transpose(ps[:, k, P * c:P * c + P], ya[:, k, P * c:P * c + P], ident[:, :])
                    mm.then_inc(q_p, 1)
                    pe.wait_ge(q_a, q * AN + 1)
                    for k in range(2):
                        for c in range(4):
                            mm = pe.matmul(ps[:, 2 + k, :], yT[:, k, P * c:P * c + P], W_sb[:, c, :], start=(c == 0), stop=(c == 3))
                    mm.then_inc(q_p, 1)
                    pe.wait_ge(q_v, q * VN + 8)
                    for c in range(4):
                        for k in range(2):
                            s_ = x1c[:, k, 0:P] if c == 0 else x1c[:, k, P + c - 1:D:3]
                            mm = pe.transpose(ps[:, c // 2, GE * (c % 2) + P * k:GE * (c % 2) + P * k + P], s_, ident[:, :])
                    mm.then_inc(q_p, 1)
                    pe.wait_ge(q_a, q * AN + 3)
                    pe.matmul(ps[:, 2, 0:GE], wpre0[:, :], xT[:, 0, :], start=True, stop=True)
                    for k in range(2):
                        for c in range(3):
                            mm = pe.matmul(ps[:, 6 + k, P * c:P * c + P], xT[:, 1 + c, P * k:P * k + P], wpre1[:, :], start=True, stop=True)
                    mm.then_inc(q_p, 1)
                    pe.wait_ge(q_a, q * AN + 4)
                    for h in range(2):
                        pe.matmul(ps[:, 3, GE * h:GE * h + GE], wg1[:, 0, P * h:P * h + P], xT[:, 0, :], start=True, stop=False)
                        mm = pe.matmul(ps[:, 3, GE * h:GE * h + GE], wg1[:, 1, P * h:P * h + P], n1T[:, :], start=False, stop=True)
                    mm.then_inc(q_p, 1)
                    pe.wait_ge(q_a, q * AN + 5)
                    for k in range(2):
                        mm = pe.matmul(ps[:, 2, GE + P * k:GE + P * k + P], p0T[:, P * k:P * k + P],
                                       ws1ab[:, :, :].rearrange("p q h -> p (q h)"), start=True, stop=True)
                    mm.then_inc(q_p, 1)
                    pe.wait_ge(q_v, q * VN + 17)
                    for h in range(2):
                        for c in range(2):
                            mm = pe.matmul(ps[:, 4, GE * h:GE * h + GE], wg2[:, c, P * h:P * h + P], hT[:, c, :], start=(c == 0), stop=(c == 1))
                    mm.then_inc(q_p, 1)
                    pe.wait_ge(q_v, q * VN + 18)
                    for k in range(2):
                        pe.matmul(ps[:, k, 0:P], gT[:, 0, P * k:P * k + P], wnd0[:, :], start=True, stop=True)
                        for c in range(3):
                            mm = pe.matmul(ps[:, k, P * (c + 1):P * (c + 2)], xgT[:, c, P * k:P * k + P], wnd1[:, :], start=True, stop=True)
                    mm.then_inc(q_p, 1)

            @block.sync
            def _(sp):
                with sp.Fori(0, NB // 2) as q:
                    sp.wait_ge(q_v, q * VN + 19)
                    sp.dma_start(tab_d[bass.ds(q * GE, GE), :].rearrange("(k p) w -> p k w", p=P), tabrow[:, :, :]).then_inc(tab_out, 16)
                sp.wait_ge(tab_out, 16 * (NB // 2))

            @block.gpsimd
            def _(gp):
                gp.wait_ge(tab_out, 16 * (NB // 2))
                gp.memset(acc[:, :, :], 0.0)

        nodes.close()
        sweep2 = ExitStack()
        oh = sb("oh", [P, R, 2, P], scope=sweep2)
        ohT = sb("ohT", [P, R, GE], F32R, scope=sweep2)
        eaT = sb("eaT", [HID, R, GE], scope=sweep2)
        P0c = sb("P0c", [P, R, P], scope=sweep2)
        prod = sb("prod", [P, 2, 3 * MUL], scope=sweep2)
        ipT = sb("ipT", [P, GE], scope=sweep2)
        absx = sb("absx", [P, 512], scope=sweep2)
        expx = sb("expx", [P, 512], scope=sweep2)
        lnx = sb("lnx", [P, 512], scope=sweep2)
        sp_ = sb("sp_", [P, 512], scope=sweep2)
        sph = sb("sph", [P, 512], F32R, scope=sweep2)
        hcomb = sb("hcomb", [P, 2, 512], F32R, scope=sweep2)
        S_sb = sb("S_sb", [P, 2, D], scope=sweep2)
        wv = sb("wv", [P, 2, D], scope=sweep2)
        t1 = sb("t1", [P, 2, P], scope=sweep2)
        dd = sb("dd", [P, 3, 2, P], scope=sweep2)
        bb = sb("bb", [P, 2, P], scope=sweep2)
        cc = sb("cc", [P, 2, 3 * P], scope=sweep2)
        msg = W_sb[:, :, :].rearrange("p (u k) n -> p u k n", u=2)

        ed2 = [sem(f"ed2_{r}") for r in range(R)]
        xj_in = [sem(f"xj_in{r}") for r in range(R)]
        issue2 = sem("issue2")
        oh_ready = sem("oh_ready")
        tr_ready = sem("tr_ready")
        ohT_ready = sem("ohT_ready")
        eaT_ready = sem("eaT_ready")
        pi_ready = sem("pi_ready")
        prod_ready = sem("prod_ready")
        ip_ready = sem("ip_ready")
        ipT_ready = sem("ipT_ready")
        hid_ready = sem("hid_ready")
        abs_done = sem("abs_done")
        exp_done = sem("exp_done")
        ln_done = sem("ln_done")
        sp_done = sem("sp_done")
        sph_done = sem("sph_done")
        comb_ready = sem("comb_ready")
        s_ready = sem("s_ready")
        s_copied = sem("s_copied")
        f_ready = sem("f_ready")
        w_done = sem("w_done")
        lv = sem("lv")
        msg_ready = sem("msg_ready")
        sum_ready = sem("sum_ready")
        acc2_done = sem("acc2_done")
        LV = 4
        psT, psI, psH, psS = ps[:, 2, :], ps[:, 3, :], ps[:, 4, :], ps[:, 5, :]

        with nc.Block() as block:
            @block.sync
            def _(sp):
                def load(g, r, n):
                    if not first(g, R):
                        sp.wait_ge(msg_ready, g - (R - 1))
                    sp.dma_start(ed[:, r, :, :], sd2[:, bass.ds(g * 2, 2), :]).then_inc(ed2[r], 16)
                turn(sp, load)

            @block.gpsimd
            def _(gp):
                def gather(g, r, n):
                    gp.wait_ge(ed2[r], n * 16)
                    gp.sem_inc(issue2, 1)
                    for k in range(2):
                        gp.indirect_dma_start(xj[:, r, k, :], None, tab_d[:, :],
                                              bass.IndirectOffsetOnAxis(ap=ed[:, r, k, JD:JD + 1].bitcast(I32), axis=0))\
                          .then_inc(xj_in[r], 16)
                turn(gp, gather)

            @block.tensor
            def _(pe):
                def early(g, r, n):
                    blk_r = pe.value_load(gblk[0:1, bass.ds(g, 1)], min_val=0, max_val=NB - 1)
                    pe.wait_ge(oh_ready, g + 1)
                    if not first(g, 1):
                        pe.wait_ge(eaT_ready, g)
                    for k in range(2):
                        pe.transpose(psT[:, P * k:P * k + P], oh[:, r, k, :], ident[:, :])
                    for k in range(2):
                        mm = pe.transpose(psT[0:EA, GE + P * k:GE + P * k + P], ed[:, r, k, 0:EA], ident[:, :])
                    mm.then_inc(tr_ready, 1)
                    pe.wait_ge(ohT_ready, g + 1)
                    if not first(g, 1):
                        pe.wait_ge(prod_ready, g)
                    for k in range(2):
                        for part, tab in enumerate((p1h, p1l)):
                            mm = pe.matmul(ps[:, k, 0:3 * MUL], ohT[:, r, P * k:P * k + P],
                                           tab[:, bass.ds(blk_r, 1), :].rearrange("p b n -> p (b n)"),
                                           start=(part == 0), stop=(part == 1))
                    mm.then_inc(pi_ready, 1)
                    pe.wait_ge(prod_ready, g + 1)
                    if not first(g, 1):
                        pe.wait_ge(ipT_ready, g)
                    for k in range(2):
                        for c in range(3):
                            mm = pe.matmul(psI[:, P * k:P * k + P], prod[:, k, P * c:P * c + P], ident[:, :],
                                           start=(c == 0), stop=(c == 2))
                    mm.then_inc(ip_ready, 1)
                    pe.wait_ge(eaT_ready, g + 1)
                    pe.wait_ge(ipT_ready, g + 1)
                    if not first(g, 1):
                        pe.wait_ge(sp_done, g)
                    pe.matmul(psH[:, 0:GE], ws1c[:, :, :].rearrange("p q h -> p (q h)"), ipT[:, :], start=True, stop=False)
                    pe.matmul(psH[:, 0:GE], P0c[:, r, :], ohT[:, r, :].bitcast(F32), start=False, stop=True)
                    pe.matmul(psH[:, GE:512], wf1r[:, :, :].rearrange("p q h -> p (q h)"), eaT[:, r, :],
                              start=True, stop=True).then_inc(hid_ready, 1)

                def late(g, r, n):
                    u = r % 2
                    pe.wait_ge(comb_ready, g + 1)
                    for k in range(2):
                        if not (k == 0 and first(g, 1)):
                            pe.wait_ge(s_copied, g * 2 + k)
                        pe.matmul(psS, hcomb[:, u, P * k:P * k + P], wstack[:, 0, :], start=True, stop=True).then_inc(s_ready, 1)
                        if k == 0 and not first(g, 1):
                            pe.wait_ge(w_done, g)
                        mm = pe.matmul(ps[:, 6 + k, :], hcomb[:, u, GE + P * k:GE + P * k + P], wstack[:, 1, :], start=True, stop=True)
                    mm.then_inc(f_ready, 1)

                def last(g, r):
                    u = r % 2
                    pe.wait_ge(msg_ready, g + 1)
                    if not first(g, 1):
                        pe.wait_ge(acc2_done, g)
                    for k in range(2):
                        mm = pe.matmul(ps[:, 3, :], oh[:, r, k, :], msg[:, u, k, :], start=(k == 0), stop=(k == 1))
                    mm.then_inc(sum_ready, 1)

                def tail(g, r, n):
                    late(g, r, n)
                    if not first(g, 1):
                        last(g - 1, (r - 1) % R)

                def head(g, r, n):
                    if not first(g, 3):
                        pe.wait_ge(acc2_done, g - 2)
                    early(g, r, n)
                skewed(pe, head, tail)
                last(NG - 1, R - 1)

            @block.scalar
            def _(act):
                def early(g, r, n):
                    blk_r = act.value_load(gblk[0:1, bass.ds(g, 1)], min_val=0, max_val=NB - 1)
                    act.activation(P0c[:, r, :], P0[:, bass.ds(blk_r, 1), :].rearrange("p b n -> p (b n)"), ACT.Copy)
                    act.wait_ge(tr_ready, g + 1)
                    act.activation(ohT[:, r, :], psT[:, 0:GE], ACT.Copy).then_inc(ohT_ready, 1)
                    act.activation(eaT[:, r, :], psT[0:EA, GE:512], ACT.Copy).then_inc(eaT_ready, 1)
                    act.wait_ge(ip_ready, g + 1)
                    act.activation(ipT[:, :], psI[:, 0:GE], ACT.Copy).then_inc(ipT_ready, 1)
                    act.wait_ge(hid_ready, g + 1)
                    act.activation(absx[:, :], psH, ACT.Abs).then_inc(abs_done, 1)
                    act.wait_ge(abs_done, g + 1)
                    act.activation(expx[:, :], absx[:, :], ACT.Exp, scale=-1.0).then_inc(exp_done, 1)
                    act.wait_ge(exp_done, g + 1)
                    if not first(g, 1):
                        act.wait_ge(sp_done, g)
                    act.activation(lnx[:, :], expx[:, :], ACT.Ln, scale=0.5, bias=half[:, 0:1]).then_inc(ln_done, 1)
                    act.wait_ge(sp_done, g + 1)
                    if not first(g, 1):
                        act.wait_ge(comb_ready, g)
                    act.activation(sph[:, :], sp_[:, :], ACT.Copy).then_inc(sph_done, 1)

                def late(g, r, n):
                    for k in range(2):
                        act.wait_ge(s_ready, g * 2 + (k + 1))
                        if k == 0 and not first(g, 1):
                            act.wait_ge(w_done, g)
                        act.activation(S_sb[:, k, :], psS, ACT.Copy).then_inc(s_copied, 1)
                skewed(act, early, late)

            @block.vector
            def _(v):
                def sh(r, k, m):
                    return ed[:, r, k, EA + m:EA + m + 1]

                def early(g, r, n):
                    v.wait_ge(ed2[r], n * 16)
                    if not first(g, R):
                        v.wait_ge(sum_ready, g - (R - 1))
                    for k in range(2):
                        ins = v.tensor_scalar(oh[:, r, k, :], iota[:, :], ed[:, r, k, IL:IL + 1], None, ALU.is_equal)
                    ins.then_inc(oh_ready, 1)
                    v.wait_ge(xj_in[r], n * 32)
                    v.wait_ge(pi_ready, g + 1)
                    if not first(g, 1):
                        v.wait_ge(ip_ready, g)
                    v.tensor_tensor(prod[:, :, :], ps[:, 0:2, 0:3 * MUL], xj[:, r, :, D:TW], ALU.mult).then_inc(prod_ready, 1)
                    v.wait_ge(ln_done, g + 1)
                    v.scalar_tensor_tensor(sp_[:, :], psH, 0.0, lnx[:, :], ALU.max, ALU.add).then_inc(sp_done, 1)

                def split(g, r, n):
                    u = r % 2
                    v.wait_ge(sph_done, g + 1)
                    if not first(g, 2):
                        v.wait_ge(f_ready, g - 1)
                    v.scalar_tensor_tensor(hcomb[:, u, :], sph[:, :].bitcast(F32), odd32[:, 0:1], sp_[:, :],
                                           ALU.mult, ALU.subtract).then_inc(comb_ready, 1)

                def late(g, r, n):
                    u = r % 2
                    v.wait_ge(f_ready, g + 1)
                    v.wait_ge(s_copied, g * 2 + 2)
                    v.tensor_tensor(wv[:, :, :], S_sb[:, :, :], ps[:, 6:8, :], ALU.mult).then_inc(w_done, 1)
                    if not first(g, 2):
                        v.wait_ge(sum_ready, g - 1)
                    v.wait_ge(w_done, g + 1)
                    lb = g * LV
                    for k in range(2):
                        v.tensor_scalar(dd[:, 0, k, :], xj[:, r, k, P:2 * P], sh(r, k, 1), None, ALU.mult)
                        v.scalar_tensor_tensor(t1[:, k, :], xj[:, r, k, 0:P], sh(r, k, 0), wv[:, k, 0:P], ALU.mult, ALU.mult)
                        v.scalar_tensor_tensor(cc[:, k, :].rearrange("p (m n) -> p m n", m=3),
                                               xj[:, r, k, P:D].rearrange("p (m n) -> p m n", m=3), sh(r, k, 0),
                                               wv[:, k, 2 * P:3 * P].unsqueeze(1).to_broadcast([P, 3, P]), ALU.mult, ALU.mult)
                    v.tensor_tensor(bb[:, :, :], wv[:, :, P:2 * P], xj[:, r, :, 0:P], ALU.mult).then_inc(lv, 1)
                    v.wait_ge(lv, lb + 1)
                    for k in range(2):
                        ins = v.scalar_tensor_tensor(dd[:, 1, k, :], xj[:, r, k, 2 * P:3 * P], sh(r, k, 2), dd[:, 0, k, :], ALU.mult, ALU.add)
                    ins.then_inc(lv, 1)
                    for m in range(3):
                        for k in range(2):
                            v.scalar_tensor_tensor(msg[:, u, k, P * (m + 1):P * (m + 2)], bb[:, k, :], sh(r, k, m + 1),
                                                   cc[:, k, P * m:P * m + P], ALU.mult, ALU.add)
                    v.wait_ge(lv, lb + 2)
                    for k in range(2):
                        ins = v.scalar_tensor_tensor(dd[:, 2, k, :], xj[:, r, k, 3 * P:D], sh(r, k, 3), dd[:, 1, k, :], ALU.mult, ALU.add)
                    ins.then_inc(lv, 1)
                    v.wait_ge(lv, lb + 3)
                    v.scalar_tensor_tensor(dd[:, 0, :, :], dd[:, 2, :, :], 1.0 / 3.0 ** 0.5, wv[:, :, 3 * P:D], ALU.mult, ALU.mult).then_inc(lv, 1)
                    v.wait_ge(lv, lb + 4)
                    v.tensor_tensor(msg[:, u, :, 0:P], t1[:, :, :], dd[:, 0, :, :], ALU.add).then_inc(msg_ready, 1)

                def last(g, r):
                    blk_r = v.value_load(gblk[0:1, bass.ds(g, 1)], min_val=0, max_val=NB - 1)
                    v.wait_ge(sum_ready, g + 1)
                    if not first(g, 1):
                        v.wait_ge(acc2_done, g)
                    dst_ = acc[:, bass.ds(blk_r, 1), 0:D].rearrange("p b n -> p (b n)")
                    v.tensor_tensor(dst_, dst_, ps[:, 3, :], ALU.add).then_inc(acc2_done, 1)

                def tail(g, r, n):
                    late(g, r, n)
                    if not first(g, 1):
                        last(g - 1, (r - 1) % R)
                skewed(v, early, tail, split)
                last(NG - 1, R - 1)

        sweep2.close()
        ya = sb("ya2", [P, 2, D])
        yT = sb("yT2", [P, 2, D])
        hb = sb("hb2", [P, 2, D])
        stats = sb("stats2", [P, 2, 6])
        mv = sb("mv2", [P, 2, 2])
        sd_ = sb("sd2_", [P, 2])
        rstd = sb("rstd2", [P, 2])
        rcp = sb("rcp2", [P, 2])
        x1c = sb("x1c2", [P, 2, D])
        f_v = sem("f_v")
        f_a = sem("f_a")
        f_p = sem("f_p")
        out_done = sem("out_done")
        FV = 8
        with nc.Block() as block:
            @block.vector
            def _(v):
                with v.Fori(0, NB // 2) as q:
                    step = [0]
                    fb = q * FV

                    def done(ins):
                        step[0] += 1
                        ins.then_inc(f_v, 1)

                    def own():
                        v.wait_ge(f_v, fb + step[0])
                    two = bass.ds(q * 2, 2)
                    done(v.tensor_tensor(ya[:, :, :], acc[:, two, 0:D], selfx[:, two, :], ALU.add))
                    v.scalar_tensor_tensor(hb[:, :, 0:P], x1[:, two, 0:P], 2.0, bo_bc[:, :].unsqueeze(1).to_broadcast([P, 2, P]),
                                           ALU.mult, ALU.add)
                    done(v.tensor_scalar(hb[:, :, P:D], x1[:, two, P:D], 2.0, None, ALU.mult))
                    own()
                    v.wait_ge(f_p, q * 2 + 2)
                    v.tensor_tensor(hb[:, :, 0:P], hb[:, :, 0:P], ps[:, 2:4, 0:P], ALU.add)
                    for k in range(2):
                        ins = v.tensor_tensor(hb[:, k, P:D].rearrange("p (n m) -> p n m", m=3),
                                              hb[:, k, P:D].rearrange("p (n m) -> p n m", m=3),
                                              ps[:, 2 + k, P:D].rearrange("p (m n) -> p n m", m=3), ALU.add)
                    done(ins)
                    own()
                    for k in range(2):
                        ins = v.bn_stats(stats[:, k, :], hb[:, k, :])
                    done(ins)
                    own()
                    v.sem_inc(issue3, 1)
                    for k in range(2):
                        ins = v.bn_aggr(mv[:, k, :], stats[:, k, :])
                    done(ins)
                    v.wait_ge(f_a, q * 2 + 2)
                    done(v.reciprocal(rstd[:, :], sd_[:, :]))
                    own()
                    for k in range(2):
                        ins = v.tensor_scalar(x1c[:, k, :], hb[:, k, :], mv[:, k, 0:1], rstd[:, k:k + 1], ALU.subtract, ALU.mult)
                    done(ins)
                    v.wait_ge(out_done, q * 16 + 16)
                    done(v.tensor_copy(rcp[:, :], rstd[:, :]))
                    assert step[0] == FV

            @block.scalar
            def _(act):
                with act.Fori(0, NB // 2) as q:
                    act.wait_ge(f_p, q * 2 + 1)
                    act.activation(yT[:, :, :], pair_psum(0, 2), ACT.Copy).then_inc(f_a, 1)
                    act.wait_ge(f_v, q * FV + 5)
                    act.activation(sd_[:, :], mv[:, :, 1], ACT.Sqrt, bias=epsc[:, 0:1]).then_inc(f_a, 1)

            @block.tensor
            def _(pe):
                with pe.Fori(0, NB // 2) as q:
                    pe.wait_ge(f_v, q * FV + 1)
                    for k in range(2):
                        for c in range(4):
                            mm = pe.transpose(ps[:, k, P * c:P * c + P], ya[:, k, P * c:P * c + P], ident[:, :])
                    mm.then_inc(f_p, 1)
                    pe.wait_ge(f_a, q * 2 + 1)
                    for k in range(2):
                        for c in range(4):
                            mm = pe.matmul(ps[:, 2 + k, P * c:P * c + P], yT[:, k, P * c:P * c + P],
                                           (wo1 if c else wo0)[:, :], start=True, stop=True)
                    mm.then_inc(f_p, 1)

            @block.sync
            def _(sp):
                with sp.Fori(0, NB // 2) as q:
                    sp.wait_ge(f_v, q * FV + 7)
                    sp.dma_start(out[bass.ds(q * GE, GE), :].rearrange("(k p) w -> p k w", p=P), x1c[:, :, :]).then_inc(out_done, 16)
                sp.wait_ge(out_done, 16 * (NB // 2))


def kernel(x, src, dst, edge_attr_32, edge_attr_4, L0_gnn_W, L0_gnn_b, L0_gnn_a, L1_gnn_W_pre0, L1_gnn_b_pre0,
           L1_gnn_W_pre1, L1_gnn_W_nd0, L1_gnn_b_nd0, L1_gnn_W_nd1, L1_gnn_W_g1, L1_gnn_b_g1, L1_gnn_W_g2,
           L1_gnn_b_g2, L1_gnn_W_f1, L1_gnn_W_f2, L1_gnn_W_s1, L1_gnn_W_s2, L1_gnn_W_o0, L1_gnn_b_o0, L1_gnn_W_o1):
    import concourse.bacc as bacc
    from concourse.bass_utils import run_bass_kernel_spmd as run
    nc = bacc.Bacc("TRN2", target_bir_lowering=False, num_devices=1)
    ea, es = np.asarray(edge_attr_32), np.asarray(edge_attr_4)
    edge_rows = np.concatenate([ea, es, np.zeros((E, ROW - EA - SH), ea.dtype)], axis=1)
    arrays = {"x": x, "src": src, "dst": dst, "edge_rows": edge_rows, "W": L0_gnn_W, "b": L0_gnn_b, "a": L0_gnn_a,
              "W_pre0": L1_gnn_W_pre0, "b_pre0": L1_gnn_b_pre0, "W_pre1": L1_gnn_W_pre1, "W_nd0": L1_gnn_W_nd0,
              "b_nd0": L1_gnn_b_nd0, "W_nd1": L1_gnn_W_nd1, "W_g1": L1_gnn_W_g1, "b_g1": L1_gnn_b_g1,
              "W_g2": L1_gnn_W_g2, "b_g2": L1_gnn_b_g2, "W_f1": L1_gnn_W_f1, "W_f2": L1_gnn_W_f2,
              "W_s1": L1_gnn_W_s1, "W_s2": L1_gnn_W_s2, "W_o0": L1_gnn_W_o0, "b_o0": L1_gnn_b_o0, "W_o1": L1_gnn_W_o1}
    arrays = {n: np.ascontiguousarray(v) for n, v in arrays.items()}
    args = [nc.dram_tensor(n, v.shape, mybir.dt.from_np(v.dtype), kind="ExternalInput").ap() for n, v in arrays.items()]
    o = nc.dram_tensor("out", [NPAD, D], F32, kind="ExternalOutput").ap()
    build(nc, *args, o)
    r = run(nc, [arrays], core_ids=[0])
    return r.results[0]["out"][:N]
```

```python
import numpy as np
import concourse.bass as bass
from concourse import mybir
from contextlib import ExitStack

F32 = mybir.dt.float32
F32R = mybir.dt.float32r
I32 = mybir.dt.int32
BF16 = mybir.dt.bfloat16
ALU = mybir.AluOpType
ACT = mybir.ActivationFunctionType
AX = mybir.AxisListType

N, D, E = 1250, 512, 20000
MUL, HID, EA, SH = 128, 32, 32, 4
P = 128
NB = -(-N // P)
NPAD = NB * P
LASTN = N - (NB - 1) * P
EP = 125
EC = E // EP
GE = 2 * P
NG = (E + NB * (GE - 1)) // GE
NT = 2 * NG
assert NG % 4 == 0
ROW = EA + SH + 2
IL, JD = EA + SH, EA + SH + 1
XT = D + 2
TC, ONE = D, D + 1
TW = D + 3 * MUL
R = 4
SLOPE = 0.1
EPS = 1e-5
NS = 4


def build(nc, x, src, dst, edge_rows, W, b, a, W_pre0, b_pre0, W_pre1, W_nd0, b_nd0, W_nd1, W_g1, b_g1,
          W_g2, b_g2, W_f1, W_f2, W_s1, W_s2, W_o0, b_o0, W_o1, out):
    ctx = ExitStack()
    with ctx:
        def sb(name, shape, dt=F32, scope=ctx):
            return scope.enter_context(nc.sbuf_tensor(name, shape, dt))

        def sem(name):
            return ctx.enter_context(nc.semaphore(name))

        slots_d = nc.dram_tensor("slots_d", [P * NT, ROW], F32, kind="Internal").ap()
        xt_d = nc.dram_tensor("xt_d", [NPAD, XT], F32, kind="Internal").ap()
        tab_d = nc.dram_tensor("tab_d", [NPAD, TW], F32, kind="Internal").ap()

        ident = sb("ident", [P, P])
        below = sb("below", [P, P])
        ones = sb("ones", [P, P])
        iota_i = sb("iota_i", [P, P], I32)
        iota = sb("iota", [P, P])
        odd32 = sb("odd32", [P, 1])
        upper = sb("upper", [P, 1])
        half = sb("half", [P, 1])
        epsc = sb("epsc", [P, 1])

        W_sb = sb("W_sb", [P, 4, D])
        b_bc = sb("b_bc", [P, D])
        bnd_bc = sb("bnd_bc", [P, MUL])
        bo_bc = sb("bo_bc", [P, MUL])
        bpre = sb("bpre", [P, 1])
        bg1 = sb("bg1", [P, 2])
        bg2 = sb("bg2", [P, 2])
        wpre0 = sb("wpre0", [P, P])
        wpre1 = sb("wpre1", [P, P])
        wnd0 = sb("wnd0", [P, P])
        wnd1 = sb("wnd1", [P, P])
        wo0 = sb("wo0", [P, P])
        wo1 = sb("wo1", [P, P])
        wg1 = sb("wg1", [P, 2, 2 * P])
        wg2 = sb("wg2", [P, 2, 2 * P])
        ws1 = sb("ws1", [P, 3, HID])
        ws1ab = sb("ws1ab", [P, 4, HID])
        ws1c = sb("ws1c", [P, 4, HID])
        wf1 = sb("wf1", [HID, HID])
        wf1r = sb("wf1r", [HID, 4, HID])
        wstack = sb("wstack", [P, 2, D], F32R)

        gblk = sb("gblk", [P, NG], I32)

        ring = sb("ring", [P, R * 2 * TW])
        er = ring[0:EP, 0:EC * ROW].rearrange("p (c w) -> p c w", w=ROW)
        xg = ring[:, 0:R * 2 * XT].rearrange("p (r k w) -> p r k w", r=R, k=2)
        xj = ring[:, :].rearrange("p (r k w) -> p r k w", r=R, k=2)
        ed = sb("ed", [P, R, 2, ROW])

        xt = sb("xt", [P, NB, XT])
        s_bc = sb("s_bc", [P, NB, P])
        acc = sb("acc", [P, NB, D + 1])
        x1 = sb("x1", [P, NB, D])
        selfx = xt[:, :, 0:D]
        p1h = sb("p1h", [P, NB, 3 * MUL], F32R)
        p1l = sb("p1l", [P, NB, 3 * MUL], F32R)
        P0 = sb("P0", [P, NB, P])

        sorting = ExitStack()
        a_bc = sb("a_bc", [P, 2, D], scope=sorting)
        wfull = sb("wfull", [P, 2, D], scope=sorting)
        whi = sb("whi", [P, 2, D], F32R, scope=sorting)
        si = sb("si", [EP, 2, EC], I32, scope=sorting)
        blk_i = sb("blk_i", [EP, EC], I32, scope=sorting)
        loc_i = sb("loc_i", [EP, EC], I32, scope=sorting)
        blk = sb("blk", [EP, EC], scope=sorting)
        oh10 = sb("oh10", [EP, NB, EC], scope=sorting)
        inc = sb("inc", [EP, NB, EC], scope=sorting)
        prev = sb("prev", [EP, NB], scope=sorting)
        rowtot = sb("rowtot", [EP, NB], scope=sorting)
        ones10 = sb("ones10", [P, NB], scope=sorting)
        ngf = sb("ngf", [P, NB], scope=sorting)
        ngi = sb("ngi", [P, NB], I32, scope=sorting)
        ngincl = sb("ngincl", [P, NB], scope=sorting)
        start = sb("start", [P, NB], scope=sorting)
        off = sb("off", [P, NB], scope=sorting)
        slot = sb("slot", [EP, EC], scope=sorting)
        slot_i = sb("slot_i", [EP, EC], I32, scope=sorting)
        slot_t = sb("slot_t", [EP, EC], I32, scope=sorting)
        slot_p = sb("slot_p", [EP, EC], I32, scope=sorting)
        rowpos = sb("rowpos", [EP, EC], I32, scope=sorting)
        cnt = sb("cnt", [P, NG], scope=sorting)
        fill = sb("fill", [P, 22, ROW], scope=sorting)
        stage = sb("stage", [EP, 2, NS, ROW], scope=sorting)
        stage_pos = sb("stage_pos", [EP, 2, NS], I32, scope=sorting)
        wa = sb("wa", [P, 4, 2], scope=sorting)
        wa_bc = sb("wa_bc", [P, 2, D], scope=sorting)
        junk = sb("junk", [P, D], scope=sorting)
        score = sb("score", [P, 2, NB], scope=sorting)
        score0 = sb("score0", [P, 2], scope=sorting)

        ps = ctx.enter_context(nc.psum_tensor("ps", [P, 8, 512], F32))

        consts = sem("consts")
        pool_c = sem("pool_c")
        in_e = sem("in_e")
        in_x = sem("in_x")
        in_w = sem("in_w")
        in_er = sem("in_er")
        fill_ready = sem("fill_ready")
        filled = sem("filled")
        wa_ready = sem("wa_ready")
        wabc_ready = sem("wabc_ready")
        score_ready = sem("score_ready")
        sbc_ready = sem("sbc_ready")
        rowtot_ready = sem("rowtot_ready")
        base_ready = sem("base_ready")
        xt_ready = sem("xt_ready")
        xt_out = sem("xt_out")
        vc = sem("vc")
        vn = [0]

        def link(eng, ins):
            vn[0] += 1
            ins.then_inc(vc, 1)
            eng.wait_ge(vc, vn[0])

        with nc.Block() as block:
            loads = [0]

            @block.sync
            def _(sp):
                sp.dma_start(si[:, 0, :], src.rearrange("(p c) -> p c", p=EP)).then_inc(in_e, 16)
                sp.dma_start(si[:, 1, :], dst.rearrange("(p c) -> p c", p=EP)).then_inc(in_e, 16)
                sp.wait_ge(consts, 1)
                sp.dma_start(xt[:, 0:NB - 1, 0:D], x[0:(NB - 1) * P, :].rearrange("(b p) n -> p b n", p=P)).then_inc(in_x, 16)
                sp.dma_start(xt[0:LASTN, NB - 1, 0:D], x[(NB - 1) * P:N, :]).then_inc(in_x, 16)
                sp.dma_start(er, edge_rows.rearrange("(p c) w -> p c w", p=EP)).then_inc(in_er, 16)
                sp.wait_ge(fill_ready, 1)
                sd = slots_d.rearrange("(p t) w -> p t w", p=P)
                for c in range(NT // 22):
                    sp.dma_start(sd[:, 22 * c:22 * c + 22, :], fill[:, :, :]).then_inc(filled, 16)
                sp.wait_ge(filled, 16 * (NT // 22))
                sp.wait_ge(xt_ready, 1)
                sp.dma_start(xt_d.rearrange("(b p) n -> p b n", p=P), xt[:, :, :]).then_inc(xt_out, 16)
                sp.wait_ge(xt_out, 16)

            @block.scalar
            def _(act):
                def load(dst_, src_):
                    loads[0] += 1
                    act.dma_start(dst_, src_).then_inc(in_w, 16)
                load(W_sb[:, :, :], W.rearrange("(c p) n -> p c n", p=P))
                load(a_bc[:, :, :].rearrange("p c n -> p (c n)"), a.rearrange("n o -> (o n)").partition_broadcast(P))
                load(b_bc[:, :], b.partition_broadcast(P))
                load(bnd_bc[:, :], b_nd0.partition_broadcast(P))
                load(bo_bc[:, :], b_o0.partition_broadcast(P))
                load(bpre[:, :], b_pre0.rearrange("(p o) -> p o", o=1))
                for c in range(2):
                    load(bg1[:, c:c + 1], b_g1[P * c:P * c + P].rearrange("(p o) -> p o", o=1))
                    load(bg2[:, c:c + 1], b_g2[P * c:P * c + P].rearrange("(p o) -> p o", o=1))
                for d_, s_ in ((wpre0, W_pre0), (wpre1, W_pre1), (wnd0, W_nd0), (wnd1, W_nd1), (wo0, W_o0), (wo1, W_o1), (wf1, W_f1)):
                    load(d_[:, :], s_)
                load(wg1[:, :, :], W_g1.rearrange("(c p) n -> p c n", p=P))
                load(wg2[:, :, :], W_g2.rearrange("(c p) n -> p c n", p=P))
                load(ws1[:, :, :], W_s1.rearrange("(c p) n -> p c n", p=P))
                for q in range(4):
                    load(wfull[32 * q:32 * q + 32, 0, :], W_s2)
                    load(wfull[32 * q:32 * q + 32, 1, :], W_f2)
                act.wait_ge(in_w, 16 * loads[0])
                act.wait_ge(wabc_ready, 1)
                act.activation(wa_bc[:, :, :], ps[:, 0:2, :], ACT.Copy).then_inc(wabc_ready, 1)
                act.wait_ge(sbc_ready, 1)
                act.activation(s_bc[:, :, :].rearrange("p b n -> p (b n)"),
                               ps[:, 2:5, :].rearrange("p b n -> p (b n)")[:, 0:NB * P], ACT.Copy).then_inc(sbc_ready, 1)

            NLOADS = 28

            @block.gpsimd
            def _(g):
                g.memset(xt[:, NB - 1, :], 0.0).then_inc(consts, 1)
                g.iota(iota_i[:, :], [[1, P]], base=0, channel_multiplier=0).then_inc(pool_c, 1)
                g.memset(ident[:, :], 0.0).then_inc(pool_c, 1)
                g.memset(ones[:, :], 1.0).then_inc(pool_c, 1)
                g.memset(fill[:, :, :], 0.0).then_inc(pool_c, 1)
                g.wait_ge(pool_c, 4)
                g.tensor_copy(iota[:, :], iota_i[:, :]).then_inc(pool_c, 1)
                g.affine_select(out=ident[:, :], in_=ident[:, :], compare_op=ALU.not_equal, fill=1.0, base=0,
                                pattern=[[-1, P]], channel_multiplier=1).then_inc(pool_c, 1)
                g.affine_select(out=below[:, :], in_=ones[:, :], compare_op=ALU.is_gt, fill=0.0, base=0,
                                pattern=[[1, P]], channel_multiplier=-1).then_inc(pool_c, 1)
                g.memset(fill[:, :, IL], -1.0).then_inc(fill_ready, 1)
                g.memset(odd32[:, :], 0.0).then_inc(pool_c, 1)
                g.memset(upper[:, :], 0.0).then_inc(pool_c, 1)
                g.memset(half[:, :], 0.5).then_inc(pool_c, 1)
                g.memset(epsc[:, :], EPS).then_inc(pool_c, 1)
                g.memset(ones10[:, :], 1.0).then_inc(pool_c, 1)
                g.memset(acc[:, :, :], 0.0).then_inc(pool_c, 1)
                g.wait_ge(pool_c, 13)
                g.affine_select(out=acc[:, NB - 1, D:D + 1], in_=acc[:, NB - 1, D:D + 1], compare_op=ALU.is_gt, fill=1.0,
                                base=LASTN, pattern=[[0, 1]], channel_multiplier=-1).then_inc(pool_c, 1)

            @block.vector
            def _(v):
                v.wait_ge(in_e, 32)
                link(v, v.tensor_scalar(blk_i[:, :], si[:, 0, :], 7, None, ALU.arith_shift_right))
                link(v, v.tensor_scalar(loc_i[:, :], si[:, 0, :], P - 1, None, ALU.bitwise_and))
                link(v, v.tensor_copy(blk[:, :], blk_i[:, :]))
                for q in range(NB):
                    ins = v.tensor_scalar(oh10[:, q, :], blk[:, :], float(q), None, ALU.is_equal)
                link(v, ins)
                v.wait_ge(pool_c, 14)
                v.memset(odd32[32:64, :], 1.0)
                v.memset(odd32[96:128, :], 1.0)
                link(v, v.memset(upper[64:128, :], 1.0))
                link(v, v.tensor_tensor_scan(inc[:, :, :].rearrange("p b c -> p (b c)"),
                                             ones[0:EP, 0:1].to_broadcast([EP, NB * EC]),
                                             oh10[:, :, :].rearrange("p b c -> p (b c)"), 0.0, ALU.mult, ALU.add))
                link(v, v.memset(prev[:, 0:1], 0.0))
                link(v, v.tensor_copy(prev[:, 1:NB], inc[:, 0:NB - 1, EC - 1]))
                link(v, v.tensor_tensor(rowtot[:, :], inc[:, :, EC - 1], prev[:, :], ALU.subtract))
                v.sem_inc(rowtot_ready, 1)
                v.wait_ge(base_ready, 1)
                link(v, v.tensor_scalar(ngi[:, :], ps[:, 5, 0:NB], float(GE - 1), None, ALU.add))
                link(v, v.tensor_scalar(ngi[:, :], ngi[:, :], 8, None, ALU.arith_shift_right))
                link(v, v.tensor_copy(ngf[:, :], ngi[:, :]))
                link(v, v.tensor_tensor_scan(ngincl[:, :], ones10[:, :], ngf[:, :], 0.0, ALU.mult, ALU.add))
                link(v, v.tensor_tensor(start[:, :], ngincl[:, :], ngf[:, :], ALU.subtract))
                link(v, v.tensor_scalar(off[:, :], start[:, :], float(GE), -1.0, ALU.mult, ALU.add))
                link(v, v.tensor_tensor(off[0:EP, :], off[0:EP, :], ps[0:EP, 6, 0:NB], ALU.add))
                link(v, v.tensor_tensor(off[0:EP, :], off[0:EP, :], prev[:, :], ALU.subtract))
                link(v, v.tensor_tensor(inc[:, :, :], inc[:, :, :], off[0:EP, :].unsqueeze(2).to_broadcast([EP, NB, EC]), ALU.add))
                link(v, v.tensor_tensor(inc[:, :, :], inc[:, :, :], oh10[:, :, :], ALU.mult))
                link(v, v.tensor_reduce(slot[:, :], inc[:, :, :].rearrange("p b c -> p c b"), AX.X, ALU.add))
                link(v, v.tensor_copy(slot_i[:, :], slot[:, :]))
                link(v, v.tensor_scalar(slot_t[:, :], slot_i[:, :], 7, None, ALU.arith_shift_right))
                link(v, v.tensor_scalar(slot_p[:, :], slot_i[:, :], P - 1, None, ALU.bitwise_and))
                link(v, v.scalar_tensor_tensor(rowpos[:, :], slot_p[:, :], float(NT), slot_t[:, :], ALU.mult, ALU.add))
                link(v, v.tensor_scalar(cnt[:, :], iota[:, 0:NG], start[:, 1:2], None, ALU.is_ge))
                for q in range(2, NB):
                    link(v, v.scalar_tensor_tensor(cnt[:, :], iota[:, 0:NG], start[:, q:q + 1], cnt[:, :], ALU.is_ge, ALU.add))
                link(v, v.tensor_copy(gblk[:, :], cnt[:, :]))
                v.wait_ge(in_er, 16)
                v.tensor_copy(er[:, :, IL], loc_i[:, :])
                link(v, v.tensor_copy(er[:, :, JD].bitcast(I32), si[:, 1, :]))
                v.wait_ge(in_w, 16 * NLOADS)
                for c in range(4):
                    for h in range(2):
                        link(v, v.scalar_tensor_tensor(junk[:, :], W_sb[:, c, :], 1.0, a_bc[:, h, :], ALU.mult, ALU.mult,
                                                       accum_out=wa[:, c, h:h + 1]))
                for h in range(2):
                    link(v, v.scalar_tensor_tensor(junk[:, :], b_bc[:, :], 1.0, a_bc[:, h, :], ALU.mult, ALU.mult,
                                                   accum_out=score0[:, h:h + 1]))
                v.sem_inc(wa_ready, 1)
                v.wait_ge(wabc_ready, 2)
                v.wait_ge(in_x, 32)
                for q in range(NB):
                    for h in range(2):
                        link(v, v.scalar_tensor_tensor(junk[:, :], xt[:, q, 0:D], 1.0, wa_bc[:, h, :], ALU.mult, ALU.mult,
                                                       accum_out=score[:, h, q:q + 1]))
                for h in range(2):
                    link(v, v.tensor_scalar(score[:, h, :], score[:, h, :], score0[:, h:h + 1], None, ALU.add))
                v.sem_inc(score_ready, 1)
                v.tensor_copy(xt[:, :, TC], score[:, 1, :])
                link(v, v.memset(xt[:, :, ONE], 1.0))
                v.sem_inc(xt_ready, 1)
                link(v, v.tensor_tensor(ws1ab[:, 0, :], ws1[:, 0, :], ws1[:, 1, :], ALU.add))
                for q in range(1, 4):
                    v.tensor_copy(ws1ab[:, q, :], ws1ab[:, 0, :])
                for q in range(4):
                    v.tensor_scalar(ws1c[:, q, :], ws1[:, 2, :], 1.0 / 3.0, None, ALU.mult)
                    v.tensor_copy(wf1r[:, q, :], wf1[:, :])
                link(v, v.tensor_copy(whi[:, :, :], wfull[:, :, :]))
                for q in range(2):
                    link(v, v.scalar_tensor_tensor(junk[:, :], whi[:, q, :].bitcast(F32), upper[:, 0:1], wfull[:, q, :], ALU.mult, ALU.subtract))
                    link(v, v.tensor_scalar(wstack[:, q, :].rearrange("p (a b n) -> p a b n", a=2, b=2),
                                            junk[:, :].rearrange("p (b a n) -> p a b n", a=2, b=2), -1.0, None, ALU.mult))

            @block.tensor
            def _(pe):
                pe.wait_ge(pool_c, 14)
                pe.wait_ge(rowtot_ready, 1)
                pe.matmul(ps[:, 5, 0:NB], ones[0:EP, :], rowtot[:, :], start=True, stop=True)
                pe.matmul(ps[0:EP, 6, 0:NB], below[0:EP, 0:EP], rowtot[:, :], start=True, stop=True).then_inc(base_ready, 1)
                pe.wait_ge(wa_ready, 1)
                for h in range(2):
                    for c in range(4):
                        mm = pe.matmul(ps[:, h, P * c:P * c + P], wa[:, c, h:h + 1].to_broadcast([P, P]), ident[:, :],
                                       start=True, stop=True)
                mm.then_inc(wabc_ready, 1)
                pe.wait_ge(score_ready, 1)
                for q in range(NB):
                    mm = pe.matmul(ps[:, 2 + q // 4, P * (q % 4):P * (q % 4) + P],
                                   score[:, 0, q:q + 1].to_broadcast([P, P]), ident[:, :], start=True, stop=True)
                mm.then_inc(sbc_ready, 1)
            assert loads[0] == NLOADS, loads[0]

        staged = sem("staged")
        issue = sem("issue")
        scattered = [sem("scattered0"), sem("scattered1")]
        with nc.Block() as block:
            @block.vector
            def _(v):
                def batch(c, h, guard):
                    if guard is not None:
                        v.wait_ge(scattered[h], guard)
                    v.tensor_scalar(stage[:, h, :, :].bitcast(I32), er[:, bass.ds(c, NS), :].bitcast(I32), 0, None, ALU.bitwise_or)
                    v.tensor_copy(stage_pos[:, h, :], rowpos[:, bass.ds(c, NS)]).then_inc(staged, 1)
                batch(0, 0, None)
                batch(NS, 1, None)
                with v.Fori(1, EC // (2 * NS)) as i:
                    for h in range(2):
                        batch(i * (2 * NS) + h * NS, h, i * (16 * NS))

            @block.gpsimd
            def _(g):
                with g.Fori(0, EC // (2 * NS)) as i:
                    for h in range(2):
                        g.wait_ge(staged, i * 2 + (h + 1))
                        g.sem_inc(issue, 1)
                        for k in range(NS):
                            g.indirect_dma_start(slots_d[:, :], bass.IndirectOffsetOnAxis(ap=stage_pos[:, h, k:k + 1], axis=0),
                                                 stage[:, h, k, :], None).then_inc(scattered[h], 16)
                for h in range(2):
                    g.wait_ge(scattered[h], 16 * NS * (EC // (2 * NS)))

        sd2 = slots_d.rearrange("(p t) w -> p t w", p=P)

        sorting.close()
        sweep1 = ExitStack()
        junk2 = sb("junk2", [P, 2, P], scope=sweep1)
        sv = sb("sv", [P, R, 2], scope=sweep1)
        z = sb("z", [P, R, 2], scope=sweep1)
        zl = sb("zl", [P, R, 2], scope=sweep1)
        ev = sb("ev", [P, R, 2], scope=sweep1)
        aw = sb("aw", [P, R, 2, P], scope=sweep1)

        ed_in = [sem(f"ed_in{r}") for r in range(R)]
        xg_in = [sem(f"xg_in{r}") for r in range(R)]
        s_done = sem("s_done")
        z_done = sem("z_done")
        zl_done = sem("zl_done")
        e_done = sem("e_done")
        a_done = sem("a_done")
        row_done = sem("row_done")
        acc_done = sem("acc_done")
        issue1 = sem("issue1")

        def pipelined(eng, *stages):
            for i in range(2 * R):
                for lag, step in stages:
                    if i >= lag:
                        step(i - lag, (i - lag) % R, (i - lag) // R + 1)
            with eng.Fori(0, (NG - 2 * R) // R) as j:
                for c in range(R):
                    for lag, step in stages:
                        g0 = 2 * R + c - lag
                        step(j * R + g0, g0 % R, j + (g0 // R + 1))
            for i in range(NG, NG + max(lag for lag, _ in stages)):
                for lag, step in stages:
                    if i - lag < NG:
                        step(i - lag, (i - lag) % R, (i - lag) // R + 1)

        def first(g, m):
            return isinstance(g, int) and g < m

        with nc.Block() as block:
            @block.sync
            def _(sp):
                def load(g, r, n):
                    if not first(g, R):
                        sp.wait_ge(a_done, g - (R - 1))
                    sp.dma_start(ed[:, r, :, :], sd2[:, bass.ds(g * 2, 2), :]).then_inc(ed_in[r], 16)
                pipelined(sp, (0, load))

            @block.gpsimd
            def _(gp):
                def gather(g, r, n):
                    if not first(g, R):
                        gp.wait_ge(row_done, g - (R - 1))
                        gp.sem_inc(issue1, 1)
                    gp.wait_ge(ed_in[r], n * 16)
                    gp.sem_inc(issue1, 1)
                    for k in range(2):
                        gp.indirect_dma_start(xg[:, r, k, :], None, xt_d[:, :],
                                              bass.IndirectOffsetOnAxis(ap=ed[:, r, k, JD:JD + 1].bitcast(I32), axis=0))\
                          .then_inc(xg_in[r], 16)
                pipelined(gp, (0, gather))

            @block.vector
            def _(v):
                def early(g, r, n):
                    blk_r = v.value_load(gblk[0:1, bass.ds(g, 1)], min_val=0, max_val=NB - 1)
                    v.wait_ge(ed_in[r], n * 16)
                    for k in range(2):
                        ins = v.scalar_tensor_tensor(junk2[:, k, :], iota[:, :], ed[:, r, k, IL:IL + 1],
                                                     s_bc[:, bass.ds(blk_r, 1), :].rearrange("p b n -> p (b n)"),
                                                     ALU.is_equal, ALU.mult, accum_out=sv[:, r, k:k + 1])
                    ins.then_inc(s_done, 1)
                    v.wait_ge(s_done, g + 1)
                    v.wait_ge(xg_in[r], n * 32)
                    v.tensor_tensor(z[:, r, :], sv[:, r, :], xg[:, r, :, TC], ALU.add).then_inc(z_done, 1)
                    v.wait_ge(z_done, g + 1)
                    v.scalar_tensor_tensor(zl[:, r, :], z[:, r, :], SLOPE, z[:, r, :], ALU.mult, ALU.max).then_inc(zl_done, 1)

                def late(g, r, n):
                    v.wait_ge(e_done, g + 1)
                    for k in range(2):
                        ins = v.tensor_scalar(aw[:, r, k, :], iota[:, :], ed[:, r, k, IL:IL + 1], ev[:, r, k:k + 1],
                                              ALU.is_equal, ALU.mult)
                    ins.then_inc(a_done, 1)

                def later(g, r, n):
                    blk_r = v.value_load(gblk[0:1, bass.ds(g, 1)], min_val=0, max_val=NB - 1)
                    v.wait_ge(row_done, g + 1)
                    u = r % 2
                    if not first(g, 1):
                        v.wait_ge(acc_done, g)
                    dst_ = acc[:, bass.ds(blk_r, 1), :].rearrange("p b n -> p (b n)")
                    v.tensor_tensor(dst_, dst_, ps[:, 2 * u:2 * u + 2, :].rearrange("p b n -> p (b n)")[:, 0:D + 1],
                                    ALU.add).then_inc(acc_done, 1)

                pipelined(v, (0, early), (1, late), (2, later))

            @block.scalar
            def _(act):
                def body(g, r, n):
                    act.wait_ge(zl_done, g + 1)
                    act.activation(ev[:, r, :], zl[:, r, :], ACT.Exp).then_inc(e_done, 1)
                pipelined(act, (0, body))

            @block.tensor
            def _(pe):
                def body(g, r, n):
                    u = r % 2
                    pe.wait_ge(a_done, g + 1)
                    if not first(g, 2):
                        pe.wait_ge(acc_done, g - 1)
                    for k in range(2):
                        pe.matmul(ps[:, 2 * u, :], aw[:, r, k, :], xg[:, r, k, 0:D], start=(k == 0), stop=(k == 1))
                        mm = pe.matmul(ps[:, 2 * u + 1, 0:1], aw[:, r, k, :], xg[:, r, k, ONE:ONE + 1],
                                       start=(k == 0), stop=(k == 1))
                    mm.then_inc(row_done, 1)
                pipelined(pe, (0, body))

        sweep1.close()
        nodes = ExitStack()
        rcp = sb("rcp", [P, 2], scope=nodes)
        ya = sb("ya", [P, 2, D], scope=nodes)
        yT = sb("yT", [P, 2, D], scope=nodes)
        hb = sb("hb", [P, 2, D], scope=nodes)
        stats = sb("stats", [P, 2, 6], scope=nodes)
        mv = sb("mv", [P, 2, 2], scope=nodes)
        sd_ = sb("sd_", [P, 2], scope=nodes)
        rstd = sb("rstd", [P, 2], scope=nodes)
        x1c = sb("x1c", [P, 2, D], scope=nodes)
        xT = sb("xT", [P, 4, GE], scope=nodes)
        sq = sb("sq", [P, 3, GE], scope=nodes)
        n1T = sb("n1T", [P, GE], scope=nodes)
        p0T = sb("p0T", [P, GE], scope=nodes)
        uT = sb("uT", [P, 2, GE], scope=nodes)
        eT = sb("eT", [P, 2, GE], scope=nodes)
        hT = sb("hT", [P, 2, GE], scope=nodes)
        gT = sb("gT", [P, 2, GE], scope=nodes)
        xgT = sb("xgT", [P, 3, GE], scope=nodes)
        tabrow = sb("tabrow", [P, 2, TW], scope=nodes)
        issue3 = sem("issue3")
        q_v = sem("q_v")
        q_a = sem("q_a")
        q_p = sem("q_p")
        tab_out = sem("tab_out")
        VN, AN, PN = 20, 9, 8

        def pair_psum(k0, n):
            return ps[:, k0:k0 + n, :]

        with nc.Block() as block:
            @block.vector
            def _(v):
                link(v, v.tensor_tensor(xt[:, :, 0:D], xt[:, :, 0:D], b_bc[:, :].unsqueeze(1).to_broadcast([P, NB, D]), ALU.add))
                with v.Fori(0, NB // 2) as q:
                    vb = q * VN
                    step = [0]

                    def done(ins):
                        step[0] += 1
                        ins.then_inc(q_v, 1)

                    def own():
                        v.wait_ge(q_v, vb + step[0])
                    two = bass.ds(q * 2, 2)
                    done(v.tensor_scalar(rcp[:, :], acc[:, two, D], 1.0, None, ALU.mult))
                    own()
                    done(v.reciprocal(rcp[:, :], rcp[:, :]))
                    own()
                    v.tensor_scalar(ya[:, 0, :], acc[:, bass.ds(q * 2, 1), 0:D].rearrange("p b n -> p (b n)"), rcp[:, 0:1], None, ALU.mult)
                    done(v.tensor_scalar(ya[:, 1, :], acc[:, bass.ds(q * 2 + 1, 1), 0:D].rearrange("p b n -> p (b n)"), rcp[:, 1:2], None, ALU.mult))
                    v.wait_ge(q_p, q * PN + 2)
                    done(v.tensor_tensor(hb[:, :, :], xt[:, two, 0:D], pair_psum(2, 2), ALU.add))
                    own()
                    for k in range(2):
                        ins = v.bn_stats(stats[:, k, :], hb[:, k, :])
                    done(ins)
                    own()
                    v.sem_inc(issue3, 1)
                    for k in range(2):
                        ins = v.bn_aggr(mv[:, k, :], stats[:, k, :])
                    done(ins)
                    v.wait_ge(q_a, q * AN + 2)
                    done(v.reciprocal(rstd[:, :], sd_[:, :]))
                    own()
                    for k in range(2):
                        ins = v.tensor_scalar(x1c[:, k, :], hb[:, k, :], mv[:, k, 0:1], rstd[:, k:k + 1], ALU.subtract, ALU.mult)
                    done(ins)
                    own()
                    done(v.tensor_scalar(x1[:, two, :], x1c[:, :, :], 1.0, None, ALU.mult))
                    v.wait_ge(q_a, q * AN + 3)
                    done(v.tensor_tensor(sq[:, :, :], xT[:, 1:4, :], xT[:, 1:4, :], ALU.mult))
                    own()
                    done(v.tensor_tensor(sq[:, 0, :], sq[:, 0, :], sq[:, 1, :], ALU.add))
                    own()
                    done(v.tensor_tensor(sq[:, 0, :], sq[:, 0, :], sq[:, 2, :], ALU.add))
                    v.wait_ge(q_p, q * PN + 4)
                    for k in range(2):
                        v.tensor_copy(tabrow[:, k, D:TW], ps[:, 6 + k, 0:3 * MUL])
                    done(v.tensor_scalar(p1h[:, two, :], ps[:, 6:8, 0:3 * MUL], 1.0, None, ALU.mult))
                    own()
                    done(v.tensor_tensor(p1l[:, two, :], ps[:, 6:8, 0:3 * MUL], p1h[:, two, :].bitcast(F32), ALU.subtract))
                    v.wait_ge(q_a, q * AN + 7)
                    done(v.tensor_scalar(eT[:, :, :], eT[:, :, :], 1.0, None, ALU.add))
                    own()
                    done(v.reciprocal(eT[:, :, :], eT[:, :, :]))
                    own()
                    done(v.tensor_tensor(hT[:, :, :], uT[:, :, :], eT[:, :, :], ALU.mult))
                    v.wait_ge(q_a, q * AN + 9)
                    done(v.tensor_tensor(xgT[:, :, :], xT[:, 1:4, :], gT[:, 1, :].unsqueeze(1).to_broadcast([P, 3, GE]), ALU.mult))
                    v.wait_ge(q_p, q * PN + 8)
                    v.tensor_copy(tabrow[:, :, P:D], ps[:, 0:2, P:D])
                    done(v.tensor_tensor(tabrow[:, :, 0:P], ps[:, 0:2, 0:P], bnd_bc[:, :].unsqueeze(1).to_broadcast([P, 2, P]), ALU.add))
                    own()
                    done(v.tensor_scalar(selfx[:, two, :], tabrow[:, :, 0:D], 1.0, None, ALU.mult))
                    assert step[0] == VN, step[0]
                    v.wait_ge(tab_out, q * 16 + 16)

            @block.scalar
            def _(act):
                with act.Fori(0, NB // 2) as q:
                    step = [0]

                    def done(ins):
                        step[0] += 1
                        ins.then_inc(q_a, 1)
                    act.wait_ge(q_p, q * PN + 1)
                    done(act.activation(yT[:, :, :], pair_psum(0, 2), ACT.Copy))
                    act.wait_ge(q_v, q * VN + 6)
                    done(act.activation(sd_[:, :], mv[:, :, 1], ACT.Sqrt, bias=epsc[:, 0:1]))
                    act.wait_ge(q_p, q * PN + 3)
                    done(act.activation(xT[:, :, :], pair_psum(0, 2), ACT.Copy))
                    act.wait_ge(q_v, q * VN + 12)
                    done(act.activation(n1T[:, :], sq[:, 0, :], ACT.Sqrt, scale=1.0 / 3.0))
                    act.wait_ge(q_p, q * PN + 4)
                    done(act.activation(p0T[:, :], ps[:, 2, 0:GE], ACT.Identity, bias=bpre[:, 0:1]))
                    act.wait_ge(q_p, q * PN + 5)
                    for h in range(2):
                        ins = act.activation(uT[:, h, :], ps[:, 3, GE * h:GE * h + GE], ACT.Identity, bias=bg1[:, h:h + 1])
                    done(ins)
                    act.wait_ge(q_a, q * AN + 6)
                    done(act.activation(eT[:, :, :], uT[:, :, :], ACT.Exp, scale=-1.0))
                    act.wait_ge(q_p, q * PN + 6)
                    done(act.activation(P0[:, bass.ds(q * 2, 2), :], ps[:, 2, GE:512].rearrange("p (k n) -> p k n", k=2), ACT.Copy))
                    act.wait_ge(q_p, q * PN + 7)
                    for h in range(2):
                        ins = act.activation(gT[:, h, :], ps[:, 4, GE * h:GE * h + GE], ACT.Identity, bias=bg2[:, h:h + 1])
                    done(ins)
                    for _ in range(AN - step[0]):
                        act.sem_inc(q_a, 1)

            @block.tensor
            def _(pe):
                with pe.Fori(0, NB // 2) as q:
                    pe.wait_ge(q_v, q * VN + 3)
                    for k in range(2):
                        for c in range(4):
                            mm = pe.transpose(ps[:, k, P * c:P * c + P], ya[:, k, P * c:P * c + P], ident[:, :])
                    mm.then_inc(q_p, 1)
                    pe.wait_ge(q_a, q * AN + 1)
                    for k in range(2):
                        for c in range(4):
                            mm = pe.matmul(ps[:, 2 + k, :], yT[:, k, P * c:P * c + P], W_sb[:, c, :], start=(c == 0), stop=(c == 3))
                    mm.then_inc(q_p, 1)
                    pe.wait_ge(q_v, q * VN + 8)
                    for c in range(4):
                        for k in range(2):
                            s_ = x1c[:, k, 0:P] if c == 0 else x1c[:, k, P + c - 1:D:3]
                            mm = pe.transpose(ps[:, c // 2, GE * (c % 2) + P * k:GE * (c % 2) + P * k + P], s_, ident[:, :])
                    mm.then_inc(q_p, 1)
                    pe.wait_ge(q_a, q * AN + 3)
                    pe.matmul(ps[:, 2, 0:GE], wpre0[:, :], xT[:, 0, :], start=True, stop=True)
                    for k in range(2):
                        for c in range(3):
                            mm = pe.matmul(ps[:, 6 + k, P * c:P * c + P], xT[:, 1 + c, P * k:P * k + P], wpre1[:, :], start=True, stop=True)
                    mm.then_inc(q_p, 1)
                    pe.wait_ge(q_a, q * AN + 4)
                    for h in range(2):
                        pe.matmul(ps[:, 3, GE * h:GE * h + GE], wg1[:, 0, P * h:P * h + P], xT[:, 0, :], start=True, stop=False)
                        mm = pe.matmul(ps[:, 3, GE * h:GE * h + GE], wg1[:, 1, P * h:P * h + P], n1T[:, :], start=False, stop=True)
                    mm.then_inc(q_p, 1)
                    pe.wait_ge(q_a, q * AN + 5)
                    for k in range(2):
                        mm = pe.matmul(ps[:, 2, GE + P * k:GE + P * k + P], p0T[:, P * k:P * k + P],
                                       ws1ab[:, :, :].rearrange("p q h -> p (q h)"), start=True, stop=True)
                    mm.then_inc(q_p, 1)
                    pe.wait_ge(q_v, q * VN + 17)
                    for h in range(2):
                        for c in range(2):
                            mm = pe.matmul(ps[:, 4, GE * h:GE * h + GE], wg2[:, c, P * h:P * h + P], hT[:, c, :], start=(c == 0), stop=(c == 1))
                    mm.then_inc(q_p, 1)
                    pe.wait_ge(q_v, q * VN + 18)
                    for k in range(2):
                        pe.matmul(ps[:, k, 0:P], gT[:, 0, P * k:P * k + P], wnd0[:, :], start=True, stop=True)
                        for c in range(3):
                            mm = pe.matmul(ps[:, k, P * (c + 1):P * (c + 2)], xgT[:, c, P * k:P * k + P], wnd1[:, :], start=True, stop=True)
                    mm.then_inc(q_p, 1)

            @block.sync
            def _(sp):
                with sp.Fori(0, NB // 2) as q:
                    sp.wait_ge(q_v, q * VN + 19)
                    sp.dma_start(tab_d[bass.ds(q * GE, GE), :].rearrange("(k p) w -> p k w", p=P), tabrow[:, :, :]).then_inc(tab_out, 16)
                sp.wait_ge(tab_out, 16 * (NB // 2))

            @block.gpsimd
            def _(gp):
                gp.wait_ge(tab_out, 16 * (NB // 2))
                gp.memset(acc[:, :, :], 0.0)

        nodes.close()
        sweep2 = ExitStack()
        oh = sb("oh", [P, R, 2, P], scope=sweep2)
        shr = sb("shr", [P, R, 2, SH], scope=sweep2)
        ohT = sb("ohT", [P, 2, GE], F32R, scope=sweep2)
        eaT = sb("eaT", [HID, 2, GE], scope=sweep2)
        P0c = sb("P0c", [P, 2, P], scope=sweep2)
        prod = sb("prod", [P, 2, 3 * MUL], scope=sweep2)
        ipT = sb("ipT", [P, GE], scope=sweep2)
        lx = sb("lx", [P, 512], scope=sweep2)
        sp_ = sb("sp_", [P, 512], scope=sweep2)
        sph = sb("sph", [P, 512], F32R, scope=sweep2)
        hcomb = sb("hcomb", [P, 2, 512], F32R, scope=sweep2)
        S_sb = sb("S_sb", [P, 2, D], scope=sweep2)
        wv = sb("wv", [P, 2, D], scope=sweep2)
        t1 = sb("t1", [P, 2, P], scope=sweep2)
        dd = sb("dd", [P, 3, 2, P], scope=sweep2)
        bb = sb("bb", [P, 2, P], scope=sweep2)
        cc = sb("cc", [P, 2, 3 * P], scope=sweep2)
        msg = W_sb[:, :, :].rearrange("p (u k) n -> p u k n", u=2)

        ed2 = [sem(f"ed2_{r}") for r in range(R)]
        xj_in = [sem(f"xj_in{r}") for r in range(R)]
        issue2 = sem("issue2")
        oh_ready = sem("oh_ready")
        tr_ready = sem("tr_ready")
        ohT_ready = sem("ohT_ready")
        eaT_ready = sem("eaT_ready")
        pi_ready = sem("pi_ready")
        prod_ready = sem("prod_ready")
        ip_ready = sem("ip_ready")
        ipT_ready = sem("ipT_ready")
        hid_ready = sem("hid_ready")
        sp_done = sem("sp_done")
        p0c_ready = sem("p0c_ready")
        abs_done = sem("abs_done")
        exp_done = sem("exp_done")
        ln_done = sem("ln_done")
        sph_done = sem("sph_done")
        comb_ready = sem("comb_ready")
        s_ready = sem("s_ready")
        s_copied = sem("s_copied")
        f_ready = sem("f_ready")
        w_done = sem("w_done")
        c_done = sem("c_done")
        lv = sem("lv")
        msg_ready = sem("msg_ready")
        sum_ready = sem("sum_ready")
        acc2_done = sem("acc2_done")
        LV = 4
        psT, psH, psS, psF, psA = ps[:, 0, :], ps[:, 3, :], ps[:, 4, :], ps[:, 5:7, :], ps[:, 7, :]

        def after(eng, s_, count):
            if not (isinstance(count, int) and count <= 0):
                eng.wait_ge(s_, count)

        with nc.Block() as block:
            @block.sync
            def _(sp):
                def load(g, r, n):
                    if not first(g, R):
                        sp.wait_ge(prod_ready, g - (R - 1))
                    sp.dma_start(ed[:, r, :, :], sd2[:, bass.ds(g * 2, 2), :]).then_inc(ed2[r], 16)
                pipelined(sp, (0, load))

            @block.gpsimd
            def _(gp):
                def gather(g, r, n):
                    if not first(g, R):
                        gp.wait_ge(msg_ready, g - (R - 1))
                        gp.sem_inc(issue2, 1)
                    gp.wait_ge(ed2[r], n * 16)
                    gp.sem_inc(issue2, 1)
                    for k in range(2):
                        gp.indirect_dma_start(xj[:, r, k, :], None, tab_d[:, :],
                                              bass.IndirectOffsetOnAxis(ap=ed[:, r, k, JD:JD + 1].bitcast(I32), axis=0))\
                          .then_inc(xj_in[r], 16)

                def vectors(g, r, n):
                    gp.wait_ge(w_done, g + 1)
                    for k in range(2):
                        ins = gp.tensor_tensor(cc[:, k, :].rearrange("p (m n) -> p m n", m=3),
                                               xj[:, r, k, P:D].rearrange("p (m n) -> p m n", m=3),
                                               wv[:, k, P:2 * P].unsqueeze(1).to_broadcast([P, 3, P]), ALU.mult)
                    ins.then_inc(c_done, 1)
                pipelined(gp, (0, gather), (3, vectors))

            @block.tensor
            def _(pe):
                def turn_rows(g, r, n):
                    pe.wait_ge(oh_ready, g + 1)
                    after(pe, ipT_ready, g)
                    after(pe, eaT_ready, g)
                    for k in range(2):
                        pe.transpose(psT[:, P * k:P * k + P], oh[:, r, k, :], ident[:, :])
                    for k in range(2):
                        mm = pe.transpose(psT[0:EA, GE + P * k:GE + P * k + P], ed[:, r, k, 0:EA], ident[:, :])
                    mm.then_inc(tr_ready, 1)

                def sources(g, r, n):
                    u = r % 2
                    blk_r = pe.value_load(gblk[0:1, bass.ds(g, 1)], min_val=0, max_val=NB - 1)
                    pe.wait_ge(ohT_ready, g + 1)
                    after(pe, prod_ready, g)
                    for k in range(2):
                        for part, tab in enumerate((p1h, p1l)):
                            mm = pe.matmul(ps[:, 1 + k, 0:3 * MUL], ohT[:, u, P * k:P * k + P],
                                           tab[:, bass.ds(blk_r, 1), :].rearrange("p b n -> p (b n)"),
                                           start=(part == 0), stop=(part == 1))
                    mm.then_inc(pi_ready, 1)

                def inner(g, r, n):
                    pe.wait_ge(prod_ready, g + 1)
                    pe.wait_ge(eaT_ready, g + 1)
                    for k in range(2):
                        for c in range(3):
                            mm = pe.matmul(psT[:, P * k:P * k + P], prod[:, k, P * c:P * c + P], ident[:, :], is_transpose=True,
                                           start=(c == 0), stop=(c == 2))
                    mm.then_inc(ip_ready, 1)

                def hidden(g, r, n):
                    u = r % 2
                    pe.wait_ge(ipT_ready, g + 1)
                    pe.wait_ge(p0c_ready, g + 1)
                    after(pe, sp_done, g)
                    pe.matmul(psH[:, 0:GE], ws1c[:, :, :].rearrange("p q h -> p (q h)"), ipT[:, :], start=True, stop=False)
                    pe.matmul(psH[:, 0:GE], P0c[:, u, :], ohT[:, u, :].bitcast(F32), start=False, stop=True)
                    pe.matmul(psH[:, GE:512], wf1r[:, :, :].rearrange("p q h -> p (q h)"), eaT[:, u, :],
                              start=True, stop=True).then_inc(hid_ready, 1)

                def factors0(g, r, n):
                    u = r % 2
                    pe.wait_ge(comb_ready, g + 1)
                    after(pe, s_copied, g * 2)
                    pe.matmul(psS, hcomb[:, u, 0:P], wstack[:, 0, :], start=True, stop=True).then_inc(s_ready, 1)
                    after(pe, w_done, g)
                    for k in range(2):
                        mm = pe.matmul(psF[:, k, :], hcomb[:, u, GE + P * k:GE + P * k + P], wstack[:, 1, :], start=True, stop=True)
                    mm.then_inc(f_ready, 1)

                def factors1(g, r, n):
                    u = r % 2
                    pe.wait_ge(s_copied, g * 2 + 1)
                    pe.matmul(psS, hcomb[:, u, P:GE], wstack[:, 0, :], start=True, stop=True).then_inc(s_ready, 1)

                def sums(g, r, n):
                    u = r % 2
                    pe.wait_ge(msg_ready, g + 1)
                    after(pe, acc2_done, g)
                    for k in range(2):
                        mm = pe.matmul(psA, oh[:, r, k, :], msg[:, u, k, :], start=(k == 0), stop=(k == 1))
                    mm.then_inc(sum_ready, 1)
                pipelined(pe, (3, factors0), (1, inner), (3, factors1), (4, sums), (0, turn_rows), (1, hidden), (0, sources))

            @block.scalar
            def _(act):
                def factor_out(g, r, n):
                    for k in range(2):
                        act.wait_ge(s_ready, g * 2 + (k + 1))
                        if k == 0:
                            after(act, w_done, g)
                        act.activation(S_sb[:, k, 0:GE], psS[:, 0:GE], ACT.Copy, scale=shr[:, r, k, 0:1])
                        act.activation(S_sb[:, k, GE:512], psS[:, GE:512], ACT.Copy).then_inc(s_copied, 1)

                def inner_out(g, r, n):
                    act.wait_ge(ip_ready, g + 1)
                    after(act, hid_ready, g)
                    act.activation(ipT[:, :], psT[:, 0:GE], ACT.Copy).then_inc(ipT_ready, 1)

                def rows_out(g, r, n):
                    u = r % 2
                    act.wait_ge(tr_ready, g + 1)
                    after(act, hid_ready, g - 1)
                    act.activation(ohT[:, u, :], psT[:, 0:GE], ACT.Copy).then_inc(ohT_ready, 1)
                    act.activation(eaT[:, u, :], psT[0:EA, GE:512], ACT.Copy).then_inc(eaT_ready, 1)

                def node_part(g, r, n):
                    u = r % 2
                    blk_r = act.value_load(gblk[0:1, bass.ds(g, 1)], min_val=0, max_val=NB - 1)
                    act.activation(P0c[:, u, :], P0[:, bass.ds(blk_r, 1), :].rearrange("p b n -> p (b n)"), ACT.Copy).then_inc(p0c_ready, 1)

                def log_part(g, r, n):
                    act.wait_ge(hid_ready, g + 1)
                    after(act, sp_done, g)
                    act.activation(lx[:, :], psH, ACT.Abs).then_inc(abs_done, 1)
                    act.wait_ge(abs_done, g + 1)
                    act.activation(lx[:, :], lx[:, :], ACT.Exp, scale=-1.0).then_inc(exp_done, 1)
                    act.wait_ge(exp_done, g + 1)
                    act.activation(lx[:, :], lx[:, :], ACT.Ln, scale=0.5, bias=half[:, 0:1]).then_inc(ln_done, 1)

                def high_part(g, r, n):
                    act.wait_ge(sp_done, g + 1)
                    after(act, comb_ready, g)
                    act.activation(sph[:, :], sp_[:, :], ACT.Copy, scale=odd32[:, 0:1]).then_inc(sph_done, 1)
                act.preload_act_table_set("natural_log_exp_and_others")
                pipelined(act, (3, factor_out), (1, inner_out), (2, high_part), (0, node_part), (0, rows_out), (1, log_part))

            @block.vector
            def _(v):
                def sh(r, k, m):
                    return shr[:, r, k, m:m + 1]

                def one_hot(g, r, n):
                    v.wait_ge(ed2[r], n * 16)
                    after(v, sum_ready, g - (R - 1))
                    v.tensor_copy(shr[:, r, :, :], ed[:, r, :, EA:EA + SH])
                    for k in range(2):
                        ins = v.tensor_scalar(oh[:, r, k, :], iota[:, :], ed[:, r, k, IL:IL + 1], None, ALU.is_equal)
                    ins.then_inc(oh_ready, 1)

                def products(g, r, n):
                    v.wait_ge(xj_in[r], n * 32)
                    v.wait_ge(pi_ready, g + 1)
                    after(v, ip_ready, g)
                    v.tensor_tensor(prod[:, :, :], ps[:, 1:3, 0:3 * MUL], xj[:, r, :, D:TW], ALU.mult).then_inc(prod_ready, 1)

                def split(g, r, n):
                    u = r % 2
                    v.wait_ge(sph_done, g + 1)
                    after(v, f_ready, g - 1)
                    after(v, s_ready, g * 2 - 2)
                    v.tensor_tensor(hcomb[:, u, :], sp_[:, :], sph[:, :].bitcast(F32), ALU.subtract).then_inc(comb_ready, 1)

                def softplus(g, r, n):
                    v.wait_ge(ln_done, g + 1)
                    after(v, comb_ready, g)
                    v.scalar_tensor_tensor(sp_[:, :], psH, 0.0, lx[:, :], ALU.max, ALU.add).then_inc(sp_done, 1)

                def messages(g, r, n):
                    u = r % 2
                    v.wait_ge(f_ready, g + 1)
                    v.wait_ge(s_copied, g * 2 + 2)
                    after(v, c_done, g)
                    v.tensor_tensor(wv[:, :, :], S_sb[:, :, :], psF, ALU.mult).then_inc(w_done, 1)
                    after(v, sum_ready, g - 1)
                    after(v, msg_ready, g)
                    lb = g * LV
                    for k in range(2):
                        v.tensor_scalar(dd[:, 0, k, :], xj[:, r, k, P:2 * P], sh(r, k, 1), None, ALU.mult)
                    v.wait_ge(w_done, g + 1)
                    v.tensor_tensor(bb[:, :, :], wv[:, :, GE:3 * P], xj[:, r, :, 0:P], ALU.mult).then_inc(lv, 1)
                    v.tensor_tensor(t1[:, :, :], wv[:, :, 0:P], xj[:, r, :, 0:P], ALU.mult)
                    v.wait_ge(lv, lb + 1)
                    for k in range(2):
                        ins = v.scalar_tensor_tensor(dd[:, 1, k, :], xj[:, r, k, 2 * P:3 * P], sh(r, k, 2), dd[:, 0, k, :], ALU.mult, ALU.add)
                    ins.then_inc(lv, 1)
                    v.wait_ge(lv, lb + 2)
                    for k in range(2):
                        ins = v.scalar_tensor_tensor(dd[:, 2, k, :], xj[:, r, k, 3 * P:D], sh(r, k, 3), dd[:, 1, k, :], ALU.mult, ALU.add)
                    ins.then_inc(lv, 1)
                    v.wait_ge(lv, lb + 3)
                    v.scalar_tensor_tensor(dd[:, 0, :, :], dd[:, 2, :, :], 1.0 / 3.0 ** 0.5, wv[:, :, 3 * P:D], ALU.mult, ALU.mult).then_inc(lv, 1)
                    v.wait_ge(lv, lb + 4)
                    v.tensor_tensor(msg[:, u, :, 0:P], t1[:, :, :], dd[:, 0, :, :], ALU.add)
                    v.wait_ge(c_done, g + 1)
                    for m in range(3):
                        for k in range(2):
                            ins = v.scalar_tensor_tensor(msg[:, u, k, P * (m + 1):P * (m + 2)], bb[:, k, :], sh(r, k, m + 1),
                                                         cc[:, k, P * m:P * m + P], ALU.mult, ALU.add)
                    ins.then_inc(msg_ready, 1)

                def accumulate(g, r, n):
                    blk_r = v.value_load(gblk[0:1, bass.ds(g, 1)], min_val=0, max_val=NB - 1)
                    v.wait_ge(sum_ready, g + 1)
                    after(v, acc2_done, g)
                    dst_ = acc[:, bass.ds(blk_r, 1), 0:D].rearrange("p b n -> p (b n)")
                    v.tensor_tensor(dst_, dst_, psA, ALU.add).then_inc(acc2_done, 1)
                pipelined(v, (1, products), (0, one_hot), (2, split), (3, messages), (1, softplus), (4, accumulate))

        sweep2.close()
        ya = sb("ya2", [P, 2, D])
        yT = sb("yT2", [P, 2, D])
        hb = sb("hb2", [P, 2, D])
        stats = sb("stats2", [P, 2, 6])
        mv = sb("mv2", [P, 2, 2])
        sd_ = sb("sd2_", [P, 2])
        rstd = sb("rstd2", [P, 2])
        rcp = sb("rcp2", [P, 2])
        x1c = sb("x1c2", [P, 2, D])
        f_v = sem("f_v")
        f_a = sem("f_a")
        f_p = sem("f_p")
        out_done = sem("out_done")
        FV = 8
        with nc.Block() as block:
            @block.vector
            def _(v):
                with v.Fori(0, NB // 2) as q:
                    step = [0]
                    fb = q * FV

                    def done(ins):
                        step[0] += 1
                        ins.then_inc(f_v, 1)

                    def own():
                        v.wait_ge(f_v, fb + step[0])
                    two = bass.ds(q * 2, 2)
                    done(v.tensor_tensor(ya[:, :, :], acc[:, two, 0:D], selfx[:, two, :], ALU.add))
                    v.scalar_tensor_tensor(hb[:, :, 0:P], x1[:, two, 0:P], 2.0, bo_bc[:, :].unsqueeze(1).to_broadcast([P, 2, P]),
                                           ALU.mult, ALU.add)
                    done(v.tensor_scalar(hb[:, :, P:D], x1[:, two, P:D], 2.0, None, ALU.mult))
                    own()
                    v.wait_ge(f_p, q * 2 + 2)
                    v.tensor_tensor(hb[:, :, 0:P], hb[:, :, 0:P], ps[:, 2:4, 0:P], ALU.add)
                    for k in range(2):
                        ins = v.tensor_tensor(hb[:, k, P:D].rearrange("p (n m) -> p n m", m=3),
                                              hb[:, k, P:D].rearrange("p (n m) -> p n m", m=3),
                                              ps[:, 2 + k, P:D].rearrange("p (m n) -> p n m", m=3), ALU.add)
                    done(ins)
                    own()
                    for k in range(2):
                        ins = v.bn_stats(stats[:, k, :], hb[:, k, :])
                    done(ins)
                    own()
                    v.sem_inc(issue3, 1)
                    for k in range(2):
                        ins = v.bn_aggr(mv[:, k, :], stats[:, k, :])
                    done(ins)
                    v.wait_ge(f_a, q * 2 + 2)
                    done(v.reciprocal(rstd[:, :], sd_[:, :]))
                    own()
                    for k in range(2):
                        ins = v.tensor_scalar(x1c[:, k, :], hb[:, k, :], mv[:, k, 0:1], rstd[:, k:k + 1], ALU.subtract, ALU.mult)
                    done(ins)
                    v.wait_ge(out_done, q * 16 + 16)
                    done(v.tensor_copy(rcp[:, :], rstd[:, :]))
                    assert step[0] == FV

            @block.scalar
            def _(act):
                with act.Fori(0, NB // 2) as q:
                    act.wait_ge(f_p, q * 2 + 1)
                    act.activation(yT[:, :, :], pair_psum(0, 2), ACT.Copy).then_inc(f_a, 1)
                    act.wait_ge(f_v, q * FV + 5)
                    act.activation(sd_[:, :], mv[:, :, 1], ACT.Sqrt, bias=epsc[:, 0:1]).then_inc(f_a, 1)

            @block.tensor
            def _(pe):
                with pe.Fori(0, NB // 2) as q:
                    pe.wait_ge(f_v, q * FV + 1)
                    for k in range(2):
                        for c in range(4):
                            mm = pe.transpose(ps[:, k, P * c:P * c + P], ya[:, k, P * c:P * c + P], ident[:, :])
                    mm.then_inc(f_p, 1)
                    pe.wait_ge(f_a, q * 2 + 1)
                    for k in range(2):
                        for c in range(4):
                            mm = pe.matmul(ps[:, 2 + k, P * c:P * c + P], yT[:, k, P * c:P * c + P],
                                           (wo1 if c else wo0)[:, :], start=True, stop=True)
                    mm.then_inc(f_p, 1)

            @block.sync
            def _(sp):
                with sp.Fori(0, NB // 2) as q:
                    sp.wait_ge(f_v, q * FV + 7)
                    sp.dma_start(out[bass.ds(q * GE, GE), :].rearrange("(k p) w -> p k w", p=P), x1c[:, :, :]).then_inc(out_done, 16)
                sp.wait_ge(out_done, 16 * (NB // 2))


def kernel(x, src, dst, edge_attr_32, edge_attr_4, L0_gnn_W, L0_gnn_b, L0_gnn_a, L1_gnn_W_pre0, L1_gnn_b_pre0,
           L1_gnn_W_pre1, L1_gnn_W_nd0, L1_gnn_b_nd0, L1_gnn_W_nd1, L1_gnn_W_g1, L1_gnn_b_g1, L1_gnn_W_g2,
           L1_gnn_b_g2, L1_gnn_W_f1, L1_gnn_W_f2, L1_gnn_W_s1, L1_gnn_W_s2, L1_gnn_W_o0, L1_gnn_b_o0, L1_gnn_W_o1):
    import concourse.bacc as bacc
    from concourse.bass_utils import run_bass_kernel_spmd as run
    nc = bacc.Bacc("TRN2", target_bir_lowering=False, num_devices=1)
    ea, es = np.asarray(edge_attr_32), np.asarray(edge_attr_4)
    edge_rows = np.concatenate([ea, es, np.zeros((E, ROW - EA - SH), ea.dtype)], axis=1)
    arrays = {"x": x, "src": src, "dst": dst, "edge_rows": edge_rows, "W": L0_gnn_W, "b": L0_gnn_b, "a": L0_gnn_a,
              "W_pre0": L1_gnn_W_pre0, "b_pre0": L1_gnn_b_pre0, "W_pre1": L1_gnn_W_pre1, "W_nd0": L1_gnn_W_nd0,
              "b_nd0": L1_gnn_b_nd0, "W_nd1": L1_gnn_W_nd1, "W_g1": L1_gnn_W_g1, "b_g1": L1_gnn_b_g1,
              "W_g2": L1_gnn_W_g2, "b_g2": L1_gnn_b_g2, "W_f1": L1_gnn_W_f1, "W_f2": L1_gnn_W_f2,
              "W_s1": L1_gnn_W_s1, "W_s2": L1_gnn_W_s2, "W_o0": L1_gnn_W_o0, "b_o0": L1_gnn_b_o0, "W_o1": L1_gnn_W_o1}
    arrays = {n: np.ascontiguousarray(v) for n, v in arrays.items()}
    args = [nc.dram_tensor(n, v.shape, mybir.dt.from_np(v.dtype), kind="ExternalInput").ap() for n, v in arrays.items()]
    o = nc.dram_tensor("out", [NPAD, D], F32, kind="ExternalOutput").ap()
    build(nc, *args, o)
    r = run(nc, [arrays], core_ids=[0])
    return r.results[0]["out"][:N]
```

```python
import numpy as np
import concourse.bass as bass
from concourse import mybir
from contextlib import ExitStack

F32 = mybir.dt.float32
F32R = mybir.dt.float32r
I32 = mybir.dt.int32
ALU = mybir.AluOpType
ACT = mybir.ActivationFunctionType
AX = mybir.AxisListType

N, D, E = 1250, 512, 20000
MUL, HID, EA, SH = 128, 32, 32, 4
P = 128
NB = -(-N // P)
NPAD = NB * P
LASTN = N - (NB - 1) * P
EP = 125
EC = E // EP
GE = 2 * P
NG = (E + NB * (GE - 1)) // GE
NT = 2 * NG
ROW = EA + SH + 2
IL, JD = EA + SH, EA + SH + 1
XT = D + 2
TC, ONE = D, D + 1
TW = D + 3 * MUL
R = 4
U = 8
assert NG % U == 0 and U % R == 0

SLOPE = 0.1
EPS = 1e-5
NS = 16
assert NS * EA == 512 and EC % (2 * NS) == 0


def build(nc, x, src, dst, edge_rows, W, b, a, W_pre0, b_pre0, W_pre1, W_nd0, b_nd0, W_nd1, W_g1, b_g1,
          W_g2, b_g2, W_f1, W_f2, W_s1, W_s2, W_o0, b_o0, W_o1, out):
    ctx = ExitStack()
    with ctx:
        def sb(name, shape, dt=F32, scope=ctx):
            return scope.enter_context(nc.sbuf_tensor(name, shape, dt))

        def sem(name):
            return ctx.enter_context(nc.semaphore(name))

        def after(eng, s_, count):
            if not (isinstance(count, int) and count <= 0):
                eng.wait_ge(s_, count)

        slots_d = nc.dram_tensor("slots_d", [P * NT, ROW], F32, kind="Internal").ap()
        xt_d = nc.dram_tensor("xt_d", [NPAD, XT], F32, kind="Internal").ap()
        tab_d = nc.dram_tensor("tab_d", [NPAD, TW], F32, kind="Internal").ap()

        ident = sb("ident", [P, P])
        below = sb("below", [P, P])
        ones = sb("ones", [P, P])
        iota_i = sb("iota_i", [P, P], I32)
        iota = sb("iota", [P, P])
        odd32 = sb("odd32", [P, 1])
        upper = sb("upper", [P, 1])
        half = sb("half", [P, 1])
        epsc = sb("epsc", [P, 1])

        W_sb = sb("W_sb", [P, 4, D])
        b_bc = sb("b_bc", [P, D])
        bnd_bc = sb("bnd_bc", [P, MUL])
        bo_bc = sb("bo_bc", [P, MUL])
        bpre = sb("bpre", [P, 1])
        bg1 = sb("bg1", [P, 2])
        bg2 = sb("bg2", [P, 2])
        wpre0 = sb("wpre0", [P, P])
        wpre1 = sb("wpre1", [P, P])
        wnd0 = sb("wnd0", [P, P])
        wnd1 = sb("wnd1", [P, P])
        wo0 = sb("wo0", [P, P])
        wo1 = sb("wo1", [P, P])
        wg1 = sb("wg1", [P, 2, 2 * P])
        wg2 = sb("wg2", [P, 2, 2 * P])
        ws1 = sb("ws1", [P, 3, HID])
        ws1ab = sb("ws1ab", [P, 4, HID])
        ws1c = sb("ws1c", [P, 4, HID])
        wstack = sb("wstack", [P, 2, D], F32R)

        gblk = sb("gblk", [P, NG], I32)

        ring = sb("ring", [P, max(R * 2 * TW, U * 2 * XT)])
        er = ring[0:EP, 0:EC * ROW].rearrange("p (c w) -> p c w", w=ROW)
        xg = ring[:, 0:U * 2 * XT].rearrange("p (r k w) -> p r k w", r=U, k=2)
        xj = ring[:, 0:R * 2 * TW].rearrange("p (r k w) -> p r k w", r=R, k=2)
        ed = sb("ed", [P, U, 2, ROW])

        xt = sb("xt", [P, NB, D])
        s_bc = sb("s_bc", [P, NB, P])
        acc = sb("acc", [P, NB, D + 1])
        x1 = sb("x1", [P, NB, D])
        selfx = xt
        p1h = sb("p1h", [P, NB, 3 * MUL], F32R)
        p1l = sb("p1l", [P, NB, 3 * MUL], F32R)
        P0 = sb("P0", [P, NB, P])

        sorting = ExitStack()
        a_bc = sb("a_bc", [P, 2, D], scope=sorting)
        wfull = sb("wfull", [P, 2, D], scope=sorting)
        whi = sb("whi", [P, 2, D], F32R, scope=sorting)
        si = sb("si", [EP, 2, EC], I32, scope=sorting)
        blk_i = sb("blk_i", [EP, EC], I32, scope=sorting)
        loc_i = sb("loc_i", [EP, EC], I32, scope=sorting)
        blk = sb("blk", [EP, EC], scope=sorting)
        oh10 = sb("oh10", [EP, NB, EC], scope=sorting)
        inc = sb("inc", [EP, NB, EC], scope=sorting)
        prev = sb("prev", [EP, NB], scope=sorting)
        rowtot = sb("rowtot", [EP, NB], scope=sorting)
        ones10 = sb("ones10", [P, NB], scope=sorting)
        ngf = sb("ngf", [P, NB], scope=sorting)
        ngi = sb("ngi", [P, NB], I32, scope=sorting)
        ngincl = sb("ngincl", [P, NB], scope=sorting)
        start = sb("start", [P, NB], scope=sorting)
        off = sb("off", [P, NB], scope=sorting)
        slot = sb("slot", [EP, EC], scope=sorting)
        slot_i = sb("slot_i", [EP, EC], I32, scope=sorting)
        slot_t = sb("slot_t", [EP, EC], I32, scope=sorting)
        slot_p = sb("slot_p", [EP, EC], I32, scope=sorting)
        rowpos = sb("rowpos", [EP, EC], I32, scope=sorting)
        cnt = sb("cnt", [P, NG], scope=sorting)
        fill = sb("fill", [P, 22, ROW], scope=sorting)
        stage = sb("stage", [EP, 2, NS, ROW], scope=sorting)
        stage_pos = sb("stage_pos", [EP, 2, NS], I32, scope=sorting)
        wa = sb("wa", [P, 4, 2], scope=sorting)
        wa_bc = sb("wa_bc", [P, 2, D], scope=sorting)
        junk = sb("junk", [P, D], scope=sorting)
        score = sb("score", [P, 2, NB], scope=sorting)
        score0 = sb("score0", [P, 2], scope=sorting)
        wf_diag = x1[:, 0, 0:P]
        att = x1[0:EP, 1, :]
        attT = x1[:, 2, 0:4 * EP]
        lf = x1[0:EP, 3, :]
        xs = x1[:, 4, :]
        xsT = x1[:, 5, :]
        xrow = x1[:, 6:8, :].rearrange("p b n -> p (b n)")[:, 0:XT]

        ps = ctx.enter_context(nc.psum_tensor("ps", [P, 8, 512], F32))

        consts = sem("consts")
        pool_c = sem("pool_c")
        in_e = sem("in_e")
        in_x = sem("in_x")
        in_a = sem("in_a")
        in_w = sem("in_w")
        in_er = sem("in_er")
        in_f = sem("in_f")
        wf_cleared = sem("wf_cleared")
        fill_ready = sem("fill_ready")
        filled = sem("filled")
        wa_ready = sem("wa_ready")
        wabc_ready = sem("wabc_ready")
        score_ready = sem("score_ready")
        sbc_ready = sem("sbc_ready")
        rowtot_ready = sem("rowtot_ready")
        base_ready = sem("base_ready")
        xt_ready = sem("xt_ready")
        xt_out = sem("xt_out")
        vc = sem("vc")
        vn = [0]

        def link(eng, ins):
            vn[0] += 1
            ins.then_inc(vc, 1)
            eng.wait_ge(vc, vn[0])

        with nc.Block() as block:

            @block.sync
            def _(sp):
                sp.dma_start(si[:, 0, :], src.rearrange("(p c) -> p c", p=EP)).then_inc(in_e, 16)
                sp.dma_start(si[:, 1, :], dst.rearrange("(p c) -> p c", p=EP)).then_inc(in_e, 16)
                sp.dma_start(er, edge_rows.rearrange("(p c) w -> p c w", p=EP)).then_inc(in_er, 16)
                sp.wait_ge(fill_ready, 1)
                sd = slots_d.rearrange("(p t) w -> p t w", p=P)
                for c in range(NT // 22):
                    sp.dma_start(sd[:, 22 * c:22 * c + 22, :], fill[:, :, :]).then_inc(filled, 16)
                sp.wait_ge(consts, 1)
                sp.dma_start(xt[:, 0:NB - 1, :], x[0:(NB - 1) * P, :].rearrange("(b p) n -> p b n", p=P)).then_inc(in_x, 16)
                sp.dma_start(xt[0:LASTN, NB - 1, :], x[(NB - 1) * P:N, :]).then_inc(in_x, 16)
                sp.wait_ge(filled, 16 * (NT // 22))

            @block.scalar
            def _(act):
                act.dma_start(W_sb[:, :, :], W.rearrange("(c p) n -> p c n", p=P)).then_inc(in_a, 16)
                act.dma_start(a_bc[:, :, :].rearrange("p c n -> p (c n)"), a.rearrange("n o -> (o n)").partition_broadcast(P)).then_inc(in_a, 16)
                act.dma_start(b_bc[:, :], b.partition_broadcast(P)).then_inc(in_a, 16)
                act.wait_ge(wf_cleared, 1)
                for q in range(4):
                    act.dma_start(wf_diag[EA * q:EA * q + EA, HID * q:HID * q + HID], W_f1).then_inc(in_f, 16)
                act.preload_act_table_set("natural_log_exp_and_others")

            @block.gpsimd
            def _(g):
                g.memset(wf_diag, 0.0).then_inc(wf_cleared, 1)
                g.memset(xt[:, NB - 1, :], 0.0).then_inc(consts, 1)
                g.iota(iota_i[:, :], [[1, P]], base=0, channel_multiplier=0).then_inc(pool_c, 1)
                g.memset(ident[:, :], 0.0).then_inc(pool_c, 1)
                g.memset(ones[:, :], 1.0).then_inc(pool_c, 1)
                g.memset(fill[:, :, :], 0.0).then_inc(pool_c, 1)
                g.wait_ge(pool_c, 4)
                g.tensor_copy(iota[:, :], iota_i[:, :]).then_inc(pool_c, 1)
                g.affine_select(out=ident[:, :], in_=ident[:, :], compare_op=ALU.not_equal, fill=1.0, base=0,
                                pattern=[[-1, P]], channel_multiplier=1).then_inc(pool_c, 1)
                g.affine_select(out=below[:, :], in_=ones[:, :], compare_op=ALU.is_gt, fill=0.0, base=0,
                                pattern=[[1, P]], channel_multiplier=-1).then_inc(pool_c, 1)
                g.memset(fill[:, :, IL], -1.0).then_inc(fill_ready, 1)
                g.memset(odd32[:, :], 0.0).then_inc(pool_c, 1)
                g.memset(upper[:, :], 0.0).then_inc(pool_c, 1)
                g.memset(half[:, :], 0.5).then_inc(pool_c, 1)
                g.memset(epsc[:, :], EPS).then_inc(pool_c, 1)
                g.memset(ones10[:, :], 1.0).then_inc(pool_c, 1)
                g.memset(acc[:, :, :], 0.0).then_inc(pool_c, 1)
                g.wait_ge(pool_c, 13)
                g.affine_select(out=acc[:, NB - 1, D:D + 1], in_=acc[:, NB - 1, D:D + 1], compare_op=ALU.is_gt, fill=1.0,
                                base=LASTN, pattern=[[0, 1]], channel_multiplier=-1).then_inc(pool_c, 1)

            @block.vector
            def _(v):
                v.wait_ge(in_e, 32)
                link(v, v.tensor_scalar(blk_i[:, :], si[:, 0, :], 7, None, ALU.arith_shift_right))
                link(v, v.tensor_scalar(loc_i[:, :], si[:, 0, :], P - 1, None, ALU.bitwise_and))
                link(v, v.tensor_copy(blk[:, :], blk_i[:, :]))
                for q in range(NB):
                    ins = v.tensor_scalar(oh10[:, q, :], blk[:, :], float(q), None, ALU.is_equal)
                link(v, ins)
                v.wait_ge(pool_c, 14)
                v.memset(odd32[32:64, :], 1.0)
                v.memset(odd32[96:128, :], 1.0)
                link(v, v.memset(upper[64:128, :], 1.0))
                link(v, v.tensor_tensor_scan(inc[:, :, :].rearrange("p b c -> p (b c)"),
                                             ones[0:EP, 0:1].to_broadcast([EP, NB * EC]),
                                             oh10[:, :, :].rearrange("p b c -> p (b c)"), 0.0, ALU.mult, ALU.add))
                link(v, v.memset(prev[:, 0:1], 0.0))
                link(v, v.tensor_copy(prev[:, 1:NB], inc[:, 0:NB - 1, EC - 1]))
                link(v, v.tensor_tensor(rowtot[:, :], inc[:, :, EC - 1], prev[:, :], ALU.subtract))
                v.sem_inc(rowtot_ready, 1)
                v.wait_ge(base_ready, 1)
                link(v, v.tensor_scalar(ngi[:, :], ps[:, 5, 0:NB], float(GE - 1), None, ALU.add))
                link(v, v.tensor_scalar(ngi[:, :], ngi[:, :], 8, None, ALU.arith_shift_right))
                link(v, v.tensor_copy(ngf[:, :], ngi[:, :]))
                link(v, v.tensor_tensor_scan(ngincl[:, :], ones10[:, :], ngf[:, :], 0.0, ALU.mult, ALU.add))
                link(v, v.tensor_tensor(start[:, :], ngincl[:, :], ngf[:, :], ALU.subtract))
                link(v, v.tensor_scalar(off[:, :], start[:, :], float(GE), -1.0, ALU.mult, ALU.add))
                link(v, v.tensor_tensor(off[0:EP, :], off[0:EP, :], ps[0:EP, 6, 0:NB], ALU.add))
                link(v, v.tensor_tensor(off[0:EP, :], off[0:EP, :], prev[:, :], ALU.subtract))
                link(v, v.tensor_tensor(inc[:, :, :], inc[:, :, :], off[0:EP, :].unsqueeze(2).to_broadcast([EP, NB, EC]), ALU.add))
                link(v, v.tensor_tensor(inc[:, :, :], inc[:, :, :], oh10[:, :, :], ALU.mult))
                link(v, v.tensor_reduce(slot[:, :], inc[:, :, :].rearrange("p b c -> p c b"), AX.X, ALU.add))
                link(v, v.tensor_copy(slot_i[:, :], slot[:, :]))
                link(v, v.tensor_scalar(slot_t[:, :], slot_i[:, :], 7, None, ALU.arith_shift_right))
                link(v, v.tensor_scalar(slot_p[:, :], slot_i[:, :], P - 1, None, ALU.bitwise_and))
                link(v, v.scalar_tensor_tensor(rowpos[:, :], slot_p[:, :], float(NT), slot_t[:, :], ALU.mult, ALU.add))
                v.wait_ge(in_er, 16)
                v.tensor_copy(er[:, :, IL], loc_i[:, :])
                link(v, v.tensor_copy(er[:, :, JD].bitcast(I32), si[:, 1, :]))

            @block.tensor
            def _(pe):
                pe.wait_ge(pool_c, 14)
                pe.wait_ge(rowtot_ready, 1)
                pe.matmul(ps[:, 5, 0:NB], ones[0:EP, :], rowtot[:, :], start=True, stop=True)
                pe.matmul(ps[0:EP, 6, 0:NB], below[0:EP, 0:EP], rowtot[:, :], start=True, stop=True).then_inc(base_ready, 1)

        staged = sem("staged")
        issue = sem("issue")
        scattered = [sem("scattered0"), sem("scattered1")]
        att_ready = sem("att_ready")
        att_turned = sem("att_turned")
        attT_ready = sem("attT_ready")
        hf_ready = sem("hf_ready")
        hf_abs = sem("hf_abs")
        hf_exp = sem("hf_exp")
        hf_ln = sem("hf_ln")
        hf_used = sem("hf_used")
        issue_a = sem("issue_a")
        xs_ready = sem("xs_ready")
        xs_turned = sem("xs_turned")
        xsT_ready = sem("xsT_ready")
        xw_ready = sem("xw_ready")

        NBATCH = EC // NS
        assert NBATCH == NB

        def batches(eng, step, attention, scores, embed):
            for b in range(2):
                step(b, b)
            attention()
            for b in range(2, 4):
                step(b, b - 2)
            scores()
            for b in range(4, 6):
                step(b, b - 4)
                embed(b - 4)
            with eng.Fori(3, NBATCH // 2) as i:
                for h in range(2):
                    step(i * 2 + h, h)
                    embed(i * 2 + (h - 4))
            for q in range(NB - 4, NB):
                embed(q)
        NLOADS = 24
        loads = [0]
        with nc.Block() as block:
            @block.vector
            def _(v):
                def rows(b, h):
                    cols = bass.ds(b * NS, NS)
                    after(v, scattered[h], (b - h) * (8 * NS))
                    v.tensor_scalar(stage[:, h, :, EA:ROW].bitcast(I32), er[:, cols, EA:ROW].bitcast(I32), 0, None, ALU.bitwise_or)
                    v.tensor_copy(stage_pos[:, h, :], rowpos[:, cols])
                    v.wait_ge(hf_ln, b + 1)
                    v.scalar_tensor_tensor(stage[:, h, :, 0:EA], ps[0:EP, 6, :].rearrange("p (c n) -> p c n", n=EA), 0.0,
                                           lf.rearrange("p (c n) -> p c n", n=EA), ALU.max, ALU.add).then_inc(hf_used, 1)
                    v.wait_ge(hf_used, b + 1)
                    v.sem_inc(staged, 1)

                def attention():
                    link(v, v.tensor_scalar(cnt[:, :], iota[:, 0:NG], start[:, 1:2], None, ALU.is_ge))
                    for q in range(2, NB):
                        link(v, v.scalar_tensor_tensor(cnt[:, :], iota[:, 0:NG], start[:, q:q + 1], cnt[:, :], ALU.is_ge, ALU.add))
                    link(v, v.tensor_copy(gblk[:, :], cnt[:, :]))
                    v.wait_ge(in_a, 48)
                    for c in range(4):
                        for h in range(2):
                            link(v, v.scalar_tensor_tensor(junk[:, :], W_sb[:, c, :], 1.0, a_bc[:, h, :], ALU.mult, ALU.mult,
                                                           accum_out=wa[:, c, h:h + 1]))
                    for h in range(2):
                        link(v, v.scalar_tensor_tensor(junk[:, :], b_bc[:, :], 1.0, a_bc[:, h, :], ALU.mult, ALU.mult,
                                                       accum_out=score0[:, h:h + 1]))
                    v.sem_inc(wa_ready, 1)

                def scores():
                    v.wait_ge(wabc_ready, 2)
                    v.wait_ge(in_x, 32)
                    for q in range(NB):
                        for h in range(2):
                            link(v, v.scalar_tensor_tensor(junk[:, :], xt[:, q, :], 1.0, wa_bc[:, h, :], ALU.mult, ALU.mult,
                                                           accum_out=score[:, h, q:q + 1]))
                    for h in range(2):
                        link(v, v.tensor_scalar(score[:, h, :], score[:, h, :], score0[:, h:h + 1], None, ALU.add))
                    v.sem_inc(score_ready, 1)
                    v.memset(xrow[:, ONE:ONE + 1], 1.0)
                    v.wait_ge(in_w, 16 * NLOADS)
                    link(v, v.tensor_tensor(ws1ab[:, 0, :], ws1[:, 0, :], ws1[:, 1, :], ALU.add))
                    for q in range(1, 4):
                        v.tensor_copy(ws1ab[:, q, :], ws1ab[:, 0, :])
                    for q in range(4):
                        v.tensor_scalar(ws1c[:, q, :], ws1[:, 2, :], 1.0 / 3.0, None, ALU.mult)
                    link(v, v.tensor_copy(whi[:, :, :], wfull[:, :, :]))
                    for q in range(2):
                        link(v, v.scalar_tensor_tensor(junk[:, :], whi[:, q, :].bitcast(F32), upper[:, 0:1], wfull[:, q, :], ALU.mult, ALU.subtract))
                        link(v, v.tensor_scalar(wstack[:, q, :].rearrange("p (a b n) -> p a b n", a=2, b=2),
                                                junk[:, :].rearrange("p (b a n) -> p a b n", a=2, b=2), -1.0, None, ALU.mult))

                def embed(q):
                    v.wait_ge(xw_ready, q + 1)
                    after(v, xt_out, q * 16)
                    v.tensor_tensor(xrow[:, 0:D], ps[:, 0, :], b_bc[:, :], ALU.add)
                    v.tensor_scalar(xrow[:, TC:TC + 1], score[:, 1, bass.ds(q, 1)], 1.0, None, ALU.mult).then_inc(xt_ready, 1)
                batches(v, rows, attention, scores, embed)

            @block.gpsimd
            def _(g):
                with g.Fori(0, EC // (2 * NS)) as i:
                    for h in range(2):
                        g.wait_ge(staged, i * 2 + (h + 1))
                        g.sem_inc(issue, 1)
                        for k in range(NS):
                            g.indirect_dma_start(slots_d[:, :], bass.IndirectOffsetOnAxis(ap=stage_pos[:, h, k:k + 1], axis=0),
                                                 stage[:, h, k, :], None).then_inc(scattered[h], 16)
                for h in range(2):
                    g.wait_ge(scattered[h], 16 * NS * (EC // (2 * NS)))

            @block.scalar
            def _(act):
                def hidden_f(b, h):
                    after(act, att_turned, b)
                    act.sem_inc(issue_a, 1)
                    act.activation(att.rearrange("p (c n) -> p c n", n=EA), er[:, bass.ds(b * NS, NS), 0:EA], ACT.Copy).then_inc(att_ready, 1)
                    act.wait_ge(att_turned, b + 1)
                    after(act, hf_ready, b)
                    act.activation(attT, ps[:, 5, 0:4 * EP], ACT.Copy).then_inc(attT_ready, 1)
                    act.wait_ge(hf_ready, b + 1)
                    after(act, hf_used, b)
                    act.activation(lf, ps[0:EP, 6, :], ACT.Abs).then_inc(hf_abs, 1)
                    act.wait_ge(hf_abs, b + 1)
                    act.activation(lf, lf, ACT.Exp, scale=-1.0).then_inc(hf_exp, 1)
                    act.wait_ge(hf_exp, b + 1)
                    act.activation(lf, lf, ACT.Ln, scale=0.5, bias=half[0:EP, 0:1]).then_inc(hf_ln, 1)

                def attention():
                    def load(dst_, src_):
                        loads[0] += 1
                        act.dma_start(dst_, src_).then_inc(in_w, 16)
                    load(bnd_bc[:, :], b_nd0.partition_broadcast(P))
                    load(bo_bc[:, :], b_o0.partition_broadcast(P))
                    load(bpre[:, :], b_pre0.rearrange("(p o) -> p o", o=1))
                    for c in range(2):
                        load(bg1[:, c:c + 1], b_g1[P * c:P * c + P].rearrange("(p o) -> p o", o=1))
                        load(bg2[:, c:c + 1], b_g2[P * c:P * c + P].rearrange("(p o) -> p o", o=1))
                    for d_, s_ in ((wpre0, W_pre0), (wpre1, W_pre1), (wnd0, W_nd0), (wnd1, W_nd1), (wo0, W_o0), (wo1, W_o1)):
                        load(d_[:, :], s_)
                    load(wg1[:, :, :], W_g1.rearrange("(c p) n -> p c n", p=P))
                    load(wg2[:, :, :], W_g2.rearrange("(c p) n -> p c n", p=P))
                    load(ws1[:, :, :], W_s1.rearrange("(c p) n -> p c n", p=P))
                    for q in range(4):
                        load(wfull[32 * q:32 * q + 32, 0, :], W_s2)
                        load(wfull[32 * q:32 * q + 32, 1, :], W_f2)
                    act.wait_ge(in_w, 16 * NLOADS)
                    act.wait_ge(wabc_ready, 1)
                    act.activation(wa_bc[:, :, :], ps[:, 0:2, :], ACT.Copy).then_inc(wabc_ready, 1)

                def scores():
                    act.wait_ge(sbc_ready, 1)
                    act.activation(s_bc[:, :, :].rearrange("p b n -> p (b n)"),
                                   ps[:, 2:5, :].rearrange("p b n -> p (b n)")[:, 0:NB * P], ACT.Copy).then_inc(sbc_ready, 1)

                def embed(q):
                    after(act, xs_turned, q)
                    act.sem_inc(issue_a, 1)
                    act.activation(xs, xt[:, bass.ds(q, 1), :].rearrange("p b n -> p (b n)"), ACT.Copy).then_inc(xs_ready, 1)
                    act.wait_ge(xs_turned, q + 1)
                    after(act, xw_ready, q)
                    act.activation(xsT, ps[:, 7, :], ACT.Copy).then_inc(xsT_ready, 1)
                batches(act, hidden_f, attention, scores, embed)

            @block.tensor
            def _(pe):
                pe.wait_ge(in_f, 64)

                def hidden_f(b, h):
                    pe.wait_ge(att_ready, b + 1)
                    after(pe, attT_ready, b)
                    for q in range(4):
                        mm = pe.transpose(ps[:, 5, EP * q:EP * q + EP], att[:, P * q:P * q + P], ident[0:EP, 0:EP])
                    mm.then_inc(att_turned, 1)
                    pe.wait_ge(attT_ready, b + 1)
                    after(pe, hf_used, b)
                    for q in range(4):
                        mm = pe.matmul(ps[0:EP, 6, P * q:P * q + P], attT[:, EP * q:EP * q + EP], wf_diag, start=True, stop=True)
                    mm.then_inc(hf_ready, 1)

                def attention():
                    pe.wait_ge(wa_ready, 1)
                    for h in range(2):
                        for c in range(4):
                            mm = pe.matmul(ps[:, h, P * c:P * c + P], wa[:, c, h:h + 1].to_broadcast([P, P]), ident[:, :],
                                           start=True, stop=True)
                    mm.then_inc(wabc_ready, 1)

                def scores():
                    pe.wait_ge(score_ready, 1)
                    for q in range(NB):
                        mm = pe.matmul(ps[:, 2 + q // 4, P * (q % 4):P * (q % 4) + P],
                                       score[:, 0, q:q + 1].to_broadcast([P, P]), ident[:, :], start=True, stop=True)
                    mm.then_inc(sbc_ready, 1)

                def embed(q):
                    pe.wait_ge(xs_ready, q + 1)
                    after(pe, xsT_ready, q)
                    for c in range(4):
                        mm = pe.transpose(ps[:, 7, P * c:P * c + P], xs[:, P * c:P * c + P], ident[:, :])
                    mm.then_inc(xs_turned, 1)
                    pe.wait_ge(xsT_ready, q + 1)
                    pe.wait_ge(wabc_ready, 2)
                    after(pe, xt_ready, q)
                    for c in range(4):
                        mm = pe.matmul(ps[:, 0, :], xsT[:, P * c:P * c + P], W_sb[:, c, :], start=(c == 0), stop=(c == 3))
                    mm.then_inc(xw_ready, 1)
                batches(pe, hidden_f, attention, scores, embed)

            @block.sync
            def _(sp):
                with sp.Fori(0, NB) as q:
                    sp.wait_ge(xt_ready, q + 1)
                    sp.dma_start(xt_d[bass.ds(q * P, P), :], xrow).then_inc(xt_out, 16)
                sp.wait_ge(xt_out, 16 * NB)

            assert loads[0] == NLOADS, loads[0]

        sd2 = slots_d.rearrange("(p t) w -> p t w", p=P)

        sorting.close()
        sweep1 = ExitStack()
        junk2 = sb("junk2", [P, 2, P], scope=sweep1)
        srow = sb("srow", [P, R, P], scope=sweep1)
        sv = sb("sv", [P, R, 2], scope=sweep1)
        z = sb("z", [P, R, 2], scope=sweep1)
        zl = sb("zl", [P, R, 2], scope=sweep1)
        ev = sb("ev", [P, R, 2], scope=sweep1)
        aw = sb("aw", [P, R, 2, P], scope=sweep1)

        ed_in = [sem(f"ed_in{c}") for c in range(U)]
        xg_in = [sem(f"xg_in{c}") for c in range(U)]
        srow_ready = sem("srow_ready")
        s_done = sem("s_done")
        z_done = sem("z_done")
        zl_done = sem("zl_done")
        e_done = sem("e_done")
        a_done = sem("a_done")
        row_done = sem("row_done")
        acc_done = sem("acc_done")
        issue1 = sem("issue1")

        def pipelined(eng, *stages, count=NG, turn=U, ring=R):
            last = max(lag for lag, _ in stages)
            peel = turn * max(-(-last // turn), 1)
            for i in range(peel):
                for lag, step in stages:
                    if i >= lag:
                        step(i - lag, (i - lag) % turn, (i - lag) // ring + 1)
            with eng.Fori(0, (count - peel) // turn) as j:
                for i in range(turn):
                    for lag, step in stages:
                        g0 = peel + i - lag
                        step(j * turn + g0, g0 % turn, j * (turn // ring) + (g0 // ring + 1))
            for i in range(count, count + last):
                for lag, step in stages:
                    if i - lag < count:
                        step(i - lag, (i - lag) % turn, (i - lag) // ring + 1)

        def pairs(eng, *stages):
            pipelined(eng, *((lag, lambda q, c, n, step=step: step(q)) for lag, step in stages), count=NB // 2, turn=1, ring=1)

        def first(g, m):
            return isinstance(g, int) and g < m

        with nc.Block() as block:
            @block.sync
            def _(sp):
                def load(g, c, n):
                    if not first(g, U):
                        sp.wait_ge(a_done, g - (U - 1))
                    sp.dma_start(ed[:, c, :, :], sd2[:, bass.ds(g * 2, 2), :]).then_inc(ed_in[c], 16)
                pipelined(sp, (0, load), ring=U)

            @block.gpsimd
            def _(gp):
                def gather(g, c, n):
                    if not first(g, U):
                        gp.wait_ge(row_done, g - (U - 1))
                        gp.sem_inc(issue1, 1)
                    gp.wait_ge(ed_in[c], n * 16)
                    gp.sem_inc(issue1, 1)
                    for k in range(2):
                        gp.indirect_dma_start(xg[:, c, k, :], None, xt_d[:, :],
                                              bass.IndirectOffsetOnAxis(ap=ed[:, c, k, JD:JD + 1].bitcast(I32), axis=0))\
                          .then_inc(xg_in[c], 16)
                pipelined(gp, (0, gather), ring=U)

            @block.vector
            def _(v):
                def source_scores(g, c, n):
                    r = c % R
                    v.wait_ge(ed_in[c], n * 16)
                    v.wait_ge(srow_ready, g + 1)
                    for k in range(2):
                        ins = v.scalar_tensor_tensor(junk2[:, k, :], iota[:, :], ed[:, c, k, IL:IL + 1], srow[:, r, :],
                                                     ALU.is_equal, ALU.mult, accum_out=sv[:, r, k:k + 1])
                    ins.then_inc(s_done, 1)

                def add_target(g, c, n):
                    r = c % R
                    v.wait_ge(s_done, g + 1)
                    v.wait_ge(xg_in[c], n * 32)
                    v.tensor_tensor(z[:, r, :], sv[:, r, :], xg[:, c, :, TC], ALU.add).then_inc(z_done, 1)

                def leaky(g, c, n):
                    r = c % R
                    v.wait_ge(z_done, g + 1)
                    v.scalar_tensor_tensor(zl[:, r, :], z[:, r, :], SLOPE, z[:, r, :], ALU.mult, ALU.max).then_inc(zl_done, 1)

                def weighted_rows(g, c, n):
                    r = c % R
                    v.wait_ge(e_done, g + 1)
                    for k in range(2):
                        ins = v.tensor_scalar(aw[:, r, k, :], iota[:, :], ed[:, c, k, IL:IL + 1], ev[:, r, k:k + 1],
                                              ALU.is_equal, ALU.mult)
                    ins.then_inc(a_done, 1)

                def accumulate(g, c, n):
                    r = c % R
                    blk_r = v.value_load(gblk[0:1, bass.ds(g, 1)], min_val=0, max_val=NB - 1)
                    v.wait_ge(row_done, g + 1)
                    u = r % 2
                    if not first(g, 1):
                        v.wait_ge(acc_done, g)
                    dst_ = acc[:, bass.ds(blk_r, 1), :].rearrange("p b n -> p (b n)")
                    v.tensor_tensor(dst_, dst_, ps[:, 2 * u:2 * u + 2, :].rearrange("p b n -> p (b n)")[:, 0:D + 1],
                                    ALU.add).then_inc(acc_done, 1)

                pipelined(v, (0, source_scores), (1, weighted_rows), (0, add_target), (2, accumulate), (0, leaky), ring=U)

            @block.scalar
            def _(act):
                def exponential(g, c, n):
                    r = c % R
                    act.wait_ge(zl_done, g + 1)
                    act.activation(ev[:, r, :], zl[:, r, :], ACT.Exp).then_inc(e_done, 1)

                def block_scores(g, c, n):
                    r = c % R
                    after(act, s_done, g - (R - 1))
                    blk_r = act.value_load(gblk[0:1, bass.ds(g, 1)], min_val=0, max_val=NB - 1)
                    act.activation(srow[:, r, :], s_bc[:, bass.ds(blk_r, 1), :].rearrange("p b n -> p (b n)"), ACT.Copy).then_inc(srow_ready, 1)
                pipelined(act, (0, block_scores), (1, exponential))

            @block.tensor
            def _(pe):
                def row_sums(g, c, n):
                    r = c % R
                    u = r % 2
                    pe.wait_ge(a_done, g + 1)
                    if not first(g, 2):
                        pe.wait_ge(acc_done, g - 1)
                    for k in range(2):
                        pe.matmul(ps[:, 2 * u, :], aw[:, r, k, :], xg[:, c, k, 0:D], start=(k == 0), stop=(k == 1))
                        mm = pe.matmul(ps[:, 2 * u + 1, 0:1], aw[:, r, k, :], xg[:, c, k, ONE:ONE + 1],
                                       start=(k == 0), stop=(k == 1))
                    mm.then_inc(row_done, 1)
                pipelined(pe, (0, row_sums))

        sweep1.close()
        nodes = ExitStack()
        rcp = sb("rcp", [P, 2, 2], scope=nodes)
        hb = sb("hb", [P, 2, D], scope=nodes)
        stats = sb("stats", [P, 2, 6], scope=nodes)
        mv = sb("mv", [P, 2, 2], scope=nodes)
        sd_ = sb("sd_", [P, 2], scope=nodes)
        rstd = sb("rstd", [P, 2], scope=nodes)
        x1c = sb("x1c", [P, 2, D], scope=nodes)
        xT = sb("xT", [P, 4, GE], scope=nodes)
        sq = sb("sq", [P, 3, GE], scope=nodes)
        n1T = sb("n1T", [P, GE], scope=nodes)
        p0T = sb("p0T", [P, GE], scope=nodes)
        hT = sb("hT", [P, 2, GE], scope=nodes)
        gT = sb("gT", [P, 2, GE], scope=nodes)
        xgT = sb("xgT", [P, 3, GE], scope=nodes)
        tabrow = sb("tabrow", [P, 2, TW], scope=nodes)
        rcp_ready = sem("rcp_ready")
        hb_ready = sem("hb_ready")
        stats_ready = sem("stats_ready")
        issue3 = sem("issue3")
        mv_ready = sem("mv_ready")
        sd_ready = sem("sd_ready")
        rstd_ready = sem("rstd_ready")
        x1_ready = sem("x1_ready")
        x1_copied = sem("x1_copied")
        xtr_ready = sem("xtr_ready")
        xT_ready = sem("xT_ready")
        sq_ready = sem("sq_ready")
        n1_ready = sem("n1_ready")
        pre_ready = sem("pre_ready")
        p0T_ready = sem("p0T_ready")
        p1_split = sem("p1_split")
        p1_copied = sem("p1_copied")
        u_ready = sem("u_ready")
        hT_ready = sem("hT_ready")
        part_ready = sem("part_ready")
        P0_ready = sem("P0_ready")
        g_ready = sem("g_ready")
        gT_ready = sem("gT_ready")
        xg_ready = sem("xg_ready")
        xn_ready = sem("xn_ready")
        row_ready = sem("row_ready")
        self_ready = sem("self_ready")
        tab_out = sem("tab_out")
        psX, psP0, psG, psN, psP1 = ps[:, 0:2, :], ps[:, 2, :], ps[:, 3, :], ps[:, 4:6, :], ps[:, 6:8, 0:3 * MUL]

        with nc.Block() as block:
            @block.vector
            def _(v):
                def residual(q):
                    v.tensor_scalar(rcp[:, 0, :], acc[:, bass.ds(q * 2, 2), D], 1.0, None, ALU.mult).then_inc(rcp_ready, 1)
                    v.wait_ge(rcp_ready, q * 2 + 1)
                    v.reciprocal(rcp[:, 1, :], rcp[:, 0, :]).then_inc(rcp_ready, 1)
                    v.wait_ge(rcp_ready, q * 2 + 2)
                    after(v, x1_ready, q)
                    for k in range(2):
                        ins = v.scalar_tensor_tensor(hb[:, k, :], acc[:, bass.ds(q * 2 + k, 1), 0:D].rearrange("p b n -> p (b n)"),
                                                     rcp[:, 1, k:k + 1], xt[:, bass.ds(q * 2 + k, 1), :].rearrange("p b n -> p (b n)"),
                                                     ALU.mult, ALU.add)
                    ins.then_inc(hb_ready, 1)
                    v.wait_ge(hb_ready, q + 1)
                    v.sem_inc(issue3, 1)
                    for k in range(2):
                        ins = v.bn_stats(stats[:, k, :], hb[:, k, :])
                    ins.then_inc(stats_ready, 1)
                    v.wait_ge(stats_ready, q + 1)
                    v.sem_inc(issue3, 1)
                    for k in range(2):
                        ins = v.bn_aggr(mv[:, k, :], stats[:, k, :])
                    ins.then_inc(mv_ready, 1)

                def norm(q):
                    v.wait_ge(sd_ready, q + 1)
                    v.reciprocal(rstd[:, :], sd_[:, :]).then_inc(rstd_ready, 1)
                    v.wait_ge(rstd_ready, q + 1)
                    after(v, xtr_ready, q)
                    after(v, x1_copied, q)
                    for k in range(2):
                        ins = v.tensor_scalar(x1c[:, k, :], hb[:, k, :], mv[:, k, 0:1], rstd[:, k:k + 1], ALU.subtract, ALU.mult)
                    ins.then_inc(x1_ready, 1)

                def squares(q):
                    v.wait_ge(xT_ready, q + 1)
                    after(v, n1_ready, q)
                    v.tensor_tensor(sq[:, :, :], xT[:, 1:4, :], xT[:, 1:4, :], ALU.mult).then_inc(sq_ready, 1)
                    v.wait_ge(sq_ready, q * 3 + 1)
                    v.tensor_tensor(sq[:, 0, :], sq[:, 0, :], sq[:, 1, :], ALU.add).then_inc(sq_ready, 1)
                    v.wait_ge(sq_ready, q * 3 + 2)
                    v.tensor_tensor(sq[:, 0, :], sq[:, 0, :], sq[:, 2, :], ALU.add).then_inc(sq_ready, 1)

                def split_p1(q):
                    two = bass.ds(q * 2, 2)
                    v.wait_ge(pre_ready, q + 1)
                    v.tensor_scalar(p1h[:, two, :], psP1, 1.0, None, ALU.mult).then_inc(p1_split, 1)
                    v.wait_ge(p1_split, q * 2 + 1)
                    v.tensor_tensor(p1l[:, two, :], psP1, p1h[:, two, :].bitcast(F32), ALU.subtract).then_inc(p1_split, 1)

                def gated(q):
                    v.wait_ge(gT_ready, q + 1)
                    after(v, xn_ready, q)
                    v.tensor_tensor(xgT[:, :, :], xT[:, 1:4, :], gT[:, 1, :].unsqueeze(1).to_broadcast([P, 3, GE]), ALU.mult).then_inc(xg_ready, 1)

                def table_row(q):
                    v.wait_ge(xn_ready, q + 1)
                    v.wait_ge(p1_copied, q + 1)
                    after(v, tab_out, q * 16)
                    after(v, self_ready, q)
                    v.tensor_copy(tabrow[:, :, P:D], psN[:, :, P:D])
                    v.tensor_tensor(tabrow[:, :, 0:P], psN[:, :, 0:P], bnd_bc[:, :].unsqueeze(1).to_broadcast([P, 2, P]), ALU.add).then_inc(row_ready, 1)
                pairs(v, (1, squares), (2, table_row), (1, split_p1), (0, residual), (0, norm), (1, gated))

            @block.scalar
            def _(act):
                def deviation(q):
                    act.wait_ge(mv_ready, q + 1)
                    act.activation(sd_[:, :], mv[:, :, 1], ACT.Sqrt, bias=epsc[:, 0:1]).then_inc(sd_ready, 1)

                def x_out(q):
                    act.wait_ge(xtr_ready, q + 1)
                    after(act, xg_ready, q)
                    act.activation(xT[:, :, :], psX, ACT.Copy).then_inc(xT_ready, 1)

                def lengths(q):
                    act.wait_ge(sq_ready, q * 3 + 3)
                    act.activation(n1T[:, :], sq[:, 0, :], ACT.Sqrt, scale=1.0 / 3.0).then_inc(n1_ready, 1)

                def p0_out(q):
                    act.wait_ge(pre_ready, q + 1)
                    act.activation(p0T[:, :], psP0[:, 0:GE], ACT.Identity, bias=bpre[:, 0:1]).then_inc(p0T_ready, 1)

                def p1_out(q):
                    act.wait_ge(p1_split, q * 2 + 2)
                    after(act, tab_out, q * 16)
                    act.activation(tabrow[:, :, D:TW], psP1, ACT.Copy).then_inc(p1_copied, 1)

                def gate_hidden(q):
                    act.wait_ge(u_ready, q + 1)
                    for h in range(2):
                        ins = act.activation(hT[:, h, :], psG[:, GE * h:GE * h + GE], ACT.Silu, bias=bg1[:, h:h + 1])
                    ins.then_inc(hT_ready, 1)

                def part_out(q):
                    act.wait_ge(part_ready, q + 1)
                    act.activation(P0[:, bass.ds(q * 2, 2), :], psP0[:, GE:512].rearrange("p (k n) -> p k n", k=2), ACT.Copy).then_inc(P0_ready, 1)

                def gate_out(q):
                    act.wait_ge(g_ready, q + 1)
                    for h in range(2):
                        ins = act.activation(gT[:, h, :], psG[:, GE * h:GE * h + GE], ACT.Identity, bias=bg2[:, h:h + 1])
                    ins.then_inc(gT_ready, 1)

                def keep_self(q):
                    act.wait_ge(row_ready, q + 1)
                    act.activation(selfx[:, bass.ds(q * 2, 2), :], tabrow[:, :, 0:D], ACT.Copy).then_inc(self_ready, 1)
                pairs(act, (1, lengths), (1, p0_out), (1, gate_hidden), (2, keep_self), (0, deviation), (1, part_out),
                      (1, gate_out), (0, x_out), (1, p1_out))

            @block.tensor
            def _(pe):
                def turn_x(q):
                    pe.wait_ge(x1_ready, q + 1)
                    after(pe, xT_ready, q)
                    for c in range(4):
                        for k in range(2):
                            s_ = x1c[:, k, 0:P] if c == 0 else x1c[:, k, P + c - 1:D:3]
                            mm = pe.transpose(psX[:, c // 2, GE * (c % 2) + P * k:GE * (c % 2) + P * k + P], s_, ident[:, :])
                    mm.then_inc(xtr_ready, 1)

                def pre(q):
                    pe.wait_ge(xT_ready, q + 1)
                    after(pe, P0_ready, q)
                    after(pe, p1_copied, q)
                    pe.matmul(psP0[:, 0:GE], wpre0[:, :], xT[:, 0, :], start=True, stop=True)
                    for k in range(2):
                        for c in range(3):
                            mm = pe.matmul(psP1[:, k, P * c:P * c + P], xT[:, 1 + c, P * k:P * k + P], wpre1[:, :], start=True, stop=True)
                    mm.then_inc(pre_ready, 1)

                def gate1(q):
                    pe.wait_ge(n1_ready, q + 1)
                    after(pe, gT_ready, q)
                    for h in range(2):
                        pe.matmul(psG[:, GE * h:GE * h + GE], wg1[:, 0, P * h:P * h + P], xT[:, 0, :], start=True, stop=False)
                        mm = pe.matmul(psG[:, GE * h:GE * h + GE], wg1[:, 1, P * h:P * h + P], n1T[:, :], start=False, stop=True)
                    mm.then_inc(u_ready, 1)

                def part(q):
                    pe.wait_ge(p0T_ready, q + 1)
                    for k in range(2):
                        mm = pe.matmul(psP0[:, GE + P * k:GE + P * k + P], p0T[:, P * k:P * k + P],
                                       ws1ab[:, :, :].rearrange("p q h -> p (q h)"), start=True, stop=True)
                    mm.then_inc(part_ready, 1)

                def gate2(q):
                    pe.wait_ge(hT_ready, q + 1)
                    for h in range(2):
                        for c in range(2):
                            mm = pe.matmul(psG[:, GE * h:GE * h + GE], wg2[:, c, P * h:P * h + P], hT[:, c, :], start=(c == 0), stop=(c == 1))
                    mm.then_inc(g_ready, 1)

                def new_x(q):
                    pe.wait_ge(xg_ready, q + 1)
                    after(pe, row_ready, q)
                    for k in range(2):
                        pe.matmul(psN[:, k, 0:P], gT[:, 0, P * k:P * k + P], wnd0[:, :], start=True, stop=True)
                        for c in range(3):
                            mm = pe.matmul(psN[:, k, P * (c + 1):P * (c + 2)], xgT[:, c, P * k:P * k + P], wnd1[:, :], start=True, stop=True)
                    mm.then_inc(xn_ready, 1)
                pairs(pe, (1, pre), (1, gate1), (1, part), (1, gate2), (0, turn_x), (1, new_x))

            @block.sync
            def _(sp):
                def row_out(q):
                    sp.wait_ge(row_ready, q + 1)
                    sp.dma_start(tab_d[bass.ds(q * GE, GE), :].rearrange("(k p) w -> p k w", p=P), tabrow[:, :, :]).then_inc(tab_out, 16)
                pairs(sp, (0, row_out))
                sp.wait_ge(tab_out, 16 * (NB // 2))

            @block.gpsimd
            def _(gp):
                def keep_x1(q):
                    gp.wait_ge(x1_ready, q + 1)
                    gp.tensor_copy(x1[:, bass.ds(q * 2, 2), :], x1c[:, :, :]).then_inc(x1_copied, 1)
                pairs(gp, (0, keep_x1))
                gp.wait_ge(hb_ready, NB // 2)
                gp.memset(acc[:, :, :], 0.0)

        nodes.close()
        sweep2 = ExitStack()
        oh = sb("oh", [P, U, 2, P], scope=sweep2)
        shr = sb("shr", [P, U, 2, SH], scope=sweep2)
        ohT = sb("ohT", [P, 2, GE], F32R, scope=sweep2)
        f4 = sb("f4", [P, 2, 2, 4, HID], F32R, scope=sweep2)
        fcomb = sb("fcomb", [P, R, GE], F32R, scope=sweep2)
        P0c = sb("P0c", [P, 2, P], scope=sweep2)
        prod = sb("prod", [P, 2, 3 * MUL], scope=sweep2)
        ipT = sb("ipT", [P, GE], scope=sweep2)
        lx = sb("lx", [P, GE], scope=sweep2)
        sp_ = sb("sp_", [P, GE], scope=sweep2)
        sph = sb("sph", [P, GE], F32R, scope=sweep2)
        hcomb = sb("hcomb", [P, 2, GE], F32R, scope=sweep2)
        S_sb = sb("S_sb", [P, 2, D], scope=sweep2)
        wv = sb("wv", [P, 2, D], scope=sweep2)
        t1 = sb("t1", [P, 2, P], scope=sweep2)
        bb = sb("bb", [P, 2, 2, P], scope=sweep2)
        oh_sh = sb("oh_sh", [P, 2, 2, 2, P], scope=sweep2)
        dd = s_bc[:, 0:6, :]
        dw = s_bc[:, 6:8, :]
        msg = W_sb[:, :, :].rearrange("p (u k) n -> p u k n", u=2)

        ed2 = [sem(f"ed2_{r}") for r in range(R)]
        xj_in = [sem(f"xj_in{r}") for r in range(R)]
        issue2 = sem("issue2")
        oh_ready = sem("oh_ready")
        tr_ready = sem("tr_ready")
        ohT_ready = sem("ohT_ready")
        fh_ready = sem("fh_ready")
        f4_ready = sem("f4_ready")
        trf_ready = sem("trf_ready")
        fcomb_ready = sem("fcomb_ready")
        pi_ready = sem("pi_ready")
        prod_ready = sem("prod_ready")
        ip_ready = sem("ip_ready")
        ipT_ready = sem("ipT_ready")
        hid_ready = sem("hid_ready")
        sp_done = sem("sp_done")
        p0c_ready = sem("p0c_ready")
        abs_done = sem("abs_done")
        exp_done = sem("exp_done")
        ln_done = sem("ln_done")
        sph_done = sem("sph_done")
        comb_ready = sem("comb_ready")
        s_ready = sem("s_ready")
        s_copied = sem("s_copied")
        f_ready = sem("f_ready")
        w_done = sem("w_done")
        c_done = sem("c_done")
        oh_sh_ready = sem("oh_sh_ready")
        lv = sem("lv")
        dx_done = sem("dx_done")
        first_done = sem("first_done")
        dd_done = sem("dd_done")
        msg_ready = sem("msg_ready")
        sum_ready = sem("sum_ready")
        acc2_done = sem("acc2_done")
        psT, psH, psI, psS, psF, psA = ps[:, 0, :], ps[:, 3, 0:GE], ps[:, 3, GE:512], ps[:, 4, :], ps[:, 5:7, :], ps[:, 7, :]

        with nc.Block() as block:
            @block.sync
            def _(sp):
                def load(g, c, n):
                    r = c % R
                    if not first(g, R):
                        sp.wait_ge(ip_ready, g - (R - 1))
                    sp.dma_start(ed[:, r, :, :], sd2[:, bass.ds(g * 2, 2), :]).then_inc(ed2[r], 16)
                pipelined(sp, (0, load))

            @block.gpsimd
            def _(gp):
                def gather(g, c, n):
                    r = c % R
                    if not first(g, R):
                        gp.wait_ge(c_done, g - (R - 1))
                        gp.sem_inc(issue2, 1)
                        gp.wait_ge(msg_ready, g - (R - 1))
                        gp.sem_inc(issue2, 1)
                    gp.wait_ge(ed2[r], n * 16)
                    gp.sem_inc(issue2, 1)
                    for k in range(2):
                        gp.indirect_dma_start(xj[:, r, k, :], None, tab_d[:, :],
                                              bass.IndirectOffsetOnAxis(ap=ed[:, r, k, JD:JD + 1].bitcast(I32), axis=0))\
                          .then_inc(xj_in[r], 16)

                def vectors(g, c, n):
                    r = c % R
                    u = c % 2
                    after(gp, sum_ready, g - 1)
                    gp.wait_ge(w_done, g + 1)
                    for k in range(2):
                        ins = gp.tensor_tensor(msg[:, u, k, P:D].rearrange("p (m n) -> p m n", m=3),
                                               xj[:, r, k, P:D].rearrange("p (m n) -> p m n", m=3),
                                               wv[:, k, P:2 * P].unsqueeze(1).to_broadcast([P, 3, P]), ALU.mult)
                    ins.then_inc(c_done, 1)

                def low_f(g, c, n):
                    r, u = c % R, c % 2
                    gp.wait_ge(fh_ready, g + 1)
                    gp.tensor_tensor(f4[:, u, :, 1::2, :], ed[:, r, :, 0:EA].unsqueeze(2).to_broadcast([P, 2, 2, HID]),
                                     f4[:, u, :, 0::2, :].bitcast(F32), ALU.subtract).then_inc(f4_ready, 1)

                def split(g, c, n):
                    r = c % R
                    u = r % 2
                    gp.wait_ge(sph_done, g + 1)
                    after(gp, f_ready, g - 1)
                    after(gp, s_ready, g * 2 - 2)
                    gp.tensor_tensor(hcomb[:, u, :], sp_[:, :], sph[:, :].bitcast(F32), ALU.subtract).then_inc(comb_ready, 1)

                pipelined(gp, (0, gather), (2, split), (0, low_f), (3, vectors))

            @block.tensor
            def _(pe):
                def turn_rows(g, c, n):
                    pe.wait_ge(oh_ready, g + 1)
                    after(pe, ohT_ready, g)
                    after(pe, fcomb_ready, g - 1)
                    for k in range(2):
                        mm = pe.transpose(psT[:, P * k:P * k + P], oh[:, c, k, :], ident[:, :])
                    mm.then_inc(tr_ready, 1)

                def turn_f(g, c, n):
                    u = c % 2
                    pe.wait_ge(f4_ready, g + 1)
                    after(pe, ohT_ready, g)
                    after(pe, fcomb_ready, g)
                    for k in range(2):
                        mm = pe.transpose(psT[:, GE + P * k:GE + P * k + P],
                                          f4[:, u, k, :, :].bitcast(F32).rearrange("p q h -> p (q h)"), ident[:, :])
                    mm.then_inc(trf_ready, 1)

                def sources(g, c, n):
                    r = c % R
                    u = r % 2
                    blk_r = pe.value_load(gblk[0:1, bass.ds(g, 1)], min_val=0, max_val=NB - 1)
                    pe.wait_ge(ohT_ready, g + 1)
                    after(pe, prod_ready, g)
                    for k in range(2):
                        for part, tab in enumerate((p1h, p1l)):
                            mm = pe.matmul(ps[:, 1 + k, 0:3 * MUL], ohT[:, u, P * k:P * k + P],
                                           tab[:, bass.ds(blk_r, 1), :].rearrange("p b n -> p (b n)"),
                                           start=(part == 0), stop=(part == 1))
                    mm.then_inc(pi_ready, 1)

                def inner(g, c, n):
                    pe.wait_ge(prod_ready, g + 1)
                    after(pe, sp_done, g)
                    after(pe, ipT_ready, g)
                    for k in range(2):
                        for m in range(3):
                            mm = pe.matmul(psI[:, P * k:P * k + P], prod[:, k, P * m:P * m + P], ident[:, :], is_transpose=True,
                                           start=(m == 0), stop=(m == 2))
                    mm.then_inc(ip_ready, 1)

                def hidden(g, c, n):
                    r = c % R
                    u = r % 2
                    pe.wait_ge(ipT_ready, g + 1)
                    pe.wait_ge(p0c_ready, g + 1)
                    after(pe, sp_done, g)
                    pe.matmul(psH, ws1c[:, :, :].rearrange("p q h -> p (q h)"), ipT[:, :], start=True, stop=False)
                    pe.matmul(psH, P0c[:, u, :], ohT[:, u, :].bitcast(F32), start=False, stop=True).then_inc(hid_ready, 1)

                def factors0(g, c, n):
                    r = c % R
                    u = r % 2
                    pe.wait_ge(comb_ready, g + 1)
                    after(pe, s_copied, g * 2)
                    pe.matmul(psS, hcomb[:, u, 0:P], wstack[:, 0, :], start=True, stop=True).then_inc(s_ready, 1)
                    pe.wait_ge(fcomb_ready, g + 1)
                    after(pe, w_done, g)
                    for k in range(2):
                        mm = pe.matmul(psF[:, k, :], fcomb[:, r, P * k:P * k + P], wstack[:, 1, :], start=True, stop=True)
                    mm.then_inc(f_ready, 1)

                def factors1(g, c, n):
                    r = c % R
                    u = r % 2
                    pe.wait_ge(s_copied, g * 2 + 1)
                    pe.matmul(psS, hcomb[:, u, P:GE], wstack[:, 0, :], start=True, stop=True).then_inc(s_ready, 1)

                def sums(g, c, n):
                    r = c % R
                    u = r % 2
                    pe.wait_ge(msg_ready, g + 1)
                    pe.wait_ge(first_done, g + 1)
                    pe.wait_ge(oh_sh_ready, g * 2 + 2)
                    after(pe, acc2_done, g)
                    pe.matmul(psA, oh[:, c, 0, :], msg[:, u, 0, :], start=True, stop=False)
                    for k in range(2):
                        for m in range(1, 3):
                            pe.matmul(psA[:, P * (m + 1):P * (m + 2)], oh_sh[:, u, k, m - 1, :], bb[:, u, k, :], start=False, stop=False)
                    mm = pe.matmul(psA, oh[:, c, 1, :], msg[:, u, 1, :], start=False, stop=True)
                    mm.then_inc(sum_ready, 1)
                pipelined(pe, (0, turn_rows), (1, turn_f), (3, factors0), (1, inner), (3, factors1), (1, hidden), (0, sources), (4, sums))

            @block.scalar
            def _(act):
                def factor_out(k):
                    def step(g, c, n):
                        act.wait_ge(s_ready, g * 2 + (k + 1))
                        if k == 0:
                            after(act, w_done, g)
                        act.activation(S_sb[:, k, 0:GE], psS[:, 0:GE], ACT.Copy, scale=shr[:, c, k, 0:1])
                        act.activation(S_sb[:, k, GE:512], psS[:, GE:512], ACT.Copy).then_inc(s_copied, 1)
                    return step

                def scaled_rows(k):
                    def step(g, c, n):
                        u = c % 2
                        after(act, sum_ready, g - 1)
                        for m in range(1, 3):
                            ins = act.activation(oh_sh[:, u, k, m - 1, :], oh[:, c, k, :], ACT.Copy, scale=shr[:, c, k, m + 1:m + 2])
                        ins.then_inc(oh_sh_ready, 1)
                    return step

                def first_component(g, c, n):
                    r = c % R
                    act.wait_ge(xj_in[r], n * 32)
                    after(act, dd_done, g * 2 - 1)
                    for k in range(2):
                        ins = act.activation(dd[:, k, :], xj[:, r, k, P:2 * P], ACT.Copy, scale=shr[:, c, k, 1:2])
                    ins.then_inc(dx_done, 1)

                def inner_out(g, c, n):
                    act.wait_ge(ip_ready, g + 1)
                    after(act, hid_ready, g)
                    act.activation(ipT[:, :], psI, ACT.Copy).then_inc(ipT_ready, 1)

                def rows_out(g, c, n):
                    r = c % R
                    u = r % 2
                    act.wait_ge(tr_ready, g + 1)
                    after(act, trf_ready, g)
                    after(act, hid_ready, g - 1)
                    act.activation(ohT[:, u, :], psT[:, 0:GE], ACT.Copy).then_inc(ohT_ready, 1)

                def high_f(g, c, n):
                    r, u = c % R, c % 2
                    act.wait_ge(ed2[r], n * 16)
                    after(act, trf_ready, g - 1)
                    act.activation(f4[:, u, :, 0::2, :], ed[:, r, :, 0:EA].unsqueeze(2).to_broadcast([P, 2, 2, HID]), ACT.Copy)\
                       .then_inc(fh_ready, 1)

                def f_out(g, c, n):
                    r = c % R
                    act.wait_ge(trf_ready, g + 1)
                    after(act, f_ready, g - (R - 1))
                    act.activation(fcomb[:, r, :], psT[:, GE:512], ACT.Copy).then_inc(fcomb_ready, 1)

                def node_part(g, c, n):
                    r = c % R
                    u = r % 2
                    blk_r = act.value_load(gblk[0:1, bass.ds(g, 1)], min_val=0, max_val=NB - 1)
                    act.activation(P0c[:, u, :], P0[:, bass.ds(blk_r, 1), :].rearrange("p b n -> p (b n)"), ACT.Copy).then_inc(p0c_ready, 1)

                def log_part(g, c, n):
                    act.wait_ge(hid_ready, g + 1)
                    after(act, sp_done, g)
                    act.activation(lx[:, :], psH, ACT.Abs).then_inc(abs_done, 1)
                    act.wait_ge(abs_done, g + 1)
                    act.activation(lx[:, :], lx[:, :], ACT.Exp, scale=-1.0).then_inc(exp_done, 1)
                    act.wait_ge(exp_done, g + 1)
                    act.activation(lx[:, :], lx[:, :], ACT.Ln, scale=0.5, bias=half[:, 0:1]).then_inc(ln_done, 1)

                def high_part(g, c, n):
                    act.wait_ge(sp_done, g + 1)
                    after(act, comb_ready, g)
                    act.activation(sph[:, :], sp_[:, :], ACT.Copy, scale=odd32[:, 0:1]).then_inc(sph_done, 1)
                act.preload_act_table_set("natural_log_exp_and_others")
                pipelined(act, (0, high_f), (2, high_part), (3, factor_out(0)), (0, rows_out), (1, inner_out), (3, factor_out(1)), (1, f_out), (3, scaled_rows(0)), (1, log_part), (3, scaled_rows(1)), (2, first_component), (0, node_part))

            @block.vector
            def _(v):
                def sh(c, k, m):
                    return shr[:, c, k, m:m + 1]

                def one_hot(g, c, n):
                    r = c % R
                    v.wait_ge(ed2[r], n * 16)
                    after(v, sum_ready, g - (U - 1))
                    v.tensor_copy(shr[:, c, :, :], ed[:, r, :, EA:EA + SH])
                    for k in range(2):
                        ins = v.tensor_scalar(oh[:, c, k, :], iota[:, :], ed[:, r, k, IL:IL + 1], None, ALU.is_equal)
                    ins.then_inc(oh_ready, 1)

                def products(g, c, n):
                    r = c % R
                    v.wait_ge(xj_in[r], n * 32)
                    v.wait_ge(pi_ready, g + 1)
                    after(v, ip_ready, g)
                    v.tensor_tensor(prod[:, :, :], ps[:, 1:3, 0:3 * MUL], xj[:, r, :, D:TW], ALU.mult).then_inc(prod_ready, 1)

                def softplus(g, c, n):
                    v.wait_ge(ln_done, g + 1)
                    after(v, comb_ready, g)
                    v.scalar_tensor_tensor(sp_[:, :], psH, 0.0, lx[:, :], ALU.max, ALU.add).then_inc(sp_done, 1)

                def inner_x(m):
                    def step(g, c, n):
                        r = c % R
                        if m == 1:
                            v.wait_ge(dx_done, g + 1)
                            after(v, msg_ready, g)
                        else:
                            v.wait_ge(dd_done, g * 2 + 1)
                        for k in range(2):
                            ins = v.scalar_tensor_tensor(dd[:, 2 * m + k, :], xj[:, r, k, P * (m + 1):P * (m + 2)], sh(c, k, m + 1),
                                                         dd[:, 2 * m - 2 + k, :], ALU.mult, ALU.add)
                        ins.then_inc(dd_done, 1)
                    return step

                def messages(g, c, n):
                    r, u = c % R, c % 2
                    v.wait_ge(f_ready, g + 1)
                    v.wait_ge(s_copied, g * 2 + 2)
                    after(v, c_done, g)
                    v.tensor_tensor(wv[:, :, :], S_sb[:, :, :], psF, ALU.mult).then_inc(w_done, 1)
                    after(v, sum_ready, g - 1)
                    v.wait_ge(w_done, g + 1)
                    v.wait_ge(dd_done, g * 2 + 2)
                    v.scalar_tensor_tensor(dw[:, :, :], dd[:, 4:6, :], 1.0 / 3.0 ** 0.5, wv[:, :, 3 * P:D], ALU.mult, ALU.mult)
                    v.tensor_tensor(t1[:, :, :], wv[:, :, 0:P], xj[:, r, :, 0:P], ALU.mult).then_inc(lv, 1)
                    v.tensor_tensor(bb[:, u, :, :], wv[:, :, GE:3 * P], xj[:, r, :, 0:P], ALU.mult)
                    v.wait_ge(lv, g + 1)
                    v.tensor_tensor(msg[:, u, :, 0:P], t1[:, :, :], dw[:, :, :], ALU.add).then_inc(msg_ready, 1)

                def first_vector(g, c, n):
                    u = c % 2
                    v.wait_ge(msg_ready, g + 1)
                    v.wait_ge(c_done, g + 1)
                    for k in range(2):
                        ins = v.scalar_tensor_tensor(msg[:, u, k, P:2 * P], bb[:, u, k, :], sh(c, k, 1), msg[:, u, k, P:2 * P],
                                                     ALU.mult, ALU.add)
                    ins.then_inc(first_done, 1)

                def accumulate(g, c, n):
                    blk_r = v.value_load(gblk[0:1, bass.ds(g, 1)], min_val=0, max_val=NB - 1)
                    v.wait_ge(sum_ready, g + 1)
                    after(v, acc2_done, g)
                    dst_ = acc[:, bass.ds(blk_r, 1), 0:D].rearrange("p b n -> p (b n)")
                    v.tensor_tensor(dst_, dst_, psA, ALU.add).then_inc(acc2_done, 1)
                pipelined(v, (0, one_hot), (1, products), (4, first_vector), (3, inner_x(1)), (5, accumulate), (3, inner_x(2)),
                          (3, messages), (1, softplus))

        sweep2.close()
        ya = sb("ya2", [P, 2, D])
        yT = sb("yT2", [P, 2, D])
        hb = sb("hb2", [P, 2, D])
        stats = sb("stats2", [P, 2, 6])
        mv = sb("mv2", [P, 2, 2])
        sd_ = sb("sd2_", [P, 2])
        rstd = sb("rstd2", [P, 2])
        outrow = sb("outrow", [P, 2, D])
        oa_ready = sem("oa_ready")
        oaT_ready = sem("oaT_ready")
        oT_ready = sem("oT_ready")
        ow_ready = sem("ow_ready")
        ores_ready = sem("ores_ready")
        oh_done = sem("oh_done")
        ostats_ready = sem("ostats_ready")
        omv_ready = sem("omv_ready")
        osd_ready = sem("osd_ready")
        orstd_ready = sem("orstd_ready")
        orow_ready = sem("orow_ready")
        out_done = sem("out_done")
        psY, psO = ps[:, 0:2, :], ps[:, 2:4, :]
        with nc.Block() as block:
            @block.vector
            def _(v):
                def residuals(q):
                    two = bass.ds(q * 2, 2)
                    after(v, orow_ready, q)
                    v.scalar_tensor_tensor(hb[:, :, 0:P], x1[:, two, 0:P], 2.0, bo_bc[:, :].unsqueeze(1).to_broadcast([P, 2, P]),
                                           ALU.mult, ALU.add)
                    v.tensor_scalar(hb[:, :, P:D], x1[:, two, P:D], 2.0, None, ALU.mult).then_inc(ores_ready, 1)

                def add_layer(q):
                    v.wait_ge(ores_ready, q + 1)
                    v.wait_ge(ow_ready, q + 1)
                    v.tensor_tensor(hb[:, :, 0:P], hb[:, :, 0:P], psO[:, :, 0:P], ALU.add)
                    for k in range(2):
                        rows = hb[:, k, P:D].rearrange("p (n m) -> p n m", m=3)
                        ins = v.tensor_tensor(rows, rows, psO[:, k, P:D].rearrange("p (m n) -> p n m", m=3), ALU.add)
                    ins.then_inc(oh_done, 1)
                    v.wait_ge(oh_done, q + 1)
                    v.sem_inc(issue3, 1)
                    for k in range(2):
                        ins = v.bn_stats(stats[:, k, :], hb[:, k, :])
                    ins.then_inc(ostats_ready, 1)
                    v.wait_ge(ostats_ready, q + 1)
                    v.sem_inc(issue3, 1)
                    for k in range(2):
                        ins = v.bn_aggr(mv[:, k, :], stats[:, k, :])
                    ins.then_inc(omv_ready, 1)

                def norm(q):
                    v.wait_ge(osd_ready, q + 1)
                    v.reciprocal(rstd[:, :], sd_[:, :]).then_inc(orstd_ready, 1)
                    v.wait_ge(orstd_ready, q + 1)
                    after(v, out_done, q * 16)
                    for k in range(2):
                        ins = v.tensor_scalar(outrow[:, k, :], hb[:, k, :], mv[:, k, 0:1], rstd[:, k:k + 1], ALU.subtract, ALU.mult)
                    ins.then_inc(orow_ready, 1)
                pairs(v, (0, residuals), (0, add_layer), (0, norm))

            @block.scalar
            def _(act):
                def sums_out(q):
                    act.wait_ge(oaT_ready, q + 1)
                    act.activation(yT[:, :, :], psY, ACT.Copy).then_inc(oT_ready, 1)

                def deviation(q):
                    act.wait_ge(omv_ready, q + 1)
                    act.activation(sd_[:, :], mv[:, :, 1], ACT.Sqrt, bias=epsc[:, 0:1]).then_inc(osd_ready, 1)
                act.preload_act_table_set("sqrt_and_others")
                pairs(act, (0, sums_out), (1, deviation))

            @block.gpsimd
            def _(gp):
                def with_self(q):
                    two = bass.ds(q * 2, 2)
                    after(gp, oaT_ready, q)
                    gp.tensor_tensor(ya[:, :, :], acc[:, two, 0:D], selfx[:, two, :], ALU.add).then_inc(oa_ready, 1)
                pairs(gp, (0, with_self))

            @block.tensor
            def _(pe):
                def turn_sums(q):
                    pe.wait_ge(oa_ready, q + 1)
                    after(pe, oT_ready, q)
                    for k in range(2):
                        for c in range(4):
                            mm = pe.transpose(psY[:, k, P * c:P * c + P], ya[:, k, P * c:P * c + P], ident[:, :])
                    mm.then_inc(oaT_ready, 1)

                def layer(q):
                    pe.wait_ge(oT_ready, q + 1)
                    after(pe, oh_done, q)
                    for k in range(2):
                        for c in range(4):
                            mm = pe.matmul(psO[:, k, P * c:P * c + P], yT[:, k, P * c:P * c + P],
                                           (wo1 if c else wo0)[:, :], start=True, stop=True)
                    mm.then_inc(ow_ready, 1)
                pairs(pe, (0, turn_sums), (0, layer))

            @block.sync
            def _(sp):
                def row_out(q):
                    sp.wait_ge(orow_ready, q + 1)
                    sp.dma_start(out[bass.ds(q * GE, GE), :].rearrange("(k p) w -> p k w", p=P), outrow[:, :, :]).then_inc(out_done, 16)
                pairs(sp, (0, row_out))
                sp.wait_ge(out_done, 16 * (NB // 2))


def kernel(x, src, dst, edge_attr_32, edge_attr_4, L0_gnn_W, L0_gnn_b, L0_gnn_a, L1_gnn_W_pre0, L1_gnn_b_pre0,
           L1_gnn_W_pre1, L1_gnn_W_nd0, L1_gnn_b_nd0, L1_gnn_W_nd1, L1_gnn_W_g1, L1_gnn_b_g1, L1_gnn_W_g2,
           L1_gnn_b_g2, L1_gnn_W_f1, L1_gnn_W_f2, L1_gnn_W_s1, L1_gnn_W_s2, L1_gnn_W_o0, L1_gnn_b_o0, L1_gnn_W_o1):
    import concourse.bacc as bacc
    from concourse.bass_utils import run_bass_kernel_spmd as run
    nc = bacc.Bacc("TRN2", target_bir_lowering=False, num_devices=1)
    ea, es = np.asarray(edge_attr_32), np.asarray(edge_attr_4)
    edge_rows = np.concatenate([ea, es, np.zeros((E, ROW - EA - SH), ea.dtype)], axis=1)
    arrays = {"x": x, "src": src, "dst": dst, "edge_rows": edge_rows, "W": L0_gnn_W, "b": L0_gnn_b, "a": L0_gnn_a,
              "W_pre0": L1_gnn_W_pre0, "b_pre0": L1_gnn_b_pre0, "W_pre1": L1_gnn_W_pre1, "W_nd0": L1_gnn_W_nd0,
              "b_nd0": L1_gnn_b_nd0, "W_nd1": L1_gnn_W_nd1, "W_g1": L1_gnn_W_g1, "b_g1": L1_gnn_b_g1,
              "W_g2": L1_gnn_W_g2, "b_g2": L1_gnn_b_g2, "W_f1": L1_gnn_W_f1, "W_f2": L1_gnn_W_f2,
              "W_s1": L1_gnn_W_s1, "W_s2": L1_gnn_W_s2, "W_o0": L1_gnn_W_o0, "b_o0": L1_gnn_b_o0, "W_o1": L1_gnn_W_o1}
    arrays = {n: np.ascontiguousarray(v) for n, v in arrays.items()}
    args = [nc.dram_tensor(n, v.shape, mybir.dt.from_np(v.dtype), kind="ExternalInput").ap() for n, v in arrays.items()]
    o = nc.dram_tensor("out", [NPAD, D], F32, kind="ExternalOutput").ap()
    build(nc, *args, o)
    r = run(nc, [arrays], core_ids=[0])
    return r.results[0]["out"][:N]
```
